# Optimizing a Trainium2 kernel written in Bass

```python
import numpy as np
import jax
import jax.numpy as jnp

def _softmax(x, axis=-1):
    return jax.nn.softmax(x, axis=axis)

def _gelu(x):
    return jax.nn.gelu(x, approximate=True)

def _silu(x):
    return jax.nn.silu(x)

def _sigmoid(x):
    return jax.nn.sigmoid(x)

def _layernorm(x, axis=-1, eps=1e-05):
    m = jnp.mean(x, axis=axis, keepdims=True)
    v = jnp.var(x, axis=axis, keepdims=True)
    return (x - m) / jnp.sqrt(v + eps)

def _scatter_add(tgt, idx, src, axis=0):
    return tgt.at[idx].add(src)

def _segment_sum(src, seg, n):
    return jax.ops.segment_sum(src, seg, n)
kernel_name = 'mk_macaron_d1_jaxref_r8_32f7de'

def setup_inputs(seed: int=0):
    np.random.seed(seed)
    _w = jnp.asarray

    def _L0_attn_setup():
        import jax, jax.numpy as jnp
        import numpy as np
        B, T, C = (2, 256, 128)
        NH = 16
        HD = C // NH

        def build_alibi_bias(n_head, max_len):
            slopes = jnp.arange(1, n_head + 1, dtype=jnp.float32) / n_head
            ar = jnp.arange(max_len, dtype=jnp.float32)
            return slopes[:, None, None] * (ar[None, None, :] - ar[None, :, None])
        key = jax.random.key(seed)
        ks = jax.random.split(key, 7)
        s = 0.02
        return {'x': jax.random.normal(ks[0], (B, T, C), dtype=jnp.float32), 'q_w': jax.random.normal(ks[1], (C, C), dtype=jnp.float32) * s, 'q_b': jnp.zeros((C,), dtype=jnp.float32), 'kv_w': jax.random.normal(ks[2], (C, 2 * C), dtype=jnp.float32) * s, 'kv_b': jnp.zeros((2 * C,), dtype=jnp.float32), 'o_w': jax.random.normal(ks[3], (C, C), dtype=jnp.float32) * s, 'o_b': jnp.zeros((C,), dtype=jnp.float32)}
    _L0_attn_in = _L0_attn_setup()

    def _L0_ffn_setup():
        import jax, jax.numpy as jnp
        import numpy as np
        from jax.scipy.linalg import expm
        B, S, D, E, K, NROT = (2, 256, 128, 8, 2, 3)
        EPS = 1e-05

        def _gelu(x):
            return jax.nn.gelu(x, approximate=False)

        def _forward(x, ln_gamma, ln_beta, abel_w, abel_b, moe_gate_w, moe_gate_b, ew1, eb1, ew2, eb2, gens, gc_w, gc_b):
            residual = x
            mu = jnp.mean(x, axis=-1, keepdims=True)
            var = jnp.mean((x - mu) ** 2, axis=-1, keepdims=True)
            xn = (x - mu) * jax.lax.rsqrt(var + EPS) * ln_gamma + ln_beta
            abel_out = _gelu(xn @ abel_w + abel_b)
            logits = xn @ moe_gate_w + moe_gate_b
            topw, topi = jax.lax.top_k(logits, K)
            topw = jax.nn.softmax(topw, axis=-1)
            w_dense = jnp.sum(jax.nn.one_hot(topi, E, dtype=xn.dtype) * topw[..., None], axis=-2)
            h = _gelu(jnp.einsum('bsd,edh->ebsh', xn, ew1) + eb1[:, None, None, :])
            eo = jnp.einsum('ebsh,ehd->ebsd', h, ew2) + eb2[:, None, None, :]
            moe_out = jnp.einsum('ebsd,bse->bsd', eo, w_dense)
            for i in range(NROT):
                moe_out = moe_out @ expm(gens[i])
            combined = jnp.concatenate([abel_out, moe_out], axis=-1)
            gate = jax.nn.sigmoid(combined @ gc_w + gc_b)
            mixed = abel_out * (1.0 - gate) + moe_out * gate
            return residual + mixed
        key = jax.random.key(seed)
        ks = jax.random.split(key, 16)
        sc = 0.02
        x = jax.random.normal(ks[0], (B, S, D), jnp.float32)
        ln_gamma = 1.0 + sc * jax.random.normal(ks[1], (D,), jnp.float32)
        ln_beta = sc * jax.random.normal(ks[2], (D,), jnp.float32)
        abel_w = sc * jax.random.normal(ks[3], (D, D), jnp.float32)
        abel_b = sc * jax.random.normal(ks[4], (D,), jnp.float32)
        moe_gate_w = sc * jax.random.normal(ks[5], (D, E), jnp.float32)
        moe_gate_b = sc * jax.random.normal(ks[6], (E,), jnp.float32)
        ew1 = sc * jax.random.normal(ks[7], (E, D, 2 * D), jnp.float32)
        eb1 = sc * jax.random.normal(ks[8], (E, 2 * D), jnp.float32)
        ew2 = sc * jax.random.normal(ks[9], (E, 2 * D, D), jnp.float32)
        eb2 = sc * jax.random.normal(ks[10], (E, D), jnp.float32)
        g = sc * jax.random.normal(ks[11], (NROT, D, D), jnp.float32)
        gens = 0.5 * (g - jnp.swapaxes(g, -1, -2))
        gc_w = sc * jax.random.normal(ks[12], (2 * D, 1), jnp.float32)
        gc_b = sc * jax.random.normal(ks[13], (1,), jnp.float32)
        return dict(x=x, ln_gamma=ln_gamma, ln_beta=ln_beta, abel_w=abel_w, abel_b=abel_b, moe_gate_w=moe_gate_w, moe_gate_b=moe_gate_b, ew1=ew1, eb1=eb1, ew2=ew2, eb2=eb2, gens=gens, gc_w=gc_w, gc_b=gc_b)
    _L0_ffn_in = _L0_ffn_setup()
    _d = {'L0_attn_x': _L0_attn_in['x'], 'L0_attn_q_w': _L0_attn_in['q_w'], 'L0_attn_q_b': _L0_attn_in['q_b'], 'L0_attn_kv_w': _L0_attn_in['kv_w'], 'L0_attn_kv_b': _L0_attn_in['kv_b'], 'L0_attn_o_w': _L0_attn_in['o_w'], 'L0_attn_o_b': _L0_attn_in['o_b'], 'L0_ffn_ln_gamma': _L0_ffn_in['ln_gamma'], 'L0_ffn_ln_beta': _L0_ffn_in['ln_beta'], 'L0_ffn_abel_w': _L0_ffn_in['abel_w'], 'L0_ffn_abel_b': _L0_ffn_in['abel_b'], 'L0_ffn_moe_gate_w': _L0_ffn_in['moe_gate_w'], 'L0_ffn_moe_gate_b': _L0_ffn_in['moe_gate_b'], 'L0_ffn_ew1': _L0_ffn_in['ew1'], 'L0_ffn_eb1': _L0_ffn_in['eb1'], 'L0_ffn_ew2': _L0_ffn_in['ew2'], 'L0_ffn_eb2': _L0_ffn_in['eb2'], 'L0_ffn_gens': _L0_ffn_in['gens'], 'L0_ffn_gc_w': _L0_ffn_in['gc_w'], 'L0_ffn_gc_b': _L0_ffn_in['gc_b']}
    _x0 = _d['L0_attn_x']
    _d['L0_attn_x'] = jax.random.normal(jax.random.fold_in(jax.random.key(seed), 1), (8, 512, 128), dtype=_x0.dtype)
    del _x0
    return _d

def reference(L0_attn_x, L0_attn_q_w, L0_attn_q_b, L0_attn_kv_w, L0_attn_kv_b, L0_attn_o_w, L0_attn_o_b, L0_ffn_ln_gamma, L0_ffn_ln_beta, L0_ffn_abel_w, L0_ffn_abel_b, L0_ffn_moe_gate_w, L0_ffn_moe_gate_b, L0_ffn_ew1, L0_ffn_eb1, L0_ffn_ew2, L0_ffn_eb2, L0_ffn_gens, L0_ffn_gc_w, L0_ffn_gc_b):

    def _L0_attn_ref(x, q_w, q_b, kv_w, kv_b, o_w, o_b):
        import jax, jax.numpy as jnp
        import numpy as np
        B, T, C = (2, 256, 128)
        NH = 16
        HD = C // NH

        def build_alibi_bias(n_head, max_len):
            slopes = jnp.arange(1, n_head + 1, dtype=jnp.float32) / n_head
            ar = jnp.arange(max_len, dtype=jnp.float32)
            return slopes[:, None, None] * (ar[None, None, :] - ar[None, :, None])
        Bx, Tx, Cx = x.shape
        q = (x @ q_w + q_b).reshape(Bx, Tx, NH, HD).transpose(0, 2, 1, 3)
        kv = (x @ kv_w + kv_b).reshape(Bx, Tx, 2, NH, HD).transpose(2, 0, 3, 1, 4)
        k, v = (kv[0], kv[1])
        att = jnp.einsum('bhqd,bhkd->bhqk', q, k) * (1.0 / np.sqrt(HD))
        att = att + build_alibi_bias(NH, Tx)[None]
        causal = jnp.tril(jnp.ones((Tx, Tx), dtype=bool))
        att = jnp.where(causal[None, None], att, -jnp.inf)
        att = jax.nn.softmax(att, axis=-1)
        y = jnp.einsum('bhqk,bhkd->bhqd', att, v)
        y = y.transpose(0, 2, 1, 3).reshape(Bx, Tx, Cx)
        return y @ o_w + o_b

    def _L0_ffn_ref(x, ln_gamma, ln_beta, abel_w, abel_b, moe_gate_w, moe_gate_b, ew1, eb1, ew2, eb2, gens, gc_w, gc_b):
        import jax, jax.numpy as jnp
        import numpy as np
        from jax.scipy.linalg import expm
        B, S, D, E, K, NROT = (2, 256, 128, 8, 2, 3)
        EPS = 1e-05

        def _gelu(x):
            return jax.nn.gelu(x, approximate=False)

        def _forward(x, ln_gamma, ln_beta, abel_w, abel_b, moe_gate_w, moe_gate_b, ew1, eb1, ew2, eb2, gens, gc_w, gc_b):
            residual = x
            mu = jnp.mean(x, axis=-1, keepdims=True)
            var = jnp.mean((x - mu) ** 2, axis=-1, keepdims=True)
            xn = (x - mu) * jax.lax.rsqrt(var + EPS) * ln_gamma + ln_beta
            abel_out = _gelu(xn @ abel_w + abel_b)
            logits = xn @ moe_gate_w + moe_gate_b
            topw, topi = jax.lax.top_k(logits, K)
            topw = jax.nn.softmax(topw, axis=-1)
            w_dense = jnp.sum(jax.nn.one_hot(topi, E, dtype=xn.dtype) * topw[..., None], axis=-2)
            h = _gelu(jnp.einsum('bsd,edh->ebsh', xn, ew1) + eb1[:, None, None, :])
            eo = jnp.einsum('ebsh,ehd->ebsd', h, ew2) + eb2[:, None, None, :]
            moe_out = jnp.einsum('ebsd,bse->bsd', eo, w_dense)
            for i in range(NROT):
                moe_out = moe_out @ expm(gens[i])
            combined = jnp.concatenate([abel_out, moe_out], axis=-1)
            gate = jax.nn.sigmoid(combined @ gc_w + gc_b)
            mixed = abel_out * (1.0 - gate) + moe_out * gate
            return residual + mixed
        return _forward(x, ln_gamma, ln_beta, abel_w, abel_b, moe_gate_w, moe_gate_b, ew1, eb1, ew2, eb2, gens, gc_w, gc_b)
    x = L0_attn_x
    x = x + 0.5 * _L0_ffn_ref(_layernorm(x, axis=-1), L0_ffn_ln_gamma, L0_ffn_ln_beta, L0_ffn_abel_w, L0_ffn_abel_b, L0_ffn_moe_gate_w, L0_ffn_moe_gate_b, L0_ffn_ew1, L0_ffn_eb1, L0_ffn_ew2, L0_ffn_eb2, L0_ffn_gens, L0_ffn_gc_w, L0_ffn_gc_b)
    x = x + _L0_attn_ref(_layernorm(x, axis=-1), L0_attn_q_w, L0_attn_q_b, L0_attn_kv_w, L0_attn_kv_b, L0_attn_o_w, L0_attn_o_b)
    x = x + 0.5 * _L0_ffn_ref(_layernorm(x, axis=-1), L0_ffn_ln_gamma, L0_ffn_ln_beta, L0_ffn_abel_w, L0_ffn_abel_b, L0_ffn_moe_gate_w, L0_ffn_moe_gate_b, L0_ffn_ew1, L0_ffn_eb1, L0_ffn_ew2, L0_ffn_eb2, L0_ffn_gens, L0_ffn_gc_w, L0_ffn_gc_b)
    return x

_drawn_inputs = setup_inputs


def setup_inputs(seed=0):
    import zlib

    import numpy as np

    out = dict(_drawn_inputs(seed))
    spreads = {'L0_attn_q_b': (0.0, 0.8), 'L0_attn_kv_b': (0.0, 0.529), 'L0_attn_o_b': (0.0, 0.1)}
    factors = {'L0_attn_q_w': 8.0,
     'L0_attn_kv_w': 3.245,
     'L0_ffn_ln_gamma': 8.0,
     'L0_ffn_ln_beta': 8.0,
     'L0_ffn_abel_b': 8.0,
     'L0_ffn_moe_gate_w': 7.639,
     'L0_ffn_moe_gate_b': 8.0,
     'L0_ffn_ew1': 7.527,
     'L0_ffn_eb1': 8.0,
     'L0_ffn_ew2': 7.393,
     'L0_ffn_eb2': 8.0,
     'L0_ffn_gens': 8.0,
     'L0_ffn_gc_w': 8.0}
    for name, (base, spread) in spreads.items():
        noise = np.random.default_rng([zlib.crc32(name.encode()), seed]).standard_normal(out[name].shape)
        drawn = base * np.exp(spread * noise) if base else spread * noise
        out[name] = jnp.asarray(drawn.astype(out[name].dtype))
    for name, factor in factors.items():
        out[name] = (out[name] * factor).astype(out[name].dtype)
    return out
```

```python
from contextlib import ExitStack

import numpy as np

import concourse.bass as bass
from concourse import mybir

FP32 = mybir.dt.float32
FP32R = mybir.dt.float32r
BF16 = mybir.dt.bfloat16
U32 = mybir.dt.uint32
ALU = mybir.AluOpType
ACT = mybir.ActivationFunctionType
AX = mybir.AxisListType

P = 128
BATCH, SEQ, D = 8, 512, 128
NT = SEQ // P
CH = BATCH
NH = 16
HD = D // NH
NG = 4
NQ = NH // NG
E = 8
HID = 2 * D
NJ = HID // P
NROT = 3
EPS = 1e-5
SCALE = HD ** -0.5
MASKED = -1e30
SQUARINGS = 18
TAYLOR = 11

ROW_BIAS = 3 * HD
ROW_MAX = ROW_BIAS + 3
Q_PARTS = (0, 0, 1)
K_PARTS = (0, 1, 0)

UNITS = 10
N_UNITS = UNITS * NG
PT_KB = (0, 640, 1024, 512)
PT_W = 1280


def units():
    for q in range(0, NQ, 2):
        yield "full", q
        yield "mixed", q
        yield "full", q + 1
        yield "mixed", q + 1
        yield "pair", q


def early(item, last):
    return isinstance(item, int) and item <= last


class Steps:

    def __init__(self, sem, per):
        self.sem, self.per = sem, per

    def value(self, item, step=None):
        return item * self.per + (self.per if step is None else step)


class Run:

    def __init__(self, engine, steps, item):
        self.engine, self.steps, self.item, self.done = engine, steps, item, 0

    def step(self, instruction):
        instruction.then_inc(self.steps.sem, 1)
        self.done += 1

    def join(self):
        self.engine.wait_ge(self.steps.sem, self.steps.value(self.item, self.done))

    def join_alone(self, passed):
        self.join()
        self.engine.sem_inc(passed, 1)

    def end(self):
        assert self.done == self.steps.per, (self.done, self.steps.per)


def macaron_block(nc, x, q_w, q_b, k_w, k_b, v_w, v_b, o_w, o_b, ln_gamma, ln_beta, abel_w, abel_b,
                  moe_gate_w, moe_gate_b, ew1, eb1, ew2, eb2, gens, gc_w, gc_b,
                  ident_c, bias_q_c, bias_k_c, consts_c, out):
    ctx = ExitStack()
    with ctx:
        def sb(name, shape, dt=FP32):
            return ctx.enter_context(nc.sbuf_tensor(name, shape, dt))

        def bank(name, shape=(P, 512), dt=FP32):
            return ctx.enter_context(nc.psum_tensor(name, list(shape), dt))

        def sem(name):
            return ctx.enter_context(nc.semaphore(name))

        x_all = sb("x_all", [P, CH * NT, D])
        ident = sb("ident", [P, P])
        ident_bf = sb("ident_bf", [P, P], BF16)
        mask_qk = sb("mask_qk", [P, 2, P], BF16)
        mask_kq = sb("mask_kq", [P, 2, P], BF16)
        expert_no = sb("expert_no", [P, NT, E])
        expert_no_i = sb("expert_no_i", [P, NT, E], mybir.dt.int32)
        consts = sb("consts", [P, 2 * SQUARINGS + 1])
        w1_hi = sb("w1_hi", [P, E, HID], FP32R)
        w1_lo = sb("w1_lo", [P, E, HID], FP32R)
        w2_rot = sb("w2_rot", [P, E, NJ, D])
        b1_sb = sb("b1_sb", [P, E, NJ])
        b2_hi = sb("b2_hi", [P, D], FP32R)
        b2_rot = sb("b2_rot", [P, D], FP32R)
        W_Q, W_K, W_V, W_AB, W_G = (i * D for i in range(5))
        small_hi = sb("small_hi", [P, 4 * D + E], FP32R)
        small_lo = sb("small_lo", [P, 4 * D + E], FP32R)
        wo_sb = sb("wo_sb", [P, D])
        cols = sb("cols", [P, 8])
        C_GAMMA, C_BETA, C_QB, C_KB, C_GCB, C_QBS, C_GCBH, C_TMP = range(8)
        rows = sb("rows", [P, 5 * D + E])
        R_AB, R_VB, R_OB, R_G1, R_G2, R_GB = (i * D for i in range(6))
        stat = sb("stat", [P, NT, 6])
        mv = sb("mv", [P, NT, 2])
        var = sb("var", [P, 2, NT])
        rstd = sb("rstd", [P, 2, NT])
        minus_half = sb("minus_half", [P, 2, NT])
        logit = sb("logit", [P, NT, E])
        top = sb("top", [P, NT, 8])
        top_i = sb("top_i", [P, NT, 8], U32)
        top_f = sb("top_f", [P, NT, 2])
        gap, th = sb("gap", [P, NT]), sb("th", [P, NT])
        w12 = sb("w12", [P, NT, 2])
        pick = sb("pick", [P, 2, NT, E])
        w_exp = [sb(f"w_exp{i}", [P, NT, E]) for i in range(2)]
        w_hi = sb("w_hi", [P, NT, E], FP32R)
        z1, z2, thg, gate = (sb(n, [P, NT]) for n in ("z1", "z2", "thg", "gate"))
        wT = sb("wT", [P, SEQ], FP32R)
        work = sb("work", [P, 3 * SEQ])
        z = work[:, 0:SEQ].rearrange("p (t d) -> p t d", t=NT)
        xn = work[:, SEQ:2 * SEQ]
        ab_in = work[:, 2 * SEQ:3 * SEQ]
        parts = sb("parts", [P, 4, SEQ], FP32R)
        xn_hi, xn_lo = [parts[:, 0, :], parts[:, 2, :]], [parts[:, 1, :], parts[:, 3, :]]
        arena = sb("arena", [P, 2 * NQ * PT_W])
        taken = [0]

        def piece(*shape):
            n = int(np.prod(shape))
            ap = arena[:, taken[0]:taken[0] + n]
            taken[0] += n
            assert taken[0] <= 2 * NQ * PT_W
            if len(shape) == 2:
                return ap.rearrange("p (a b) -> p a b", a=shape[0])
            if len(shape) == 3:
                return ap.rearrange("p (a b c) -> p a b c", a=shape[0], b=shape[1])
            return ap

        w1_in = piece(E, HID)
        w2_in = piece(E, NJ, D)
        bias_k = piece(NQ, SEQ)
        bias_q = piece(NG, SEQ)
        small_w = piece(4 * D + E)
        b2_in = piece(D)
        b2_T = piece(P)
        b2_f = piece(D)
        w2_T = w1_in.rearrange("p e (j d) -> p e j d", j=NJ)
        taken[0] = 0
        hT = [piece(NJ, SEQ) for _ in range(2)]
        y = [piece(NT, D) for _ in range(2)]
        ab = [piece(NT, D) for _ in range(2)]
        moe = [piece(NT, D) for _ in range(2)]
        skip, diff = piece(NT, D), piece(NT, D)
        w_pad = piece(NT, P)
        dot = piece(NT, D)
        taken[0] = 0
        pT = [piece(NQ, PT_W) for _ in range(2)]
        xh, qf, kf, yn = z, xn, work[:, 2 * SEQ:3 * SEQ], z
        yT = xn.rearrange("p (t d) -> p t d", t=NT)
        x_hi, x_lo, qs, ks = parts[:, 0, :], parts[:, 1, :], parts[:, 2:4, :], parts[:, 0:2, :]
        qT = [sb(f"qT{i}", [P, NG, SEQ], FP32R) for i in range(2)]
        kZ = [sb(f"kZ{i}", [P, NH, SEQ], FP32R) for i in range(2)]
        vA = [sb(f"vA{i}", [P, NT, NH, HD + 1]) for i in range(2)]
        mx = sb("mx", [P, NT, NQ, NG])
        mx_h = sb("mx_h", [P, NT, NQ, NG], FP32R)
        mx2 = sb("mx2", [P, NT, NQ, 2, NG])
        mT_zero = sb("mT_zero", [34, SEQ], FP32R)
        mT, zero2 = mT_zero[0:32, :], mT_zero[32:34, :]
        oT = sb("oT", [P, NG, SEQ])
        rden = [sb(f"rden{i}", [P, NG, NQ]) for i in range(2)]
        o_flat = oT[:, :, :].rearrange("p a b -> p (a b)")
        gen_sb, gen_T, pow2, pow3, pow3_T = (
            o_flat[:, i * NROT * P:(i + 1) * NROT * P].rearrange("p (r n) -> p r n", r=NROT) for i in range(5))
        poly, poly2, exp_m, exp_T = (
            work[:, i * NROT * P:(i + 1) * NROT * P].rearrange("p (r n) -> p r n", r=NROT) for i in range(4))
        norm, norm_all, shrink_m = (sb(n, [P, NROT]) for n in ("norm", "norm_all", "shrink_m"))
        over = sb("over", [P, NROT, SQUARINGS])
        shrink = sb("shrink", [P, NROT, SQUARINGS])

        pair = bank("pair", (P, 2, 512))
        banks = [bank(f"bank{i}") for i in range(6)] + [pair[:, 0, :], pair[:, 1, :]]
        ps_up, ps_dn = banks[0:2], banks[2:4]
        ps_T, ps_w = banks[4], banks[5]
        DA = D + E
        ps_al = pair[:, :, 0:2 * DA].rearrange("p b (t n) -> p b t n", t=2)
        ps_a, ps_b, ps_o, ps_m = banks[0:2], banks[2:4], banks[4:6], banks[6:8]

        ld_x, ld_w, ld_gen, ld_bias = sem("ld_x"), sem("ld_w"), sem("ld_gen"), sem("ld_bias")
        LOADS_W = 19
        ld_pool = sem("ld_pool")
        cst = sem("cst")
        w_pad_zero = sem("w_pad_zero")
        v_ones = sem("v_ones")
        norm_ok, norm_max = sem("norm_ok"), sem("norm_max")
        bias_in = sem("bias_in")
        set_dve = Steps(sem("set_dve"), 10**6)
        scaled, genT_ok, pow2_ok, pow3_ok = sem("scaled"), sem("genT_ok"), sem("pow2_ok"), sem("pow3_ok")
        horner, squared = sem("horner"), sem("squared")
        rot_ok, w2T_ok, b2T_ok = sem("rot_ok"), sem("w2T_ok"), sem("b2T_ok")
        setup_pe = sem("setup_pe")
        w_ready = sem("w_ready")
        gelu_table = sem("gelu_table")
        passed = sem("passed")
        stored = sem("stored")
        ln = Steps(sem("ln"), 14)
        pw = Steps(sem("pw"), 1)
        yn1 = Steps(sem("yn1"), 2)
        tr = Steps(sem("tr"), 1)
        xnf = Steps(sem("xnf"), 1)
        split = Steps(sem("split"), 2)
        alg = Steps(sem("alg"), 1)
        route = Steps(sem("route"), 22)
        thd = Steps(sem("thd"), 1)
        abb = Steps(sem("abb"), 1)
        abg = Steps(sem("abg"), 1)
        wtr = Steps(sem("wtr"), 1)
        wtc = Steps(sem("wtc"), 1)
        bim = Steps(sem("bim"), 1)
        moe0 = Steps(sem("moe0"), 1)
        up = Steps(sem("up"), E * NJ)
        gel = Steps(sem("gel"), E * NJ)
        dn = Steps(sem("dn"), E)
        acc = Steps(sem("acc"), E * NT)
        fza = Steps(sem("fza"), 2 * NT)
        fth = Steps(sem("fth"), 1)
        fzb = Steps(sem("fzb"), 2 + NT)
        fsk = Steps(sem("fsk"), 1)
        fdf = Steps(sem("fdf"), 1)
        aln = Steps(sem("aln"), 14)
        pwa = Steps(sem("pwa"), 1)
        atr = Steps(sem("atr"), 1)
        asp = Steps(sem("asp"), 2)
        qpj, kpj, vpj = Steps(sem("qpj"), 1), Steps(sem("kpj"), 1), Steps(sem("vpj"), 1)
        qev, kev = Steps(sem("qev"), 1), Steps(sem("kev"), 1)
        qks = Steps(sem("qks"), 4)
        vev = Steps(sem("vev"), 1)
        N_OPD = 2 * 3 * NQ * 16 + NQ * 16
        opd = Steps(sem("opd"), N_OPD)
        sa = Steps(sem("sa"), N_UNITS)
        red = Steps(sem("red"), N_UNITS)
        mxs = Steps(sem("mxs"), 3)
        mtr = Steps(sem("mtr"), 1)
        mev = Steps(sem("mev"), 1)
        mdm = Steps(sem("mdm"), NQ * 16)
        sbq = Steps(sem("sbq"), N_UNITS)
        ex = Steps(sem("ex"), N_UNITS)
        pv = Steps(sem("pv"), NG)
        oev = Steps(sem("oev"), NG)
        otr = Steps(sem("otr"), NT)
        yno = Steps(sem("yno"), 2 * NT)
        ytr = Steps(sem("ytr"), 1)
        yev = Steps(sem("yev"), 1)
        opj = Steps(sem("opj"), 1)
        xob = Steps(sem("xob"), 1)
        xat = Steps(sem("xat"), 1)

        block = ctx.enter_context(nc.Block())

        def wait(engine, steps, item, step=None):
            engine.wait_ge(steps.sem, steps.value(item, step))

        def over_chunks(engine, body):
            body(0, 0, True, False)
            with engine.Fori(0, (CH - 2) // 2) as i:
                body(2 * i + 1, 1, False, False)
                body(2 * i + 2, 0, False, False)
            body(CH - 1, 1, False, True)

        def xs(b, t=None):
            if isinstance(b, int):
                return x_all[:, NT * b:NT * b + NT, :] if t is None else x_all[:, NT * b + t, :]
            if t is None:
                return x_all[:, bass.ds(NT * b, NT), :]
            return x_all[:, bass.ds(NT * b + t, 1), :].rearrange("p a d -> p (a d)")

        def over_tiles(row, width):
            return rows[:, row:row + width].unsqueeze(1).to_broadcast([P, NT, width])

        @block.sync
        def _(sp):
            sp.dma_start(gen_sb, gens.rearrange("r p n -> p r n")).then_inc(ld_gen, 16)
            sp.dma_start(consts[:, :], consts_c).then_inc(ld_gen, 16)
            sp.dma_start(ident[:, :], ident_c).then_inc(ld_gen, 16)
            for dst, src in ((small_w[:, W_AB:W_AB + D], abel_w), (small_w[:, W_Q:W_Q + D], q_w),
                             (small_w[:, W_K:W_K + D], k_w), (small_w[:, W_V:W_V + D], v_w), (small_w[:, W_G:W_G + E], moe_gate_w),
                             (wo_sb[:, :], o_w), (w1_in, ew1.rearrange("e p h -> p e h")),
                             (w2_in, ew2.rearrange("e (j p) d -> p e j d", p=P))):
                sp.dma_start(dst, src).then_inc(ld_w, 16)
            sp.dma_start(x_all[:, :, :], x.rearrange("b (t p) d -> p (b t) d", p=P)).then_inc(ld_x, 16)

            def operands(b, u, first):
                wait(sp, qks, b)
                if first:
                    sp.wait_ge(bias_in, 2 * (1 + NQ))
                    sp.wait_ge(cst, 7)
                else:
                    wait(sp, sbq, b - 2)
                for g in range(NQ):
                    for r in range(3):
                        row = 32 * g + HD * r
                        for src, dst, prt in ((qs, qT[u][row:row + HD, :, :], Q_PARTS),
                                                (ks, kZ[u][row:row + HD, NG * g:NG * g + NG, :], K_PARTS)):
                            heads = src[NG * HD * g:NG * HD * (g + 1), prt[r], :]
                            sp.dma_start(dst.bitcast(FP32), heads.bitcast(FP32)).then_inc(opd.sem, 16)
                    sp.dma_start(qT[u][32 * g + ROW_MAX:32 * g + ROW_MAX + 2, :, :].bitcast(FP32),
                                 zero2.bitcast(FP32).unsqueeze(1).to_broadcast([2, NG, SEQ])).then_inc(opd.sem, 16)

            def maxima(b, u):
                wait(sp, mev, b)
                for g in range(NQ):
                    sp.dma_start(qT[u][32 * g + ROW_MAX:32 * g + ROW_MAX + 2, :, :].bitcast(FP32),
                                 mT[8 * g:8 * g + 8, :].bitcast(FP32)).then_inc(mdm.sem, 16)

            operands(0, 0, True)
            maxima(0, 0)

            def batch(b, u, first, last):
                if not last:
                    operands(b + 1, 1 - u, first)
                    maxima(b + 1, 1 - u)

            over_chunks(sp, batch)

            ov = out.rearrange("b (t p) d -> p (b t) d", p=P)
            with sp.Fori(0, CH) as c:
                wait(sp, fzb, CH + c)
                sp.dma_start(ov[:, bass.ds(NT * c, NT), :], x_all[:, bass.ds(NT * c, NT), :]).then_inc(stored, 16)
            sp.wait_ge(stored, 16 * CH)

        @block.gpsimd
        def _(pool):
            nc.gpsimd.memset(b2_in, 0.0).then_inc(cst, 1)
            nc.gpsimd.memset(mask_qk[:, :, :], 0.0).then_inc(cst, 1)
            nc.gpsimd.memset(mask_kq[:, :, :], 0.0).then_inc(cst, 1)
            nc.gpsimd.iota(expert_no_i[:, :, :], pattern=[[0, NT], [1, E]], base=0,
                           channel_multiplier=0).then_inc(cst, 1)
            pool.wait_ge(cst, 4)
            nc.gpsimd.affine_select(out=mask_qk[:, :, :], in_=mask_qk[:, :, :], compare_op=ALU.is_ge,
                                    fill=MASKED, base=0, pattern=[[0, 2], [-1, P]],
                                    channel_multiplier=1).then_inc(cst, 1)
            nc.gpsimd.affine_select(out=mask_kq[:, :, :], in_=mask_kq[:, :, :], compare_op=ALU.is_ge,
                                    fill=MASKED, base=0, pattern=[[0, 2], [1, P]],
                                    channel_multiplier=-1).then_inc(cst, 1)
            for part in range(3):
                pool.dma_start(b2_in[E * part:E * (part + 1), :], eb2).then_inc(ld_pool, 16)
            pool.dma_start(b1_sb[:, :, :], eb1).then_inc(ld_pool, 16)
            pool.wait_ge(norm_ok, 1)
            nc.gpsimd.partition_all_reduce(norm_all[:, :], norm[:, :], P,
                                           bass.bass_isa.ReduceOp.max).then_inc(norm_max, 1)
            pool.wait_ge(norm_max, 1)
            nc.gpsimd.memset(zero2.bitcast(FP32), 0.0).then_inc(cst, 1)
            pool.wait_ge(cst, 7)
            nc.gpsimd.memset(minus_half[:, :, :], -0.5).then_inc(cst, 1)
            for u in range(2):
                nc.gpsimd.memset(vA[u][:, :, :, HD:HD + 1], 1.0).then_inc(v_ones, 1)
            pool.wait_ge(w_ready, 1)
            nc.gpsimd.memset(w_pad, 0.0).then_inc(w_pad_zero, 1)
            pool.wait_ge(cst, 8)

            def inverse_roots(steps):
                nc.gpsimd.tensor_tensor(rstd[:, :, :], var[:, :, :], minus_half[:, :, :],
                                        ALU.pow).then_inc(steps.sem, 1)

            def ffn(layer):
                def roots(g):
                    wait(pool, ln, g, 10)
                    inverse_roots(pw)

                def first_norm(g, c, u):
                    wait(pool, pw, g)
                    if not early(g, 1):
                        wait(pool, fsk, g - 2)
                    nc.gpsimd.tensor_tensor(y[u], xs(c), mv[:, :, 0:1].to_broadcast([P, NT, D]),
                                            ALU.subtract).then_inc(yn1.sem, 1)
                    wait(pool, yn1, g, 1)
                    nc.gpsimd.tensor_tensor(y[u], y[u], rstd[:, 0, :].unsqueeze(2).to_broadcast([P, NT, D]),
                                            ALU.mult).then_inc(yn1.sem, 1)

                def difference(g, u):
                    wait(pool, acc, g)
                    if not early(g, 0):
                        wait(pool, fzb, g - 1)
                    nc.gpsimd.tensor_tensor(diff, moe[u], ab[u], ALU.subtract).then_inc(fdf.sem, 1)

                def chunk(c, u, first, last):
                    g = CH * layer + c
                    if not first:
                        difference(g - 1, 1 - u)
                    if not last:
                        roots(g + 1)
                        first_norm(g + 1, c + 1, 1 - u)
                    wait(pool, abg, g)
                    wait(pool, yn1, g)
                    if not early(g, 0):
                        wait(pool, fzb, g - 1, 1)
                    nc.gpsimd.tensor_tensor(skip, y[u], ab[u], ALU.add).then_inc(fsk.sem, 1)

                roots(CH * layer)
                first_norm(CH * layer, 0, 0)
                over_chunks(pool, chunk)
                difference(CH * layer + CH - 1, 1)

            ffn(0)

            def obias(b, u, first, last):
                wait(pool, aln, b, 10)
                inverse_roots(pwa)
                wait(pool, aln, b)
                nc.gpsimd.tensor_tensor(xs(b), xs(b), over_tiles(R_OB, D),
                                        ALU.add).then_inc(xob.sem, 1)
            over_chunks(pool, obias)
            wait(pool, pv, BATCH - 1)
            nc.gpsimd.memset(w_pad, 0.0).then_inc(w_pad_zero, 1)
            ffn(1)

        @block.scalar
        def _(act):
            act.dma_start(bias_k, bias_k_c).then_inc(ld_bias, 16)
            act.dma_start(bias_q, bias_q_c).then_inc(ld_bias, 16)
            for dst, vec in ((C_GAMMA, ln_gamma), (C_BETA, ln_beta), (C_QB, q_b), (C_KB, k_b)):
                act.dma_start(cols[:, dst:dst + 1], vec.rearrange("(p a) -> p a", a=1)).then_inc(ld_w, 16)
            act.dma_start(cols[:, C_GCB:C_GCB + 1], gc_b.partition_broadcast(P)).then_inc(ld_w, 16)
            for dst, vec in ((R_AB, abel_b), (R_VB, v_b), (R_OB, o_b),
                             (R_G1, gc_w[0:D, 0]), (R_G2, gc_w[D:2 * D, 0]), (R_GB, moe_gate_b)):
                n = vec.shape[0]
                act.dma_start(rows[:, dst:dst + n], vec.partition_broadcast(P)).then_inc(ld_w, 16)
            act.wait_ge(ld_bias, 32)
            for u in range(2):
                nc.scalar.activation(qT[u][:, :, :], bias_q, ACT.Copy).then_inc(bias_in, 1)
                for g in range(NQ):
                    nc.scalar.activation(kZ[u][:, NG * g:NG * g + NG, :], bias_k[:, g:g + 1, :].to_broadcast([P, NG, SEQ]),
                                         ACT.Copy).then_inc(bias_in, 1)
            act.wait_ge(w_ready, 1)
            nc.scalar.activation(cols[:, C_TMP:C_TMP + 1], cols[:, C_BETA:C_BETA + 1],
                                 ACT.Gelu).then_inc(gelu_table, 1)

            def ffn(layer):
                def xn_(g):
                    wait(act, tr, g)
                    if not early(g, 0):
                        wait(act, split, g - 1)
                    nc.scalar.activation(xn, ps_T[:, :], ACT.Identity, bias=cols[:, C_BETA:C_BETA + 1],
                                         scale=cols[:, C_GAMMA:C_GAMMA + 1]).then_inc(xnf.sem, 1)

                def tanh_gap(g):
                    wait(act, route, g, 10)
                    nc.scalar.activation(th[:, :], gap[:, :], ACT.Tanh, scale=0.5).then_inc(thd.sem, 1)

                def abel(g, u):
                    wait(act, abb, g)
                    if not early(g, 1):
                        wait(act, fzb, g - 2)
                    nc.scalar.activation(ab[u], ab_in.rearrange("p (t d) -> p t d", t=NT),
                                         ACT.Gelu).then_inc(abg.sem, 1)

                def w_rows(g):
                    wait(act, wtr, g)
                    if not early(g, 0):
                        wait(act, bim, g - 1)
                    nc.scalar.activation(wT[:, :], ps_w[:, :], ACT.Copy).then_inc(wtc.sem, 1)

                def moe_start(g, u):
                    wait(act, bim, g)
                    if not early(g, 1):
                        wait(act, fzb, g - 2)
                    nc.scalar.activation(moe[u], ps_w[:, :].rearrange("p (t d) -> p t d", t=NT),
                                         ACT.Copy).then_inc(moe0.sem, 1)

                def hidden(g, e):
                    for j in range(NJ):
                        n = 2 * e + j
                        wait(act, up, g, n + 1)
                        if not (early(g, 0) and e < 2):
                            act.wait_ge(dn.sem, dn.value(g, e - 1))
                        nc.scalar.activation(hT[e % 2][:, j, :], ps_up[j][:, :], ACT.Gelu,
                                             bias=b1_sb[:, e, j:j + 1]).then_inc(gel.sem, 1)

                def gate_tanh(g):
                    wait(act, fza, g)
                    nc.scalar.activation(thg[:, :], z2[:, :], ACT.Tanh, bias=cols[:, C_GCBH:C_GCBH + 1],
                                         scale=0.5).then_inc(fth.sem, 1)

                def chunk(c, u, first, last):
                    g = CH * layer + c
                    hidden(g, 0)
                    w_rows(g)
                    hidden(g, 1)
                    moe_start(g, u)
                    hidden(g, 2)
                    if not first:
                        gate_tanh(g - 1)
                    hidden(g, 3)
                    if not last:
                        xn_(g + 1)
                    for e in range(4, E):
                        hidden(g, e)
                    if not last:
                        abel(g + 1, 1 - u)
                        tanh_gap(g + 1)

                g0 = CH * layer
                xn_(g0)
                abel(g0, 0)
                tanh_gap(g0)
                over_chunks(act, chunk)
                gate_tanh(g0 + CH - 1)

            def attention():
                def q_k(b):
                    wait(act, qpj, b)
                    if early(b, 0):
                        wait(act, split, CH - 1)
                    elif early(b, 1):
                        wait(act, qks, b - 1)
                    nc.scalar.activation(qf, ps_m[1][:, :], ACT.Identity, bias=cols[:, C_QBS:C_QBS + 1],
                                         scale=SCALE).then_inc(qev.sem, 1)
                    wait(act, kpj, b)
                    nc.scalar.activation(kf, ps_m[0][:, :], ACT.Identity, bias=cols[:, C_KB:C_KB + 1]).then_inc(kev.sem, 1)

                def exps(b, t):
                    n = UNITS * t
                    for i, (kind, q) in enumerate(units()):
                        wait(act, sbq, b, n + i + 1)
                        if i == 0 and not (early(b, 0) and t < 2):
                            act.wait_ge(pv.sem, pv.value(b, t - 1))
                        if kind == "full":
                            dst, src = pT[t % 2][:, q, 0:512], ps_b[i % 2][:, :]
                        elif kind == "mixed":
                            dst, src = pT[t % 2][:, q, 512:1024], ps_b[i % 2][:, :]
                        else:
                            dst = pT[t % 2][:, q:q + 2, 1024:PT_W]
                            src = ps_b[i % 2][:, :].rearrange("p (h n) -> p h n", h=2)
                        nc.scalar.activation(dst, src, ACT.Exp).then_inc(ex.sem, 1)

                def o_evac(b, t):
                    act.wait_ge(pv.sem, pv.value(b, t + 1))
                    if not early(b, 0):
                        wait(act, otr, b - 1)
                    nc.scalar.activation(oT[:, t, :], ps_o[t % 2][:, :], ACT.Copy).then_inc(oev.sem, 1)

                def y_evac(b, last):
                    wait(act, ytr, b)
                    if not last:
                        wait(act, qks, b + 2)
                    nc.scalar.activation(yT, ps_m[0][:, :].rearrange("p (t d) -> p t d", t=NT),
                                         ACT.Copy).then_inc(yev.sem, 1)

                def batch(b, u, first, last):
                    if not first:
                        o_evac(b - 1, 3)
                    if not last:
                        q_k(b + 1)
                    exps(b, 0)
                    if not first:
                        y_evac(b - 1, last)
                    exps(b, 1)
                    o_evac(b, 0)
                    exps(b, 2)
                    o_evac(b, 1)
                    exps(b, 3)
                    o_evac(b, 2)

                q_k(0)
                over_chunks(act, batch)
                o_evac(BATCH - 1, 3)
                y_evac(BATCH - 1, True)

            ffn(0)
            attention()
            nc.scalar.activation(cols[:, C_TMP:C_TMP + 1], cols[:, C_BETA:C_BETA + 1],
                                 ACT.Gelu).then_inc(gelu_table, 1)
            ffn(1)

        @block.vector
        def _(dve):
            v = nc.vector
            s = Run(dve, set_dve, 0)

            def hand(semaphore):
                s.join()
                dve.sem_inc(semaphore, 1)

            dve.wait_ge(ld_gen, 48)
            v.tensor_reduce(norm[:, :], gen_sb, AX.X, ALU.add,
                            apply_absolute_value=True).then_inc(norm_ok, 1)
            s.step(v.tensor_copy(ident_bf[:, :], ident[:, :]))
            dve.wait_ge(cst, 6)
            s.step(v.tensor_copy(expert_no[:, :, :], expert_no_i[:, :, :]))
            dve.wait_ge(norm_max, 1)
            for r in range(NROT):
                s.step(v.tensor_scalar(over[:, r, :], consts[:, 0:SQUARINGS], norm_all[:, r:r + 1], None,
                                       ALU.is_lt))
            s.join()
            s.step(v.tensor_tensor(shrink[:, :, :], over[:, :, :],
                                   consts[:, SQUARINGS:2 * SQUARINGS].unsqueeze(1)
                                   .to_broadcast([P, NROT, SQUARINGS]), ALU.mult))
            s.join()
            s.step(v.tensor_scalar(shrink[:, :, :], shrink[:, :, :], 1.0, None, ALU.add))
            s.join()
            s.step(v.tensor_reduce(shrink_m[:, :], shrink[:, :, :], AX.X, ALU.min))
            s.join()
            for r in range(NROT):
                s.step(v.tensor_scalar(gen_sb[:, r, :], gen_sb[:, r, :], shrink_m[:, r:r + 1], None, ALU.mult))
            hand(scaled)

            dve.wait_ge(ld_w, LOADS_W * 16)
            dve.wait_ge(ld_pool, 4 * 16)
            s.step(v.tensor_copy(small_hi[:, :], small_w))
            s.step(v.tensor_scalar(cols[:, C_QBS:C_QBS + 1], cols[:, C_QB:C_QB + 1], SCALE, None, ALU.mult))
            s.step(v.tensor_scalar(cols[:, C_GCBH:C_GCBH + 1], cols[:, C_GCB:C_GCB + 1], 0.5, None, ALU.mult))
            s.step(v.tensor_copy(w1_hi[:, :, :], w1_in))
            s.join()
            s.step(v.tensor_tensor(small_lo[:, :], small_w, small_hi[:, :].bitcast(FP32), ALU.subtract))
            s.step(v.tensor_tensor(w1_lo[:, :, :], w1_in, w1_hi[:, :, :].bitcast(FP32), ALU.subtract))

            fact = [1.0]
            for k in range(1, TAYLOR + 1):
                fact.append(fact[-1] / k)
            identity = ident[:, :].unsqueeze(1).to_broadcast([P, NROT, P])

            def product(i):
                return banks[i][:, 0:NROT * P].rearrange("p (r n) -> p r n", r=NROT)

            dve.wait_ge(setup_pe, 1)
            s.step(v.tensor_copy(gen_T, product(0)))
            hand(genT_ok)
            dve.wait_ge(setup_pe, 2)
            s.step(v.tensor_copy(pow2, product(1)))
            hand(pow2_ok)
            dve.wait_ge(setup_pe, 4)
            s.step(v.tensor_copy(pow3_T, product(3)))
            hand(pow3_ok)

            def series(dst, k):
                s.step(v.tensor_scalar(poly, gen_sb, fact[k + 1], None, ALU.mult))
                s.join()
                s.step(v.scalar_tensor_tensor(poly, pow2, fact[k + 2], poly, ALU.mult, ALU.add))
                s.join()
                s.step(v.scalar_tensor_tensor(dst, identity, fact[k], poly, ALU.mult, ALU.add))
                s.join()

            series(exp_m, 9)
            hand(horner)
            for i, k in enumerate((6, 3, 0)):
                series(poly2, k)
                dve.wait_ge(setup_pe, 5 + i)
                s.step(v.tensor_tensor(exp_m, product(i % 2), poly2, ALU.add))
                hand(horner)
            dve.wait_ge(setup_pe, 8)
            s.step(v.tensor_copy(exp_T, product(2)))
            hand(squared)
            for i in range(SQUARINGS):
                chosen = over[:, :, i:i + 1].bitcast(U32).to_broadcast([P, NROT, P])
                dve.wait_ge(setup_pe, 10 + 2 * i)
                s.step(v.copy_predicated(exp_m, chosen, product(2 * (i % 2))))
                s.step(v.copy_predicated(exp_T, chosen, product(1 + 2 * (i % 2))))
                hand(squared)
            n = 9 + 2 * SQUARINGS
            dve.wait_ge(setup_pe, n)
            s.step(v.tensor_copy(poly[:, 0, :], banks[4][:, 0:P]))
            hand(rot_ok)
            dve.wait_ge(setup_pe, n + 1)
            s.step(v.tensor_copy(poly[:, 1, :], banks[5][:, 0:P]))
            hand(rot_ok)
            for q in range(4):
                dve.wait_ge(setup_pe, n + 2 + q)
                s.step(v.tensor_copy(w2_T[:, 2 * q:2 * q + 2, :, :],
                                     banks[q][:, :].rearrange("p (e j d) -> p e j d", e=2, j=NJ)))
            hand(w2T_ok)
            dve.wait_ge(setup_pe, n + 6)
            s.step(v.tensor_copy(b2_T, banks[6][:, 0:P]))
            hand(b2T_ok)
            for q in range(4):
                dve.wait_ge(setup_pe, n + 7 + q)
                s.step(v.tensor_copy(w2_rot[:, 2 * q:2 * q + 2, :, :],
                                     banks[q][:, :].rearrange("p (e j d) -> p e j d", e=2, j=NJ)))
            dve.wait_ge(setup_pe, n + 11)
            s.step(v.tensor_copy(b2_f, banks[7][:, 0:D]))
            s.join()
            s.step(v.tensor_copy(b2_hi[:, :], b2_f))
            s.join()
            s.step(v.scalar_tensor_tensor(b2_rot[:, :], b2_hi[:, :].bitcast(FP32),
                                          consts[:, 2 * SQUARINGS:2 * SQUARINGS + 1], b2_f, ALU.mult, ALU.add))
            dve.wait_ge(bias_in, 2 * (1 + NQ))
            s.join()
            dve.sem_inc(w_ready, 1)

            def statistics(run, src):
                for t in range(NT):
                    run.step(v.bn_stats(stat[:, t, :], src(t)))
                run.join_alone(passed)
                for t in range(NT):
                    run.step(v.bn_aggr(mv[:, t, :], stat[:, t, :]))
                run.join()
                run.step(v.tensor_scalar(var[:, 0, :], mv[:, :, 1], EPS, None, ALU.add))
                run.step(v.tensor_scalar(var[:, 1, :], mv[:, :, 1], 1.0 + EPS, EPS * EPS, ALU.mult, ALU.add))

            def normalise_tiles(run, src, rs, dst):
                for t in range(NT):
                    run.step(v.tensor_scalar(dst(t), src(t), mv[:, t, 0:1], rs[:, t:t + 1],
                                             ALU.subtract, ALU.mult))

            def ffn(layer):
                def stats_(g, c):
                    if not early(g, 0):
                        wait(dve, yn1, g - 1)
                    run = Run(dve, ln, g)
                    statistics(run, lambda t: xs(c, t))

                def norms(g, c):
                    run = Run(dve, ln, g)
                    run.done = 10
                    wait(dve, pw, g)
                    if isinstance(g, int) and g == CH:
                        wait(dve, atr, BATCH - 1)
                    elif not early(g, 0):
                        wait(dve, tr, g - 1)
                    normalise_tiles(run, lambda t: xs(c, t), rstd[:, 1, :], lambda t: z[:, t, :])
                    run.end()

                def split_(g, u):
                    run = Run(dve, split, g)
                    wait(dve, xnf, g)
                    if isinstance(g, int) and g == CH:
                        wait(dve, vpj, BATCH - 1)
                    elif not early(g, 1):
                        wait(dve, up, g - 2)
                    run.step(v.tensor_copy(xn_hi[u], xn))
                    run.join()
                    run.step(v.tensor_tensor(xn_lo[u], xn, xn_hi[u].bitcast(FP32), ALU.subtract))
                    run.end()

                def top_two(g):
                    run = Run(dve, route, g)
                    wait(dve, alg, g)
                    run.step(v.tensor_tensor(logit[:, :, :].rearrange("p (b t) e -> p b t e", b=2),
                                             ps_al[:, :, :, D:DA],
                                             rows[:, R_GB:R_GB + E].unsqueeze(1).unsqueeze(1)
                                             .to_broadcast([P, 2, 2, E]), ALU.add))
                    run.join_alone(passed)
                    for t in range(NT):
                        run.step(v.max(top[:, t, :], logit[:, t, :]))
                    run.join_alone(passed)
                    for t in range(NT):
                        run.step(v.max_index(top_i[:, t, :], top[:, t, :], logit[:, t, :]))
                    run.step(v.tensor_tensor(gap[:, :], top[:, :, 0], top[:, :, 1], ALU.subtract))

                def expert_weights(g, u):
                    run = Run(dve, route, g)
                    run.done = 10
                    run.join()
                    run.step(v.tensor_copy(top_f[:, :, :], top_i[:, :, 0:2]))
                    run.join()
                    for k in range(2):
                        run.step(v.tensor_tensor(pick[:, k, :, :], expert_no[:, :, :],
                                                 top_f[:, :, k:k + 1].to_broadcast([P, NT, E]), ALU.is_equal))
                    wait(dve, thd, g)
                    run.step(v.tensor_scalar(w12[:, :, 0], th[:, :], 0.5, 0.5, ALU.mult, ALU.add))
                    run.step(v.tensor_scalar(w12[:, :, 1], th[:, :], -0.5, 0.5, ALU.mult, ALU.add))
                    run.join()
                    for k in range(2):
                        run.step(v.tensor_tensor(pick[:, k, :, :], pick[:, k, :, :],
                                                 w12[:, :, k:k + 1].to_broadcast([P, NT, E]), ALU.mult))
                    run.join()
                    run.step(v.tensor_tensor(w_exp[u][:, :, :], pick[:, 0, :, :], pick[:, 1, :, :], ALU.add))
                    run.join()
                    run.step(v.tensor_copy(w_hi[:, :, :], w_exp[u][:, :, :]))
                    run.join()
                    if early(g, 0) or (isinstance(g, int) and g == CH):
                        dve.wait_ge(w_pad_zero, 1 + layer)
                    else:
                        wait(dve, wtr, g - 1)
                    run.step(v.tensor_copy(w_pad[:, :, 0:E], w_hi[:, :, :].bitcast(FP32)))
                    run.step(v.tensor_tensor(w_pad[:, :, E:2 * E], w_exp[u][:, :, :],
                                             w_hi[:, :, :].bitcast(FP32), ALU.subtract))
                    run.step(v.tensor_copy(w_pad[:, :, 2 * E:3 * E], w_hi[:, :, :].bitcast(FP32)))
                    run.end()

                def abel_bias(g):
                    wait(dve, alg, g)
                    if not early(g, 0):
                        wait(dve, abg, g - 1)
                    v.tensor_tensor(ab_in.rearrange("p (b t d) -> p b t d", b=2, t=2), ps_al[:, :, :, 0:D],
                                    rows[:, R_AB:R_AB + D].unsqueeze(1).unsqueeze(1)
                                    .to_broadcast([P, 2, 2, D]), ALU.add).then_inc(abb.sem, 1)

                def accumulate(g, u, e):
                    wait(dve, dn, g, e + 1)
                    if e == 0:
                        wait(dve, moe0, g)
                    else:
                        wait(dve, acc, g, NT * e)
                    for t in range(NT):
                        v.scalar_tensor_tensor(moe[u][:, t, :], ps_dn[e % 2][:, t * D:(t + 1) * D],
                                               w_exp[u][:, t, e:e + 1], moe[u][:, t, :],
                                               ALU.mult, ALU.add).then_inc(acc.sem, 1)

                def gate_dots(g, src, row, ins, outs, step):
                    run = Run(dve, fza, g)
                    run.done = step
                    if step:
                        wait(dve, acc, g)
                        run.join()
                    else:
                        wait(dve, abg, g)
                        if not early(g, 0):
                            wait(dve, fza, g - 1)
                    for t in range(NT):
                        run.step(v.tensor_tensor_reduce(out=dot[:, t, :], in0=src[:, t, :], in1=rows[:, row:row + D],
                                                        scale=1.0, scalar=ins(t), op0=ALU.mult, op1=ALU.add,
                                                        accum_out=outs[:, t:t + 1]))

                def abel_dots(g, u):
                    gate_dots(g, ab[u], R_G1, lambda t: 0.0, z1, 0)

                def moe_dots(g, u):
                    gate_dots(g, moe[u], R_G2, lambda t: z1[:, t:t + 1], z2, NT)

                def finish_skip(g, c):
                    run = Run(dve, fzb, g)
                    wait(dve, fsk, g)
                    run.step(v.scalar_tensor_tensor(xs(c), skip, 0.5, xs(c), ALU.mult, ALU.add))

                def finish_gate(g, c):
                    run = Run(dve, fzb, g)
                    run.done = 1
                    wait(dve, fth, g)
                    run.step(v.tensor_scalar(gate[:, :], thg[:, :], 0.25, 0.25, ALU.mult, ALU.add))
                    wait(dve, fdf, g)
                    run.join()
                    for t in range(NT):
                        run.step(v.scalar_tensor_tensor(xs(c, t), diff[:, t, :], gate[:, t:t + 1], xs(c, t),
                                                        ALU.mult, ALU.add))
                    run.end()

                def chunk(c, u, first, last):
                    g = CH * layer + c
                    if not last:
                        stats_(g + 1, c + 1)
                    accumulate(g, u, 0)
                    if not last:
                        norms(g + 1, c + 1)
                    accumulate(g, u, 1)
                    if not first:
                        finish_skip(g - 1, c - 1)
                    accumulate(g, u, 2)
                    if not first:
                        finish_gate(g - 1, c - 1)
                    accumulate(g, u, 3)
                    if not last:
                        split_(g + 1, 1 - u)
                    accumulate(g, u, 4)
                    abel_dots(g, u)
                    accumulate(g, u, 5)
                    if not last:
                        abel_bias(g + 1)
                        top_two(g + 1)
                    accumulate(g, u, 6)
                    if not last:
                        expert_weights(g + 1, 1 - u)
                    accumulate(g, u, 7)
                    moe_dots(g, u)

                g0 = CH * layer
                stats_(g0, 0)
                norms(g0, 0)
                split_(g0, 0)
                abel_bias(g0)
                top_two(g0)
                expert_weights(g0, 0)
                over_chunks(dve, chunk)
                finish_skip(g0 + CH - 1, CH - 1)
                finish_gate(g0 + CH - 1, CH - 1)

            def attention():
                def norms(b):
                    run = Run(dve, aln, b)
                    if early(b, 0):
                        wait(dve, tr, CH - 1)
                    else:
                        wait(dve, atr, b - 1)
                    statistics(run, lambda t: xs(b, t))
                    wait(dve, pwa, b)
                    normalise_tiles(run, lambda t: xs(b, t), rstd[:, 0, :], lambda t: xh[:, t, :])
                    run.end()

                def split_(b):
                    run = Run(dve, asp, b)
                    wait(dve, atr, b)
                    if early(b, 0):
                        wait(dve, up, CH - 1)
                    else:
                        wait(dve, opd, b - 1)
                    run.step(v.tensor_copy(x_hi, ps_m[0][:, :]))
                    run.join()
                    run.step(v.tensor_tensor(x_lo, ps_m[0][:, :], x_hi.bitcast(FP32), ALU.subtract))
                    run.end()

                def split_qk(b):
                    run = Run(dve, qks, b)
                    wait(dve, qev, b)
                    run.step(v.tensor_copy(qs[:, 0, :], qf))
                    wait(dve, kev, b)
                    wait(dve, vpj, b)
                    run.step(v.tensor_copy(ks[:, 0, :], kf))
                    run.join()
                    run.step(v.tensor_tensor(qs[:, 1, :], qf, qs[:, 0, :].bitcast(FP32), ALU.subtract))
                    run.step(v.tensor_tensor(ks[:, 1, :], kf,
                                             ks[:, 0, :].bitcast(FP32), ALU.subtract))
                    run.end()

                def v_evac(b, u):
                    wait(dve, vpj, b)
                    if early(b, 0):
                        dve.wait_ge(v_ones, 2)
                    if not early(b, 1):
                        wait(dve, pv, b - 2)
                    v.tensor_tensor(vA[u][:, :, :, 0:HD],
                                    ps_m[1][:, :].rearrange("p (t h d) -> p t h d", t=NT, h=NH),
                                    rows[:, R_VB:R_VB + D].rearrange("p (h d) -> p h d", h=NH).unsqueeze(1)
                                    .to_broadcast([P, NT, NH, HD]), ALU.add).then_inc(vev.sem, 1)

                def reduce_(b, n):
                    t, i = divmod(n, UNITS)
                    kind, q = list(units())[i]
                    wait(dve, sa, b, n + 1)
                    if n == 0 and not early(b, 0):
                        wait(dve, mxs, b - 1)
                    src = ps_a[n % 2]
                    if kind == "full":
                        v.tensor_reduce(mx[:, 3, q, t:t + 1], src[:, :], AX.X, ALU.max).then_inc(red.sem, 1)
                    elif kind == "mixed":
                        v.tensor_reduce(mx[:, 2, q, t:t + 1], src[:, 0:384], AX.X, ALU.max)
                        v.tensor_reduce(mx[:, 0, q, t:t + 1], src[:, 384:512], AX.X, ALU.max).then_inc(red.sem, 1)
                    else:
                        v.tensor_reduce(mx[:, 1, q:q + 2, t], src[:, :].rearrange("p (h n) -> p h n", h=2),
                                        AX.X, ALU.max).then_inc(red.sem, 1)

                def maxima(b):
                    run = Run(dve, mxs, b)
                    wait(dve, red, b)
                    run.step(v.tensor_scalar(mx_h[:, :, :, :], mx[:, :, :, :], -1.0, None, ALU.mult))
                    run.join()
                    if not early(b, 0):
                        wait(dve, mtr, b - 1)
                    mh = mx_h[:, :, :, :].bitcast(FP32)
                    run.step(v.tensor_copy(mx2[:, :, :, 0, :], mh))
                    run.step(v.scalar_tensor_tensor(mx2[:, :, :, 1, :], mx[:, :, :, :], -1.0, mh,
                                                    ALU.mult, ALU.subtract))
                    run.end()
                    wait(dve, mtr, b)
                    if not early(b, 0):
                        wait(dve, mdm, b - 1)
                    v.tensor_copy(mT, ps_m[0][0:32, :]).then_inc(mev.sem, 1)

                def normalise(b, i):
                    run = Run(dve, yno, b)
                    run.done = 2 * i
                    wait(dve, otr, b, i + 1)
                    src = ps_m[i % 2][:, :].rearrange("p (t q c) -> p t q c", t=NG, q=NQ)
                    if i == 0 and not early(b, 0):
                        wait(dve, ytr, b - 1)
                    run.step(v.reciprocal(rden[i % 2][:, :, :], src[:, :, :, HD]))
                    run.join()
                    run.step(v.tensor_tensor(yn[:, i, :].rearrange("p (q t c) -> p t q c", t=NG, q=NQ),
                                             src[:, :, :, 0:HD],
                                             rden[i % 2][:, :, :].unsqueeze(3).to_broadcast([P, NG, NQ, HD]), ALU.mult))

                def add_out(b):
                    wait(dve, opj, b)
                    wait(dve, xob, b)
                    v.tensor_tensor(xs(b), ps_m[1][:, :].rearrange("p (t d) -> p t d", t=NT), xs(b),
                                    ALU.add).then_inc(xat.sem, 1)

                def batch(b, u, first, last):
                    if not last:
                        norms(b + 1)
                        split_(b + 1)
                        split_qk(b + 1)
                        v_evac(b + 1, 1 - u)
                    if not first:
                        for i in range(NT):
                            normalise(b - 1, i)
                        add_out(b - 1)
                    if not last:
                        for n in range(N_UNITS):
                            reduce_(b + 1, n)
                        maxima(b + 1)

                norms(0)
                split_(0)
                split_qk(0)
                v_evac(0, 0)
                for n in range(N_UNITS):
                    reduce_(0, n)
                maxima(0)
                over_chunks(dve, batch)
                for i in range(NT):
                    normalise(BATCH - 1, i)
                add_out(BATCH - 1)

            dve.wait_ge(ld_x, 16)
            ffn(0)
            wait(dve, fzb, CH - 1)
            attention()
            wait(dve, xat, BATCH - 1)
            ffn(1)

        @block.tensor
        def _(pe):
            mm = nc.tensor.matmul

            def split_product(outp, a_hi, a_lo, b_hi, b_lo):
                mm(outp, a_hi, b_hi, start=True, stop=False)
                mm(outp, a_hi, b_lo, start=False, stop=False)
                return mm(outp, a_lo, b_hi, start=False, stop=True)

            def each(bank_, lhsT, rhs):
                for r in range(NROT):
                    last = mm(banks[bank_][:, r * P:(r + 1) * P], lhsT[:, r, :], rhs[:, r, :], start=True, stop=True)
                last.then_inc(setup_pe, 1)

            def each_transposed(bank_, src):
                for r in range(NROT):
                    last = nc.tensor.transpose(banks[bank_][:, r * P:(r + 1) * P], src[:, r, :], ident[:, :])
                last.then_inc(setup_pe, 1)

            pe.wait_ge(scaled, 1)
            each_transposed(0, gen_sb)
            pe.wait_ge(genT_ok, 1)
            each(1, gen_T, gen_sb)
            pe.wait_ge(pow2_ok, 1)
            each(2, gen_T, pow2)
            each(3, pow2, gen_T)
            pe.wait_ge(pow3_ok, 1)
            for i in range(3):
                pe.wait_ge(horner, 1 + i)
                each(i % 2, pow3_T, exp_m)
            pe.wait_ge(horner, 4)
            each_transposed(2, exp_m)
            for i in range(SQUARINGS):
                pe.wait_ge(squared, 1 + i)
                each(2 * (i % 2), exp_T, exp_m)
                each(1 + 2 * (i % 2), exp_m, exp_T)
            pe.wait_ge(squared, 1 + SQUARINGS)
            mm(banks[4][:, 0:P], exp_T[:, 1, :], exp_m[:, 2, :], start=True, stop=True).then_inc(setup_pe, 1)
            pe.wait_ge(rot_ok, 1)
            mm(banks[5][:, 0:P], exp_T[:, 0, :], poly[:, 0, :], start=True, stop=True).then_inc(setup_pe, 1)
            for q in range(4):
                for i in range(4):
                    e, j = 2 * q + i // 2, i % 2
                    last = nc.tensor.transpose(banks[q][:, i * P:(i + 1) * P], w2_in[:, e, j, :], ident[:, :])
                last.then_inc(setup_pe, 1)
            nc.tensor.transpose(banks[6][:, 0:P], b2_in, ident[:, :]).then_inc(setup_pe, 1)
            pe.wait_ge(w2T_ok, 1)
            pe.wait_ge(rot_ok, 2)
            for q in range(4):
                for i in range(4):
                    e, j = 2 * q + i // 2, i % 2
                    last = mm(banks[q][:, i * P:(i + 1) * P], w2_T[:, e, j, :], poly[:, 1, :], start=True, stop=True)
                last.then_inc(setup_pe, 1)
            pe.wait_ge(b2T_ok, 1)
            mm(banks[7][:, 0:P], b2_T, poly[:, 1, :], start=True, stop=True).then_inc(setup_pe, 1)
            pe.wait_ge(w_ready, 1)

            def tile(ap, t):
                return ap[:, t * P:(t + 1) * P]

            def ffn(layer):
                def at_turn(g):
                    return isinstance(g, int) and g == CH

                def transpose_z(g):
                    wait(pe, ln, g)
                    if at_turn(g):
                        wait(pe, oev, BATCH - 1)
                    elif not early(g, 0):
                        wait(pe, xnf, g - 1)
                    for t in range(NT):
                        last = nc.tensor.transpose(tile(ps_T, t), z[:, t, :], ident[:, :])
                    last.then_inc(tr.sem, 1)

                def abel_logits(g, u):
                    wait(pe, split, g)
                    if at_turn(g):
                        wait(pe, yev, BATCH - 1)
                        wait(pe, xat, BATCH - 1)
                    elif not early(g, 0):
                        wait(pe, route, g - 1, 1)
                        wait(pe, abb, g - 1)
                    for t in range(NT):
                        last = split_product(ps_al[:, t // 2, t % 2, :], tile(xn_hi[u], t), tile(xn_lo[u], t),
                                             small_hi[:, W_AB:W_AB + DA], small_lo[:, W_AB:W_AB + DA])
                    last.then_inc(alg.sem, 1)

                def transpose_w(g):
                    wait(pe, route, g)
                    if at_turn(g):
                        wait(pe, oev, BATCH - 1)
                    elif not early(g, 0):
                        wait(pe, moe0, g - 1)
                    for t in range(NT):
                        last = nc.tensor.transpose(tile(ps_w, t), w_pad[:, t, :], ident[:, :])
                    last.then_inc(wtr.sem, 1)

                def weighted_bias(g):
                    wait(pe, wtc, g)
                    for t in range(NT):
                        last = mm(tile(ps_w, t), tile(wT, t), b2_rot[:, :], start=True, stop=True)
                    last.then_inc(bim.sem, 1)

                def up_(g, u, e):
                    for j in range(NJ):
                        n = NJ * e + j
                        if not (early(g, 0) and e == 0):
                            if at_turn(g) and e == 0:
                                wait(pe, red, BATCH - 1)
                            pe.wait_ge(gel.sem, gel.value(g, n - 1))
                        last = split_product(ps_up[j][:, :], w1_hi[:, e, j * P:(j + 1) * P],
                                             w1_lo[:, e, j * P:(j + 1) * P], xn_hi[u], xn_lo[u])
                        last.then_inc(up.sem, 1)

                def down(g, e):
                    wait(pe, gel, g, NJ * (e + 1))
                    if at_turn(g) and e < 2:
                        wait(pe, ex, BATCH - 1)
                    elif not (early(g, 0) and e < 2):
                        pe.wait_ge(acc.sem, acc.value(g, NT * (e - 1)))
                    for t in range(NT):
                        for j in range(NJ):
                            last = mm(tile(ps_dn[e % 2], t), hT[e % 2][:, j, t * P:(t + 1) * P],
                                      w2_rot[:, e, j, :], start=(j == 0), stop=(j == NJ - 1))
                    last.then_inc(dn.sem, 1)

                def chunk(c, u, first, last):
                    g = CH * layer + c
                    up_(g, u, 0)
                    transpose_w(g)
                    up_(g, u, 1)
                    weighted_bias(g)
                    down(g, 0)
                    up_(g, u, 2)
                    down(g, 1)
                    up_(g, u, 3)
                    down(g, 2)
                    if not last:
                        transpose_z(g + 1)
                    up_(g, u, 4)
                    down(g, 3)
                    up_(g, u, 5)
                    down(g, 4)
                    if not last:
                        abel_logits(g + 1, 1 - u)
                    up_(g, u, 6)
                    down(g, 5)
                    up_(g, u, 7)
                    down(g, 6)
                    down(g, 7)

                g0 = CH * layer
                transpose_z(g0)
                abel_logits(g0, 0)
                over_chunks(pe, chunk)

            def attention():
                def transpose_x(b):
                    wait(pe, aln, b)
                    if early(b, 0):
                        wait(pe, route, CH - 1)
                        wait(pe, abb, CH - 1)
                    else:
                        wait(pe, mev, b - 1)
                    for t in range(NT):
                        last = nc.tensor.transpose(tile(ps_m[0], t), xh[:, t, :], ident[:, :])
                    last.then_inc(atr.sem, 1)

                def project_q(b):
                    wait(pe, asp, b)
                    split_product(ps_m[1][:, :], small_hi[:, W_Q:W_Q + D], small_lo[:, W_Q:W_Q + D],
                                  x_hi, x_lo).then_inc(qpj.sem, 1)

                def project_k(b):
                    split_product(ps_m[0][:, :], small_hi[:, W_K:W_K + D], small_lo[:, W_K:W_K + D],
                                  x_hi, x_lo).then_inc(kpj.sem, 1)

                def project_v(b):
                    wait(pe, qev, b)
                    for t in range(NT):
                        last = split_product(tile(ps_m[1], t), tile(x_hi, t), tile(x_lo, t),
                                             small_hi[:, W_V:W_V + D], small_lo[:, W_V:W_V + D])
                    last.then_inc(vpj.sem, 1)

                def masks(bank_, kind, mask, cols_):
                    if kind == "full":
                        return mm(bank_[:, cols_[0]:cols_[0] + P], ident_bf[:, :], mask[:, 0, :],
                                  start=False, stop=True)
                    if kind == "mixed":
                        return mm(bank_[:, cols_[1]:cols_[1] + 2 * P], ident_bf[:, :],
                                  mask[:, :, :].rearrange("p a n -> p (a n)"), start=False, stop=True,
                                  skip_group_check=True)
                    return mm(bank_[:, :].rearrange("p (a n) -> p a n", a=2)[:, :, cols_[2]:cols_[2] + P],
                              ident_bf[:, :], mask[:, :, :], start=False, stop=True, skip_group_check=True)

                def scores_for_max(b, u, n):
                    t, i = divmod(n, UNITS)
                    kind, q = list(units())[i]
                    bank_ = ps_a[n % 2]
                    if n == 0:
                        wait(pe, opd, b)
                    if early(b, 0) and n < 2:
                        wait(pe, gel, CH - 1)
                    else:
                        pe.wait_ge(red.sem, red.value(b, n - 1))
                    head = NG * q + t

                    def rows_keys(outp, query_tile, h, keys, start):
                        mm(outp, qT[u][:, t, query_tile * P:(query_tile + 1) * P], kZ[u][:, h, 0:keys],
                           start=start, stop=False, skip_group_check=(kind != "full"))

                    if kind == "full":
                        rows_keys(bank_[:, :], 3, head, 4 * P, True)
                    elif kind == "mixed":
                        rows_keys(bank_[:, 0:3 * P], 2, head, 3 * P, True)
                        rows_keys(bank_[:, 3 * P:4 * P], 0, head, P, False)
                    else:
                        rows_keys(bank_[:, 0:2 * P], 1, head, 2 * P, True)
                        rows_keys(bank_[:, 2 * P:4 * P], 1, head + NG, 2 * P, False)
                    masks(bank_, kind, mask_qk, (3 * P, 2 * P, P)).then_inc(sa.sem, 1)

                def transpose_max(b, last_user):
                    wait(pe, mxs, b)
                    last_user()
                    for i in range(NT):
                        last = nc.tensor.transpose(ps_m[0][0:32, i * P:(i + 1) * P],
                                                   mx2[:, i, :, :, :].rearrange("p g a t -> p (g a t)"), ident[:, :])
                    last.then_inc(mtr.sem, 1)

                def scores(b, u, n):
                    t, i = divmod(n, UNITS)
                    kind, q = list(units())[i]
                    bank_ = ps_b[n % 2]
                    if n == 0:
                        wait(pe, mdm, b)
                    if early(b, 0) and n < 2:
                        wait(pe, acc, CH - 1)
                    else:
                        pe.wait_ge(ex.sem, ex.value(b, n - 1))
                    head = NG * q + t

                    def keys_rows(outp, block_, h, start):
                        lo = block_ * P
                        mm(outp, kZ[u][:, h, lo:lo + P], qT[u][:, t, lo:SEQ], start=start, stop=False,
                           skip_group_check=(kind != "full"))

                    if kind == "full":
                        keys_rows(bank_[:, :], 0, head, True)
                    elif kind == "mixed":
                        keys_rows(bank_[:, 0:P], 3, head, True)
                        keys_rows(bank_[:, P:4 * P], 1, head, False)
                    else:
                        keys_rows(bank_[:, 0:2 * P], 2, head, True)
                        keys_rows(bank_[:, 2 * P:4 * P], 2, head + NG, False)
                    masks(bank_, kind, mask_kq, (0, 0, 0)).then_inc(sbq.sem, 1)

                def values(b, u, t, kb):
                    if kb == 0:
                        pe.wait_ge(ex.sem, ex.value(b, UNITS * (t + 1)))
                        wait(pe, vev, b)
                        if early(b, 0) and t < 2:
                            wait(pe, xnf, CH - 1)
                            wait(pe, moe0, CH - 1)
                        else:
                            pe.wait_ge(oev.sem, oev.value(b, t - 1))
                    for q in range(NQ):
                        n = SEQ - kb * P
                        last = mm(ps_o[t % 2][32 * q:32 * q + HD + 1, kb * P:SEQ],
                                  vA[u][:, kb, NG * q + t, :], pT[t % 2][:, q, PT_KB[kb]:PT_KB[kb] + n],
                                  start=(kb == 0), stop=(kb == NT - 1))
                    if kb == NT - 1:
                        last.then_inc(pv.sem, 1)

                def transpose_o(b, i, last):
                    if i == 0:
                        wait(pe, oev, b)
                        if isinstance(b, int) and b == BATCH - 1:
                            wait(pe, yev, b - 1)
                        elif last:
                            wait(pe, mev, BATCH - 1)
                        else:
                            wait(pe, kev, b + 2)
                    elif i == 1:
                        if isinstance(b, int) and b == BATCH - 1:
                            wait(pe, xat, b - 1)
                        elif last:
                            wait(pe, vev, BATCH - 1)
                        else:
                            wait(pe, vev, b + 2)
                    else:
                        wait(pe, yno, b, 2 * (i - 1))
                    for t in range(NG):
                        ins = nc.tensor.transpose(tile(ps_m[i % 2], t), oT[:, t, i * P:(i + 1) * P], ident[:, :])
                    ins.then_inc(otr.sem, 1)

                def transpose_y(b):
                    wait(pe, yno, b)
                    for t in range(NT):
                        ins = nc.tensor.transpose(tile(ps_m[0], t), yn[:, t, :], ident[:, :])
                    ins.then_inc(ytr.sem, 1)

                def project_o(b):
                    wait(pe, yev, b)
                    for t in range(NT):
                        ins = mm(tile(ps_m[1], t), yT[:, t, :], wo_sb[:, :], start=True, stop=True)
                    ins.then_inc(opj.sem, 1)

                def batch(b, u, first, last):
                    if not first:
                        for kb in range(NT):
                            values(b - 1, 1 - u, 3, kb)
                    if not last:
                        transpose_x(b + 1)
                        project_q(b + 1)
                        project_k(b + 1)
                    scores(b, u, 0)
                    scores(b, u, 1)
                    if not last:
                        project_v(b + 1)
                    scores(b, u, 2)
                    for i in range(NT):
                        if not first:
                            transpose_o(b - 1, i, last)
                        if i % 2:
                            scores(b, u, 3 + i // 2)
                    scores(b, u, 5)
                    if not first:
                        transpose_y(b - 1)
                    for n in range(6, UNITS):
                        scores(b, u, n)
                    ahead = 0
                    for t in range(1, NG):
                        for i in range(UNITS):
                            scores(b, u, UNITS * t + i)
                            if i % 3 == 0:
                                values(b, u, t - 1, i // 3)
                            if t == 1 and i == 0 and not first:
                                project_o(b - 1)
                            if not last:
                                until = N_UNITS * (UNITS * (t - 1) + i + 1) // (3 * UNITS)
                                for n in range(ahead, until):
                                    scores_for_max(b + 1, 1 - u, n)
                                ahead = until
                    if not last:
                        transpose_max(b + 1, (lambda: wait(pe, kev, b + 1)) if first
                                      else (lambda: wait(pe, yev, b - 1)))

                transpose_x(0)
                project_q(0)
                project_k(0)
                project_v(0)
                for n in range(N_UNITS):
                    scores_for_max(0, 0, n)
                transpose_max(0, lambda: wait(pe, kev, 0))
                over_chunks(pe, batch)
                for kb in range(NT):
                    values(BATCH - 1, 1, 3, kb)
                for i in range(NT):
                    transpose_o(BATCH - 1, i, True)
                transpose_y(BATCH - 1)
                project_o(BATCH - 1)

            ffn(0)
            attention()
            ffn(1)


_FFN = ["ln_gamma", "ln_beta", "abel_w", "abel_b", "moe_gate_w", "moe_gate_b", "ew1", "eb1", "ew2", "eb2",
        "gens", "gc_w", "gc_b"]


def by_group(a):
    parts = a.reshape(a.shape[:-1] + (NQ, NG, HD))
    return parts.swapaxes(-1, -2).reshape(a.shape)


def arguments(inputs):
    att = {n[len("L0_attn_"):]: np.asarray(a) for n, a in inputs.items() if n.startswith("L0_attn_")}
    named = {"x": att["x"], "q_w": by_group(att["q_w"]), "q_b": by_group(att["q_b"]),
             "k_w": by_group(att["kv_w"][:, :D]), "k_b": by_group(att["kv_b"][:D]),
             "v_w": att["kv_w"][:, D:], "v_b": att["kv_b"][D:], "o_w": att["o_w"], "o_b": att["o_b"]}
    named.update({n: np.asarray(inputs["L0_ffn_" + n]) for n in _FFN})
    named["eb1"] = named["eb1"].reshape(E, NJ, P).transpose(2, 0, 1)
    named.update(constants())
    return named


def constants():
    f = np.float32
    i = np.arange(SEQ)
    bias_q = np.zeros((P, NG, SEQ), f)
    bias_k = np.zeros((P, NQ, SEQ), f)
    for q in range(NQ):
        row = 32 * q + ROW_BIAS
        for t in range(NG):
            slope = (NG * q + t + 1) / NH
            bias_q[row, t] = slope
            bias_q[row + 1, t] = -slope * (i - i % 32)
            bias_q[row + 2, t] = -slope * (i % 32)
        bias_k[row, q] = i
        bias_k[row + 1:row + 5, q] = 1.0
    powers = np.zeros((P, 2 * SQUARINGS + 1), f)
    powers[:, :SQUARINGS] = 2.0 ** np.arange(SQUARINGS)
    powers[:, SQUARINGS:2 * SQUARINGS] = 2.0 ** -(np.arange(SQUARINGS) + 1.0) - 1.0
    powers[2 * E:, 2 * SQUARINGS] = -1.0
    return {"ident": np.eye(P, dtype=f), "bias_q": bias_q, "bias_k": bias_k, "powers": powers}


def kernel(**inputs):
    import concourse.bacc as bacc
    from concourse.bass_utils import run_bass_kernel_spmd

    nc = bacc.Bacc("TRN2", target_bir_lowering=False, num_devices=1)
    arrays, args = {}, []
    for name, a in arguments(inputs).items():
        a = np.ascontiguousarray(a)
        arrays[f"in_{name}"] = a
        args.append(nc.dram_tensor(f"in_{name}", a.shape, mybir.dt.from_np(a.dtype), kind="ExternalInput").ap())
    out = nc.dram_tensor("out", (BATCH, SEQ, D), FP32, kind="ExternalOutput").ap()
    macaron_block(nc, *args, out)
    r = run_bass_kernel_spmd(nc, [arrays], core_ids=[0])
    return r.results[0]["out"]
```

```python
from contextlib import ExitStack

import numpy as np

import concourse.bass as bass
from concourse import mybir

FP32 = mybir.dt.float32
FP32R = mybir.dt.float32r
BF16 = mybir.dt.bfloat16
U32 = mybir.dt.uint32
ALU = mybir.AluOpType
ACT = mybir.ActivationFunctionType
AX = mybir.AxisListType

P = 128
BATCH, SEQ, D = 8, 512, 128
NT = SEQ // P
CH = BATCH
NH = 16
HD = D // NH
NG = 4
NQ = NH // NG
E = 8
HID = 2 * D
NJ = HID // P
NROT = 3
EPS = 1e-5
SCALE = HD ** -0.5
MASKED = -1e30
SQUARINGS = 18
TAYLOR = 11

BLOCK = NQ * HD
ROW_MAX = 3 * BLOCK
ROW_BIAS = ROW_MAX + 2 * NQ
Q_PARTS = (0, 0, 1)
K_PARTS = (0, 1, 0)
HALF = NG // 2

UNITS = 10
N_UNITS = UNITS * NG
A_SLOTS = 34
PT_KB = (0, 640, 1024, 512)
PT_W = 1280


def units():
    for q in range(0, NQ, 2):
        yield "full", q
        yield "mixed", q
        yield "full", q + 1
        yield "mixed", q + 1
        yield "pair", q


def beside(slot):
    return range(min(N_UNITS, N_UNITS * slot // A_SLOTS), min(N_UNITS, N_UNITS * (slot + 1) // A_SLOTS))


def early(item, last):
    return isinstance(item, int) and item <= last


class Steps:

    def __init__(self, sem, per):
        self.sem, self.per = sem, per

    def value(self, item, step=None):
        return item * self.per + (self.per if step is None else step)


class Run:

    def __init__(self, engine, steps, item):
        self.engine, self.steps, self.item, self.done = engine, steps, item, 0

    def step(self, instruction):
        instruction.then_inc(self.steps.sem, 1)
        self.done += 1

    def join(self):
        self.engine.wait_ge(self.steps.sem, self.steps.value(self.item, self.done))

    def join_alone(self, passed):
        self.join()
        self.engine.sem_inc(passed, 1)

    def end(self):
        assert self.done == self.steps.per, (self.done, self.steps.per)


def macaron_block(nc, x, q_w, q_b, k_w, k_b, v_w, v_b, o_w, o_b, ln_gamma, ln_beta, abel_w, abel_b,
                  moe_gate_w, moe_gate_b, ew1, eb1, ew2, eb2, gens, gc_w, gc_b,
                  ident_c, bias_q_c, bias_k_c, consts_c, out):
    ctx = ExitStack()
    with ctx:
        def sb(name, shape, dt=FP32):
            return ctx.enter_context(nc.sbuf_tensor(name, shape, dt))

        def bank(name, shape=(P, 512), dt=FP32):
            return ctx.enter_context(nc.psum_tensor(name, list(shape), dt))

        def sem(name):
            return ctx.enter_context(nc.semaphore(name))

        x_all = sb("x_all", [P, CH * NT, D])
        ident = sb("ident", [P, P])
        ident_bf = sb("ident_bf", [P, P], BF16)
        mask_qk = sb("mask_qk", [P, 2, P], BF16)
        mask_kq = sb("mask_kq", [P, 2, P], BF16)
        expert_no = sb("expert_no", [P, NT, E])
        expert_no_i = sb("expert_no_i", [P, NT, E], mybir.dt.int32)
        consts = sb("consts", [P, 2 * SQUARINGS + 1])
        w1_hi = sb("w1_hi", [P, E, HID], FP32R)
        w1_lo = sb("w1_lo", [P, E, HID], FP32R)
        w2_rot = sb("w2_rot", [P, E, NJ, D])
        b1_sb = sb("b1_sb", [P, E, NJ])
        b2_hi = sb("b2_hi", [P, D], FP32R)
        b2_rot = sb("b2_rot", [P, D], FP32R)
        W_Q, W_K, W_V, W_AB, W_G = (i * D for i in range(5))
        small_hi = sb("small_hi", [P, 4 * D + E], FP32R)
        small_lo = sb("small_lo", [P, 4 * D + E], FP32R)
        wo_sb = sb("wo_sb", [P, D])
        cols = sb("cols", [P, 8])
        C_GAMMA, C_BETA, C_QB, C_KB, C_GCB, C_QBS, C_GCBH, C_TMP = range(8)
        rows = sb("rows", [P, 5 * D + E])
        R_AB, R_VB, R_OB, R_G1, R_G2, R_GB = (i * D for i in range(6))
        stat = sb("stat", [P, NT, 6])
        mv = sb("mv", [P, NT, 2])
        var = sb("var", [P, 2, NT])
        rstd = sb("rstd", [P, 2, NT])
        minus_half = sb("minus_half", [P, 2, NT])
        logit = sb("logit", [P, NT, E])
        top = sb("top", [P, NT, 8])
        top_i = sb("top_i", [P, NT, 8], U32)
        top_f = sb("top_f", [P, NT, 2])
        gap, th = sb("gap", [P, NT]), sb("th", [P, NT])
        w12 = sb("w12", [P, NT, 2])
        pick = sb("pick", [P, 2, NT, E])
        w_exp = [sb(f"w_exp{i}", [P, NT, E]) for i in range(2)]
        w_hi = sb("w_hi", [P, NT, E], FP32R)
        z1, z2, thg, gate = (sb(n, [P, NT]) for n in ("z1", "z2", "thg", "gate"))
        wT = sb("wT", [P, SEQ], FP32R)
        work = sb("work", [P, 3 * SEQ])
        z = work[:, 0:SEQ].rearrange("p (t d) -> p t d", t=NT)
        xn = work[:, SEQ:2 * SEQ]
        ab_in = work[:, 2 * SEQ:3 * SEQ]
        parts = sb("parts", [P, 4, SEQ], FP32R)
        xn_hi, xn_lo = [parts[:, 0, :], parts[:, 2, :]], [parts[:, 1, :], parts[:, 3, :]]
        arena = sb("arena", [P, 2 * NQ * PT_W])
        taken = [0]

        def piece(*shape):
            n = int(np.prod(shape))
            ap = arena[:, taken[0]:taken[0] + n]
            taken[0] += n
            assert taken[0] <= 2 * NQ * PT_W
            if len(shape) == 2:
                return ap.rearrange("p (a b) -> p a b", a=shape[0])
            if len(shape) == 3:
                return ap.rearrange("p (a b c) -> p a b c", a=shape[0], b=shape[1])
            return ap

        w1_in = piece(E, HID)
        w2_in = piece(E, NJ, D)
        bias_k = piece(NQ, SEQ)
        bias_q = piece(NG, SEQ)
        small_w = piece(4 * D + E)
        b2_in = piece(D)
        b2_T = piece(P)
        b2_f = piece(D)
        w2_T = w1_in.rearrange("p e (j d) -> p e j d", j=NJ)
        taken[0] = 0
        hT = [piece(NJ, SEQ) for _ in range(2)]
        y = [piece(NT, D) for _ in range(2)]
        ab = [piece(NT, D) for _ in range(2)]
        moe = [piece(NT, D) for _ in range(2)]
        skip, diff = piece(NT, D), piece(NT, D)
        w_pad = piece(NT, P)
        dot = piece(NT, D)
        taken[0] = 0
        pT = [piece(NQ, PT_W) for _ in range(2)]
        xh, qf, kf, yn = z, xn, work[:, 2 * SEQ:3 * SEQ], z
        yT = xn.rearrange("p (t d) -> p t d", t=NT)
        x_hi, x_lo, qs, ks = parts[:, 0, :], parts[:, 1, :], parts[:, 2:4, :], parts[:, 0:2, :]
        qT = [sb(f"qT{i}", [P, NG, SEQ], FP32R) for i in range(2)]
        kZ = [sb(f"kZ{i}", [P, NH, SEQ], FP32R) for i in range(2)]
        vA = [sb(f"vA{i}", [P, NT, NH, HD + 1]) for i in range(2)]
        mx = sb("mx", [P, NT, NQ, NG])
        mx_h = sb("mx_h", [P, NT, NQ, NG], FP32R)
        mx2 = sb("mx2", [P, NT, NQ, 2, NG])
        mT_zero = sb("mT_zero", [32 + 2 * NQ, SEQ], FP32R)
        mT, zeros_max = mT_zero[0:32, :], mT_zero[32:32 + 2 * NQ, :]
        v_next = sb("v_next", [P, SEQ])
        oT = sb("oT", [P, NG, SEQ])
        rden = [sb(f"rden{i}", [P, NG, NQ]) for i in range(2)]
        o_flat = oT[:, :, :].rearrange("p a b -> p (a b)")
        gen_sb, gen_T, pow2, pow3, pow3_T = (
            o_flat[:, i * NROT * P:(i + 1) * NROT * P].rearrange("p (r n) -> p r n", r=NROT) for i in range(5))
        poly, poly2, exp_m, exp_T = (
            work[:, i * NROT * P:(i + 1) * NROT * P].rearrange("p (r n) -> p r n", r=NROT) for i in range(4))
        norm, norm_all, shrink_m = (sb(n, [P, NROT]) for n in ("norm", "norm_all", "shrink_m"))
        over = sb("over", [P, NROT, SQUARINGS])
        shrink = sb("shrink", [P, NROT, SQUARINGS])

        pair = bank("pair", (P, 2, 512))
        banks = [bank(f"bank{i}") for i in range(6)] + [pair[:, 0, :], pair[:, 1, :]]
        ps_up, ps_dn = banks[0:2], banks[2:4]
        ps_T, ps_w = banks[4], banks[5]
        DA = D + E
        ps_al = pair[:, :, 0:2 * DA].rearrange("p b (t n) -> p b t n", t=2)
        ps_a, ps_b, ps_o, ps_m = banks[0:2], banks[2:4], banks[4:6], banks[6:8]

        ld_x, ld_w, ld_gen, ld_bias = sem("ld_x"), sem("ld_w"), sem("ld_gen"), sem("ld_bias")
        LOADS_W = 19
        ld_pool = sem("ld_pool")
        cst = sem("cst")
        w_pad_zero = sem("w_pad_zero")
        v_ones = sem("v_ones")
        norm_ok, norm_max = sem("norm_ok"), sem("norm_max")
        bias_in = sem("bias_in")
        set_dve = Steps(sem("set_dve"), 10**6)
        scaled, genT_ok, pow2_ok, pow3_ok = sem("scaled"), sem("genT_ok"), sem("pow2_ok"), sem("pow3_ok")
        horner, squared = sem("horner"), sem("squared")
        rot_ok, w2T_ok, b2T_ok = sem("rot_ok"), sem("w2T_ok"), sem("b2T_ok")
        setup_pe = sem("setup_pe")
        w_ready = sem("w_ready")
        gelu_table = sem("gelu_table")
        passed = sem("passed")
        stored = sem("stored")
        ln = Steps(sem("ln"), 14)
        pw = Steps(sem("pw"), 1)
        yn1 = Steps(sem("yn1"), 2)
        tr = Steps(sem("tr"), 1)
        xnf = Steps(sem("xnf"), 1)
        split = Steps(sem("split"), 2)
        alg = Steps(sem("alg"), 1)
        route = Steps(sem("route"), 22)
        thd = Steps(sem("thd"), 1)
        abb = Steps(sem("abb"), 1)
        abg = Steps(sem("abg"), 1)
        wtr = Steps(sem("wtr"), 1)
        wtc = Steps(sem("wtc"), 1)
        bim = Steps(sem("bim"), 1)
        moe0 = Steps(sem("moe0"), 1)
        up = Steps(sem("up"), E * NJ)
        gel = Steps(sem("gel"), E * NJ)
        dn = Steps(sem("dn"), E)
        acc = Steps(sem("acc"), E * NT)
        fza = Steps(sem("fza"), 2 * NT)
        fth = Steps(sem("fth"), 1)
        fzb = Steps(sem("fzb"), 2 + NT)
        fsk = Steps(sem("fsk"), 1)
        fdf = Steps(sem("fdf"), 1)
        aln = Steps(sem("aln"), 14)
        pwa = Steps(sem("pwa"), 1)
        atr = Steps(sem("atr"), 1)
        ahi = Steps(sem("ahi"), 1)
        asp = Steps(sem("asp"), 1)
        qpj, kpj, vpj = Steps(sem("qpj"), 1), Steps(sem("kpj"), 1), Steps(sem("vpj"), 1)
        qev, kev, qhi, khi = (Steps(sem(n), 1) for n in ("qev", "kev", "qhi", "khi"))
        vnx = Steps(sem("vnx"), 1)
        qks = Steps(sem("qks"), 2)
        vev = Steps(sem("vev"), 1)
        opd = [Steps(sem(f"opd{h}"), 16 * (3 + 3 * NQ + 1)) for h in range(2)]
        sa = Steps(sem("sa"), N_UNITS)
        red = Steps(sem("red"), N_UNITS)
        mxs = Steps(sem("mxs"), 3)
        mtr = Steps(sem("mtr"), 1)
        mev = Steps(sem("mev"), 1)
        mdm = Steps(sem("mdm"), 16)
        sbq = Steps(sem("sbq"), N_UNITS)
        ex = Steps(sem("ex"), N_UNITS)
        pv = Steps(sem("pv"), NG)
        oev = Steps(sem("oev"), NG)
        otr = Steps(sem("otr"), NT)
        yno = Steps(sem("yno"), 2 * NT)
        ytr = Steps(sem("ytr"), 1)
        yev = Steps(sem("yev"), 1)
        opj = Steps(sem("opj"), 1)
        xob = Steps(sem("xob"), 1)
        xat = Steps(sem("xat"), 1)

        block = ctx.enter_context(nc.Block())

        def wait(engine, steps, item, step=None):
            engine.wait_ge(steps.sem, steps.value(item, step))

        def over_chunks(engine, body):
            body(0, 0, True, False)
            with engine.Fori(0, (CH - 2) // 2) as i:
                body(2 * i + 1, 1, False, False)
                body(2 * i + 2, 0, False, False)
            body(CH - 1, 1, False, True)

        def over_batches(engine, body):
            body(0, 0, True, 2)
            with engine.Fori(0, (BATCH - 4) // 2) as i:
                body(2 * i + 1, 1, False, 2)
                body(2 * i + 2, 0, False, 2)
            for b in range(BATCH - 3, BATCH):
                body(b, b % 2, False, min(2, BATCH - 1 - b))

        def xs(b, t=None):
            if isinstance(b, int):
                return x_all[:, NT * b:NT * b + NT, :] if t is None else x_all[:, NT * b + t, :]
            if t is None:
                return x_all[:, bass.ds(NT * b, NT), :]
            return x_all[:, bass.ds(NT * b + t, 1), :].rearrange("p a d -> p (a d)")

        def over_tiles(row, width):
            return rows[:, row:row + width].unsqueeze(1).to_broadcast([P, NT, width])

        @block.sync
        def _(sp):
            sp.dma_start(gen_sb, gens.rearrange("r p n -> p r n")).then_inc(ld_gen, 16)
            sp.dma_start(consts[:, :], consts_c).then_inc(ld_gen, 16)
            sp.dma_start(ident[:, :], ident_c).then_inc(ld_gen, 16)
            for dst, src in ((small_w[:, W_AB:W_AB + D], abel_w), (small_w[:, W_Q:W_Q + D], q_w),
                             (small_w[:, W_K:W_K + D], k_w), (small_w[:, W_V:W_V + D], v_w), (small_w[:, W_G:W_G + E], moe_gate_w),
                             (wo_sb[:, :], o_w), (w1_in, ew1.rearrange("e p h -> p e h")),
                             (w2_in, ew2.rearrange("e (j p) d -> p e j d", p=P))):
                sp.dma_start(dst, src).then_inc(ld_w, 16)
            sp.dma_start(x_all[:, :, :], x.rearrange("b (t p) d -> p (b t) d", p=P)).then_inc(ld_x, 16)

            def operands(b, u, h):
                if early(b, 1):
                    sp.wait_ge(bias_in, 2 * (1 + NQ))
                    sp.wait_ge(cst, 7)
                else:
                    wait(sp, sbq, b - 2, UNITS * HALF * (h + 1))
                wait(sp, qks, b)
                groups = slice(HALF * h, HALF * (h + 1))
                sp.dma_start(qT[u][ROW_MAX:ROW_MAX + 2 * NQ, groups, :].bitcast(FP32),
                             zeros_max.bitcast(FP32).unsqueeze(1)
                             .to_broadcast([2 * NQ, HALF, SEQ])).then_inc(opd[h].sem, 16)
                rows_h = P // 2 * h
                for r in range(3):
                    sp.dma_start(qT[u][BLOCK * r:BLOCK * (r + 1), groups, :].bitcast(FP32),
                                 qs[rows_h:rows_h + P // 2, Q_PARTS[r], :].bitcast(FP32)).then_inc(opd[h].sem, 16)
                    for q in range(NQ):
                        row, src = BLOCK * r + HD * q, rows_h + HD * HALF * q
                        sp.dma_start(kZ[u][row:row + HD, NG * q + HALF * h:NG * q + HALF * (h + 1), :].bitcast(FP32),
                                     ks[src:src + HD * HALF, K_PARTS[r], :].bitcast(FP32)).then_inc(opd[h].sem, 16)

            def maxima(b, u):
                wait(sp, mev, b)
                sp.dma_start(qT[u][ROW_MAX:ROW_MAX + 2 * NQ, :, :].bitcast(FP32),
                             mT.bitcast(FP32)).then_inc(mdm.sem, 16)

            operands(0, 0, 0)
            operands(0, 0, 1)
            operands(1, 1, 0)
            maxima(0, 0)

            def batch(b, u, first, later):
                if later >= 1:
                    operands(b + 1, 1 - u, 1)
                if later == 2:
                    operands(b + 2, u, 0)
                if later >= 1:
                    maxima(b + 1, 1 - u)

            over_batches(sp, batch)

            ov = out.rearrange("b (t p) d -> p (b t) d", p=P)
            with sp.Fori(0, CH) as c:
                wait(sp, fzb, CH + c)
                sp.dma_start(ov[:, bass.ds(NT * c, NT), :], x_all[:, bass.ds(NT * c, NT), :]).then_inc(stored, 16)
            sp.wait_ge(stored, 16 * CH)

        @block.gpsimd
        def _(pool):
            nc.gpsimd.memset(b2_in, 0.0).then_inc(cst, 1)
            nc.gpsimd.memset(mask_qk[:, :, :], 0.0).then_inc(cst, 1)
            nc.gpsimd.memset(mask_kq[:, :, :], 0.0).then_inc(cst, 1)
            nc.gpsimd.iota(expert_no_i[:, :, :], pattern=[[0, NT], [1, E]], base=0,
                           channel_multiplier=0).then_inc(cst, 1)
            pool.wait_ge(cst, 4)
            nc.gpsimd.affine_select(out=mask_qk[:, :, :], in_=mask_qk[:, :, :], compare_op=ALU.is_ge,
                                    fill=MASKED, base=0, pattern=[[0, 2], [-1, P]],
                                    channel_multiplier=1).then_inc(cst, 1)
            nc.gpsimd.affine_select(out=mask_kq[:, :, :], in_=mask_kq[:, :, :], compare_op=ALU.is_ge,
                                    fill=MASKED, base=0, pattern=[[0, 2], [1, P]],
                                    channel_multiplier=-1).then_inc(cst, 1)
            for part in range(3):
                pool.dma_start(b2_in[E * part:E * (part + 1), :], eb2).then_inc(ld_pool, 16)
            pool.dma_start(b1_sb[:, :, :], eb1).then_inc(ld_pool, 16)
            pool.wait_ge(norm_ok, 1)
            nc.gpsimd.partition_all_reduce(norm_all[:, :], norm[:, :], P,
                                           bass.bass_isa.ReduceOp.max).then_inc(norm_max, 1)
            pool.wait_ge(norm_max, 1)
            nc.gpsimd.memset(zeros_max.bitcast(FP32), 0.0).then_inc(cst, 1)
            pool.wait_ge(cst, 7)
            nc.gpsimd.memset(minus_half[:, :, :], -0.5).then_inc(cst, 1)
            for u in range(2):
                nc.gpsimd.memset(vA[u][:, :, :, HD:HD + 1], 1.0).then_inc(v_ones, 1)
            pool.wait_ge(w_ready, 1)
            nc.gpsimd.memset(w_pad, 0.0).then_inc(w_pad_zero, 1)
            pool.wait_ge(cst, 8)

            def inverse_roots(steps):
                nc.gpsimd.tensor_tensor(rstd[:, :, :], var[:, :, :], minus_half[:, :, :],
                                        ALU.pow).then_inc(steps.sem, 1)

            def attention_roots(b):
                wait(pool, aln, b, 10)
                inverse_roots(pwa)

            def ffn(layer):
                def roots(g):
                    wait(pool, ln, g, 10)
                    inverse_roots(pw)

                def first_norm(g, c, u):
                    wait(pool, pw, g)
                    if not early(g, 1):
                        wait(pool, fsk, g - 2)
                    nc.gpsimd.tensor_tensor(y[u], xs(c), mv[:, :, 0:1].to_broadcast([P, NT, D]),
                                            ALU.subtract).then_inc(yn1.sem, 1)
                    wait(pool, yn1, g, 1)
                    nc.gpsimd.tensor_tensor(y[u], y[u], rstd[:, 0, :].unsqueeze(2).to_broadcast([P, NT, D]),
                                            ALU.mult).then_inc(yn1.sem, 1)

                def difference(g, u):
                    wait(pool, acc, g)
                    if not early(g, 0):
                        wait(pool, fzb, g - 1)
                    nc.gpsimd.tensor_tensor(diff, moe[u], ab[u], ALU.subtract).then_inc(fdf.sem, 1)

                def chunk(c, u, first, last):
                    g = CH * layer + c
                    if not first:
                        difference(g - 1, 1 - u)
                    if not last:
                        roots(g + 1)
                        first_norm(g + 1, c + 1, 1 - u)
                    if last and layer == 0:
                        attention_roots(0)
                    wait(pool, abg, g)
                    wait(pool, yn1, g)
                    if not early(g, 0):
                        wait(pool, fzb, g - 1, 1)
                    nc.gpsimd.tensor_tensor(skip, y[u], ab[u], ALU.add).then_inc(fsk.sem, 1)

                roots(CH * layer)
                first_norm(CH * layer, 0, 0)
                over_chunks(pool, chunk)
                difference(CH * layer + CH - 1, 1)

            ffn(0)

            def obias(b):
                wait(pool, aln, b)
                nc.gpsimd.tensor_tensor(xs(b), xs(b), over_tiles(R_OB, D),
                                        ALU.add).then_inc(xob.sem, 1)

            def v_place(b, u):
                wait(pool, vnx, b)
                if early(b, 0):
                    pool.wait_ge(v_ones, 2)
                if not early(b, 1):
                    wait(pool, pv, b - 2)
                nc.gpsimd.tensor_tensor(vA[u][:, :, :, 0:HD],
                                        v_next[:, :].rearrange("p (t h d) -> p t h d", t=NT, h=NH),
                                        rows[:, R_VB:R_VB + D].rearrange("p (h d) -> p h d", h=NH).unsqueeze(1)
                                        .to_broadcast([P, NT, NH, HD]), ALU.add).then_inc(vev.sem, 1)

            def batch(b, u, first, later):
                if later >= 1:
                    v_place(b + 1, 1 - u)
                if later == 2:
                    attention_roots(b + 2)
                    obias(b + 2)

            obias(0)
            v_place(0, 0)
            attention_roots(1)
            obias(1)
            over_batches(pool, batch)
            wait(pool, pv, BATCH - 1)
            nc.gpsimd.memset(w_pad, 0.0).then_inc(w_pad_zero, 1)
            ffn(1)

        @block.scalar
        def _(act):
            def x_high(b):
                wait(act, atr, b)
                if early(b, 0):
                    wait(act, up, CH - 2)
                else:
                    for half in opd:
                        wait(act, half, b - 1)
                nc.scalar.activation(x_hi, ps_m[0][:, :], ACT.Copy).then_inc(ahi.sem, 1)

            def q_k(b):
                wait(act, qpj, b)
                if early(b, 0):
                    wait(act, split, CH - 1)
                elif early(b, 2):
                    wait(act, qks, b - 1)
                else:
                    wait(act, opj, b - 3)
                nc.scalar.activation(qf, ps_m[1][:, :], ACT.Identity, bias=cols[:, C_QBS:C_QBS + 1],
                                     scale=SCALE).then_inc(qev.sem, 1)
                wait(act, kpj, b)
                if early(b, 0):
                    wait(act, abg, CH - 1)
                nc.scalar.activation(kf, ps_m[0][:, :], ACT.Identity,
                                     bias=cols[:, C_KB:C_KB + 1]).then_inc(kev.sem, 1)

            def v_k_high(b):
                wait(act, vpj, b)
                if not early(b, 0):
                    wait(act, vev, b - 1)
                nc.scalar.activation(v_next[:, :], ps_m[1][:, :], ACT.Copy).then_inc(vnx.sem, 1)
                wait(act, asp, b)
                wait(act, kev, b)
                nc.scalar.activation(ks[:, 0, :], kf, ACT.Copy).then_inc(khi.sem, 1)

            def q_high(b):
                if early(b, 0):
                    wait(act, up, CH - 1)
                wait(act, qev, b)
                nc.scalar.activation(qs[:, 0, :], qf, ACT.Copy).then_inc(qhi.sem, 1)

            act.dma_start(bias_k, bias_k_c).then_inc(ld_bias, 16)
            act.dma_start(bias_q, bias_q_c).then_inc(ld_bias, 16)
            for dst, vec in ((C_GAMMA, ln_gamma), (C_BETA, ln_beta), (C_QB, q_b), (C_KB, k_b)):
                act.dma_start(cols[:, dst:dst + 1], vec.rearrange("(p a) -> p a", a=1)).then_inc(ld_w, 16)
            act.dma_start(cols[:, C_GCB:C_GCB + 1], gc_b.partition_broadcast(P)).then_inc(ld_w, 16)
            for dst, vec in ((R_AB, abel_b), (R_VB, v_b), (R_OB, o_b),
                             (R_G1, gc_w[0:D, 0]), (R_G2, gc_w[D:2 * D, 0]), (R_GB, moe_gate_b)):
                n = vec.shape[0]
                act.dma_start(rows[:, dst:dst + n], vec.partition_broadcast(P)).then_inc(ld_w, 16)
            act.wait_ge(ld_bias, 32)
            for u in range(2):
                nc.scalar.activation(qT[u][:, :, :], bias_q, ACT.Copy).then_inc(bias_in, 1)
                for g in range(NQ):
                    nc.scalar.activation(kZ[u][:, NG * g:NG * g + NG, :], bias_k[:, g:g + 1, :].to_broadcast([P, NG, SEQ]),
                                         ACT.Copy).then_inc(bias_in, 1)
            act.wait_ge(w_ready, 1)
            nc.scalar.activation(cols[:, C_TMP:C_TMP + 1], cols[:, C_BETA:C_BETA + 1],
                                 ACT.Gelu).then_inc(gelu_table, 1)

            def ffn(layer):
                def xn_(g):
                    wait(act, tr, g)
                    if not early(g, 0):
                        wait(act, split, g - 1)
                    nc.scalar.activation(xn, ps_T[:, :], ACT.Identity, bias=cols[:, C_BETA:C_BETA + 1],
                                         scale=cols[:, C_GAMMA:C_GAMMA + 1]).then_inc(xnf.sem, 1)

                def tanh_gap(g):
                    wait(act, route, g, 10)
                    nc.scalar.activation(th[:, :], gap[:, :], ACT.Tanh, scale=0.5).then_inc(thd.sem, 1)

                def abel(g, u):
                    wait(act, abb, g)
                    if not early(g, 1):
                        wait(act, fzb, g - 2)
                    nc.scalar.activation(ab[u], ab_in.rearrange("p (t d) -> p t d", t=NT),
                                         ACT.Gelu).then_inc(abg.sem, 1)

                def w_rows(g):
                    wait(act, wtr, g)
                    if not early(g, 0):
                        wait(act, bim, g - 1)
                    nc.scalar.activation(wT[:, :], ps_w[:, :], ACT.Copy).then_inc(wtc.sem, 1)

                def moe_start(g, u):
                    wait(act, bim, g)
                    if not early(g, 1):
                        wait(act, fzb, g - 2)
                    nc.scalar.activation(moe[u], ps_w[:, :].rearrange("p (t d) -> p t d", t=NT),
                                         ACT.Copy).then_inc(moe0.sem, 1)

                def hidden(g, e):
                    for j in range(NJ):
                        n = 2 * e + j
                        wait(act, up, g, n + 1)
                        if not (early(g, 0) and e < 2):
                            act.wait_ge(dn.sem, dn.value(g, e - 1))
                        nc.scalar.activation(hT[e % 2][:, j, :], ps_up[j][:, :], ACT.Gelu,
                                             bias=b1_sb[:, e, j:j + 1]).then_inc(gel.sem, 1)

                def gate_tanh(g):
                    wait(act, fza, g)
                    nc.scalar.activation(thg[:, :], z2[:, :], ACT.Tanh, bias=cols[:, C_GCBH:C_GCBH + 1],
                                         scale=0.5).then_inc(fth.sem, 1)

                def chunk(c, u, first, last):
                    g = CH * layer + c
                    hidden(g, 0)
                    w_rows(g)
                    hidden(g, 1)
                    moe_start(g, u)
                    hidden(g, 2)
                    if not first:
                        gate_tanh(g - 1)
                    hidden(g, 3)
                    if not last:
                        xn_(g + 1)
                    elif layer == 0:
                        x_high(0)
                    hidden(g, 4)
                    hidden(g, 5)
                    if last and layer == 0:
                        q_k(0)
                    hidden(g, 6)
                    if last and layer == 0:
                        v_k_high(0)
                    hidden(g, 7)
                    if last and layer == 0:
                        q_high(0)
                    if not last:
                        abel(g + 1, 1 - u)
                        tanh_gap(g + 1)

                g0 = CH * layer
                xn_(g0)
                abel(g0, 0)
                tanh_gap(g0)
                over_chunks(act, chunk)
                gate_tanh(g0 + CH - 1)

            def attention():
                def exp_(b, n):
                    t, i = divmod(n, UNITS)
                    kind, q = list(units())[i]
                    wait(act, sbq, b, n + 1)
                    if i == 0 and not (early(b, 0) and t < 2):
                        act.wait_ge(pv.sem, pv.value(b, t - 1))
                    if kind == "full":
                        dst, src = pT[t % 2][:, q, 0:512], ps_b[i % 2][:, :]
                    elif kind == "mixed":
                        dst, src = pT[t % 2][:, q, 512:1024], ps_b[i % 2][:, :]
                    else:
                        dst = pT[t % 2][:, q:q + 2, 1024:PT_W]
                        src = ps_b[i % 2][:, :].rearrange("p (h n) -> p h n", h=2)
                    nc.scalar.activation(dst, src, ACT.Exp).then_inc(ex.sem, 1)

                def maxima(b):
                    wait(act, mtr, b)
                    if not early(b, 0):
                        wait(act, mdm, b - 1)
                    nc.scalar.activation(mT, ps_m[0][0:32, :], ACT.Copy).then_inc(mev.sem, 1)

                def o_evac(b, t):
                    act.wait_ge(pv.sem, pv.value(b, t + 1))
                    if not early(b, 0):
                        wait(act, otr, b - 1)
                    nc.scalar.activation(oT[:, t, :], ps_o[t % 2][:, :], ACT.Copy).then_inc(oev.sem, 1)

                def y_evac(b):
                    wait(act, ytr, b)
                    if isinstance(b, int) and b >= BATCH - 2:
                        wait(act, qks, BATCH - 1)
                    else:
                        wait(act, qks, b + 2)
                    nc.scalar.activation(yT, ps_m[0][:, :].rearrange("p (t d) -> p t d", t=NT),
                                         ACT.Copy).then_inc(yev.sem, 1)

                def batch(b, u, first, later):
                    for n in range(N_UNITS):
                        exp_(b, n)
                        if n == 4 and not first:
                            o_evac(b - 1, 3)
                        if n == 13 and not first:
                            y_evac(b - 1)
                        if later == 2:
                            if n == 17:
                                x_high(b + 2)
                            if n == 21:
                                q_k(b + 2)
                                q_high(b + 2)
                            if n == 23:
                                v_k_high(b + 2)
                        if n % UNITS == UNITS - 1 and n > UNITS:
                            o_evac(b, n // UNITS - 1)
                        if n == 37 and later >= 1:
                            maxima(b + 1)

                x_high(1)
                q_k(1)
                q_high(1)
                v_k_high(1)
                maxima(0)
                over_batches(act, batch)
                o_evac(BATCH - 1, 3)
                y_evac(BATCH - 1)

            ffn(0)
            attention()
            nc.scalar.activation(cols[:, C_TMP:C_TMP + 1], cols[:, C_BETA:C_BETA + 1],
                                 ACT.Gelu).then_inc(gelu_table, 1)
            ffn(1)

        @block.vector
        def _(dve):
            v = nc.vector
            s = Run(dve, set_dve, 0)

            def hand(semaphore):
                s.join()
                dve.sem_inc(semaphore, 1)

            dve.wait_ge(ld_gen, 48)
            v.tensor_reduce(norm[:, :], gen_sb, AX.X, ALU.add,
                            apply_absolute_value=True).then_inc(norm_ok, 1)
            s.step(v.tensor_copy(ident_bf[:, :], ident[:, :]))
            dve.wait_ge(cst, 6)
            s.step(v.tensor_copy(expert_no[:, :, :], expert_no_i[:, :, :]))
            dve.wait_ge(norm_max, 1)
            for r in range(NROT):
                s.step(v.tensor_scalar(over[:, r, :], consts[:, 0:SQUARINGS], norm_all[:, r:r + 1], None,
                                       ALU.is_lt))
            s.join()
            s.step(v.tensor_tensor(shrink[:, :, :], over[:, :, :],
                                   consts[:, SQUARINGS:2 * SQUARINGS].unsqueeze(1)
                                   .to_broadcast([P, NROT, SQUARINGS]), ALU.mult))
            s.join()
            s.step(v.tensor_scalar(shrink[:, :, :], shrink[:, :, :], 1.0, None, ALU.add))
            s.join()
            s.step(v.tensor_reduce(shrink_m[:, :], shrink[:, :, :], AX.X, ALU.min))
            s.join()
            for r in range(NROT):
                s.step(v.tensor_scalar(gen_sb[:, r, :], gen_sb[:, r, :], shrink_m[:, r:r + 1], None, ALU.mult))
            hand(scaled)

            dve.wait_ge(ld_w, LOADS_W * 16)
            dve.wait_ge(ld_pool, 4 * 16)
            s.step(v.tensor_copy(small_hi[:, :], small_w))
            s.step(v.tensor_scalar(cols[:, C_QBS:C_QBS + 1], cols[:, C_QB:C_QB + 1], SCALE, None, ALU.mult))
            s.step(v.tensor_scalar(cols[:, C_GCBH:C_GCBH + 1], cols[:, C_GCB:C_GCB + 1], 0.5, None, ALU.mult))
            s.step(v.tensor_copy(w1_hi[:, :, :], w1_in))
            s.join()
            s.step(v.tensor_tensor(small_lo[:, :], small_w, small_hi[:, :].bitcast(FP32), ALU.subtract))
            s.step(v.tensor_tensor(w1_lo[:, :, :], w1_in, w1_hi[:, :, :].bitcast(FP32), ALU.subtract))

            fact = [1.0]
            for k in range(1, TAYLOR + 1):
                fact.append(fact[-1] / k)
            identity = ident[:, :].unsqueeze(1).to_broadcast([P, NROT, P])

            def product(i):
                return banks[i][:, 0:NROT * P].rearrange("p (r n) -> p r n", r=NROT)

            dve.wait_ge(setup_pe, 1)
            s.step(v.tensor_copy(gen_T, product(0)))
            hand(genT_ok)
            dve.wait_ge(setup_pe, 2)
            s.step(v.tensor_copy(pow2, product(1)))
            hand(pow2_ok)
            dve.wait_ge(setup_pe, 4)
            s.step(v.tensor_copy(pow3_T, product(3)))
            hand(pow3_ok)

            def series(dst, k):
                s.step(v.tensor_scalar(poly, gen_sb, fact[k + 1], None, ALU.mult))
                s.join()
                s.step(v.scalar_tensor_tensor(poly, pow2, fact[k + 2], poly, ALU.mult, ALU.add))
                s.join()
                s.step(v.scalar_tensor_tensor(dst, identity, fact[k], poly, ALU.mult, ALU.add))
                s.join()

            series(exp_m, 9)
            hand(horner)
            for i, k in enumerate((6, 3, 0)):
                series(poly2, k)
                dve.wait_ge(setup_pe, 5 + i)
                s.step(v.tensor_tensor(exp_m, product(i % 2), poly2, ALU.add))
                hand(horner)
            dve.wait_ge(setup_pe, 8)
            s.step(v.tensor_copy(exp_T, product(2)))
            hand(squared)
            for i in range(SQUARINGS):
                chosen = over[:, :, i:i + 1].bitcast(U32).to_broadcast([P, NROT, P])
                dve.wait_ge(setup_pe, 10 + 2 * i)
                s.step(v.copy_predicated(exp_m, chosen, product(2 * (i % 2))))
                s.step(v.copy_predicated(exp_T, chosen, product(1 + 2 * (i % 2))))
                hand(squared)
            n = 9 + 2 * SQUARINGS
            dve.wait_ge(setup_pe, n)
            s.step(v.tensor_copy(poly[:, 0, :], banks[4][:, 0:P]))
            hand(rot_ok)
            dve.wait_ge(setup_pe, n + 1)
            s.step(v.tensor_copy(poly[:, 1, :], banks[5][:, 0:P]))
            hand(rot_ok)
            for q in range(4):
                dve.wait_ge(setup_pe, n + 2 + q)
                s.step(v.tensor_copy(w2_T[:, 2 * q:2 * q + 2, :, :],
                                     banks[q][:, :].rearrange("p (e j d) -> p e j d", e=2, j=NJ)))
            hand(w2T_ok)
            dve.wait_ge(setup_pe, n + 6)
            s.step(v.tensor_copy(b2_T, banks[6][:, 0:P]))
            hand(b2T_ok)
            for q in range(4):
                dve.wait_ge(setup_pe, n + 7 + q)
                s.step(v.tensor_copy(w2_rot[:, 2 * q:2 * q + 2, :, :],
                                     banks[q][:, :].rearrange("p (e j d) -> p e j d", e=2, j=NJ)))
            dve.wait_ge(setup_pe, n + 11)
            s.step(v.tensor_copy(b2_f, banks[7][:, 0:D]))
            s.join()
            s.step(v.tensor_copy(b2_hi[:, :], b2_f))
            s.join()
            s.step(v.scalar_tensor_tensor(b2_rot[:, :], b2_hi[:, :].bitcast(FP32),
                                          consts[:, 2 * SQUARINGS:2 * SQUARINGS + 1], b2_f, ALU.mult, ALU.add))
            dve.wait_ge(bias_in, 2 * (1 + NQ))
            s.join()
            dve.sem_inc(w_ready, 1)

            def statistics(run, src):
                for t in range(NT):
                    run.step(v.bn_stats(stat[:, t, :], src(t)))
                run.join_alone(passed)
                for t in range(NT):
                    run.step(v.bn_aggr(mv[:, t, :], stat[:, t, :]))
                run.join()
                run.step(v.tensor_scalar(var[:, 0, :], mv[:, :, 1], EPS, None, ALU.add))
                run.step(v.tensor_scalar(var[:, 1, :], mv[:, :, 1], 1.0 + EPS, EPS * EPS, ALU.mult, ALU.add))

            def normalise_tiles(run, src, rs, dst):
                for t in range(NT):
                    run.step(v.tensor_scalar(dst(t), src(t), mv[:, t, 0:1], rs[:, t:t + 1],
                                             ALU.subtract, ALU.mult))

            def attention_stats(b):
                if early(b, 0):
                    wait(dve, yn1, CH - 1)
                statistics(Run(dve, aln, b), lambda t: xs(b, t))

            def attention_norm(b):
                run = Run(dve, aln, b)
                run.done = 10
                if early(b, 0):
                    wait(dve, tr, CH - 1)
                elif early(b, 2):
                    wait(dve, atr, b - 1)
                else:
                    wait(dve, ytr, b - 3)
                wait(dve, pwa, b)
                normalise_tiles(run, lambda t: xs(b, t), rstd[:, 0, :], lambda t: xh[:, t, :])
                run.end()

            def x_low(b):
                wait(dve, ahi, b)
                v.tensor_tensor(x_lo, ps_m[0][:, :], x_hi.bitcast(FP32), ALU.subtract).then_inc(asp.sem, 1)

            def q_k_low(b):
                wait(dve, qhi, b)
                v.tensor_tensor(qs[:, 1, :], qf, qs[:, 0, :].bitcast(FP32), ALU.subtract).then_inc(qks.sem, 1)
                wait(dve, khi, b)
                v.tensor_tensor(ks[:, 1, :], kf, ks[:, 0, :].bitcast(FP32), ALU.subtract).then_inc(qks.sem, 1)

            def ffn(layer):
                def stats_(g, c):
                    if not early(g, 0):
                        wait(dve, yn1, g - 1)
                    run = Run(dve, ln, g)
                    statistics(run, lambda t: xs(c, t))

                def norms(g, c):
                    run = Run(dve, ln, g)
                    run.done = 10
                    wait(dve, pw, g)
                    if isinstance(g, int) and g == CH:
                        wait(dve, atr, BATCH - 1)
                    elif not early(g, 0):
                        wait(dve, tr, g - 1)
                    normalise_tiles(run, lambda t: xs(c, t), rstd[:, 1, :], lambda t: z[:, t, :])
                    run.end()

                def split_(g, u):
                    run = Run(dve, split, g)
                    wait(dve, xnf, g)
                    if isinstance(g, int) and g == CH:
                        wait(dve, vpj, BATCH - 1)
                    elif not early(g, 1):
                        wait(dve, up, g - 2)
                    run.step(v.tensor_copy(xn_hi[u], xn))
                    run.join()
                    run.step(v.tensor_tensor(xn_lo[u], xn, xn_hi[u].bitcast(FP32), ALU.subtract))
                    run.end()

                def top_two(g):
                    run = Run(dve, route, g)
                    wait(dve, alg, g)
                    run.step(v.tensor_tensor(logit[:, :, :].rearrange("p (b t) e -> p b t e", b=2),
                                             ps_al[:, :, :, D:DA],
                                             rows[:, R_GB:R_GB + E].unsqueeze(1).unsqueeze(1)
                                             .to_broadcast([P, 2, 2, E]), ALU.add))
                    run.join_alone(passed)
                    for t in range(NT):
                        run.step(v.max(top[:, t, :], logit[:, t, :]))
                    run.join_alone(passed)
                    for t in range(NT):
                        run.step(v.max_index(top_i[:, t, :], top[:, t, :], logit[:, t, :]))
                    run.step(v.tensor_tensor(gap[:, :], top[:, :, 0], top[:, :, 1], ALU.subtract))

                def expert_weights(g, u):
                    run = Run(dve, route, g)
                    run.done = 10
                    run.join()
                    run.step(v.tensor_copy(top_f[:, :, :], top_i[:, :, 0:2]))
                    run.join()
                    for k in range(2):
                        run.step(v.tensor_tensor(pick[:, k, :, :], expert_no[:, :, :],
                                                 top_f[:, :, k:k + 1].to_broadcast([P, NT, E]), ALU.is_equal))
                    wait(dve, thd, g)
                    run.step(v.tensor_scalar(w12[:, :, 0], th[:, :], 0.5, 0.5, ALU.mult, ALU.add))
                    run.step(v.tensor_scalar(w12[:, :, 1], th[:, :], -0.5, 0.5, ALU.mult, ALU.add))
                    run.join()
                    for k in range(2):
                        run.step(v.tensor_tensor(pick[:, k, :, :], pick[:, k, :, :],
                                                 w12[:, :, k:k + 1].to_broadcast([P, NT, E]), ALU.mult))
                    run.join()
                    run.step(v.tensor_tensor(w_exp[u][:, :, :], pick[:, 0, :, :], pick[:, 1, :, :], ALU.add))
                    run.join()
                    run.step(v.tensor_copy(w_hi[:, :, :], w_exp[u][:, :, :]))
                    run.join()
                    if early(g, 0) or (isinstance(g, int) and g == CH):
                        dve.wait_ge(w_pad_zero, 1 + layer)
                    else:
                        wait(dve, wtr, g - 1)
                    run.step(v.tensor_copy(w_pad[:, :, 0:E], w_hi[:, :, :].bitcast(FP32)))
                    run.step(v.tensor_tensor(w_pad[:, :, E:2 * E], w_exp[u][:, :, :],
                                             w_hi[:, :, :].bitcast(FP32), ALU.subtract))
                    run.step(v.tensor_copy(w_pad[:, :, 2 * E:3 * E], w_hi[:, :, :].bitcast(FP32)))
                    run.end()

                def abel_bias(g):
                    wait(dve, alg, g)
                    if not early(g, 0):
                        wait(dve, abg, g - 1)
                    v.tensor_tensor(ab_in.rearrange("p (b t d) -> p b t d", b=2, t=2), ps_al[:, :, :, 0:D],
                                    rows[:, R_AB:R_AB + D].unsqueeze(1).unsqueeze(1)
                                    .to_broadcast([P, 2, 2, D]), ALU.add).then_inc(abb.sem, 1)

                def accumulate(g, u, e):
                    wait(dve, dn, g, e + 1)
                    if e == 0:
                        wait(dve, moe0, g)
                    else:
                        wait(dve, acc, g, NT * e)
                    for t in range(NT):
                        v.scalar_tensor_tensor(moe[u][:, t, :], ps_dn[e % 2][:, t * D:(t + 1) * D],
                                               w_exp[u][:, t, e:e + 1], moe[u][:, t, :],
                                               ALU.mult, ALU.add).then_inc(acc.sem, 1)

                def gate_dots(g, src, row, ins, outs, step):
                    run = Run(dve, fza, g)
                    run.done = step
                    if step:
                        wait(dve, acc, g)
                        run.join()
                    else:
                        wait(dve, abg, g)
                        if not early(g, 0):
                            wait(dve, fza, g - 1)
                    for t in range(NT):
                        run.step(v.tensor_tensor_reduce(out=dot[:, t, :], in0=src[:, t, :], in1=rows[:, row:row + D],
                                                        scale=1.0, scalar=ins(t), op0=ALU.mult, op1=ALU.add,
                                                        accum_out=outs[:, t:t + 1]))

                def abel_dots(g, u):
                    gate_dots(g, ab[u], R_G1, lambda t: 0.0, z1, 0)

                def moe_dots(g, u):
                    gate_dots(g, moe[u], R_G2, lambda t: z1[:, t:t + 1], z2, NT)

                def finish_skip(g, c):
                    run = Run(dve, fzb, g)
                    wait(dve, fsk, g)
                    run.step(v.scalar_tensor_tensor(xs(c), skip, 0.5, xs(c), ALU.mult, ALU.add))

                def finish_gate(g, c):
                    run = Run(dve, fzb, g)
                    run.done = 1
                    wait(dve, fth, g)
                    run.step(v.tensor_scalar(gate[:, :], thg[:, :], 0.25, 0.25, ALU.mult, ALU.add))
                    wait(dve, fdf, g)
                    run.join()
                    for t in range(NT):
                        run.step(v.scalar_tensor_tensor(xs(c, t), diff[:, t, :], gate[:, t:t + 1], xs(c, t),
                                                        ALU.mult, ALU.add))
                    run.end()

                def chunk(c, u, first, last):
                    g = CH * layer + c
                    if not last:
                        stats_(g + 1, c + 1)
                    elif layer == 0:
                        attention_stats(0)
                    accumulate(g, u, 0)
                    if not last:
                        norms(g + 1, c + 1)
                    elif layer == 0:
                        attention_norm(0)
                    accumulate(g, u, 1)
                    if not first:
                        finish_skip(g - 1, c - 1)
                    accumulate(g, u, 2)
                    if not first:
                        finish_gate(g - 1, c - 1)
                    accumulate(g, u, 3)
                    if not last:
                        split_(g + 1, 1 - u)
                    elif layer == 0:
                        x_low(0)
                    accumulate(g, u, 4)
                    abel_dots(g, u)
                    accumulate(g, u, 5)
                    if not last:
                        abel_bias(g + 1)
                        top_two(g + 1)
                    accumulate(g, u, 6)
                    if not last:
                        expert_weights(g + 1, 1 - u)
                    accumulate(g, u, 7)
                    moe_dots(g, u)

                g0 = CH * layer
                stats_(g0, 0)
                norms(g0, 0)
                split_(g0, 0)
                abel_bias(g0)
                top_two(g0)
                expert_weights(g0, 0)
                over_chunks(dve, chunk)
                if layer == 0:
                    q_k_low(0)
                finish_skip(g0 + CH - 1, CH - 1)
                finish_gate(g0 + CH - 1, CH - 1)

            def attention():
                def reduce_(b, n):
                    t, i = divmod(n, UNITS)
                    kind, q = list(units())[i]
                    wait(dve, sa, b, n + 1)
                    if n == 0 and not early(b, 0):
                        wait(dve, mxs, b - 1)
                    src = ps_a[n % 2]
                    if kind == "full":
                        v.tensor_reduce(mx[:, 3, q, t:t + 1], src[:, :], AX.X, ALU.max).then_inc(red.sem, 1)
                    elif kind == "mixed":
                        v.tensor_reduce(mx[:, 2, q, t:t + 1], src[:, 0:384], AX.X, ALU.max)
                        v.tensor_reduce(mx[:, 0, q, t:t + 1], src[:, 384:512], AX.X, ALU.max).then_inc(red.sem, 1)
                    else:
                        v.tensor_reduce(mx[:, 1, q:q + 2, t], src[:, :].rearrange("p (h n) -> p h n", h=2),
                                        AX.X, ALU.max).then_inc(red.sem, 1)

                def maxima(b):
                    run = Run(dve, mxs, b)
                    wait(dve, red, b)
                    run.step(v.tensor_scalar(mx_h[:, :, :, :], mx[:, :, :, :], -1.0, None, ALU.mult))
                    run.join()
                    if not early(b, 0):
                        wait(dve, mtr, b - 1)
                    mh = mx_h[:, :, :, :].bitcast(FP32)
                    run.step(v.tensor_copy(mx2[:, :, :, 0, :], mh))
                    run.step(v.scalar_tensor_tensor(mx2[:, :, :, 1, :], mx[:, :, :, :], -1.0, mh,
                                                    ALU.mult, ALU.subtract))
                    run.end()

                def normalise(b, i):
                    run = Run(dve, yno, b)
                    run.done = 2 * i
                    wait(dve, otr, b, i + 1)
                    src = ps_m[i % 2][:, :].rearrange("p (t q c) -> p t q c", t=NG, q=NQ)
                    if i == 0 and not early(b, 0):
                        wait(dve, ytr, b - 1)
                    run.step(v.reciprocal(rden[i % 2][:, :, :], src[:, :, :, HD]))
                    run.join()
                    run.step(v.tensor_tensor(yn[:, i, :].rearrange("p (q t c) -> p t q c", t=NG, q=NQ),
                                             src[:, :, :, 0:HD],
                                             rden[i % 2][:, :, :].unsqueeze(3).to_broadcast([P, NG, NQ, HD]), ALU.mult))

                def add_out(b):
                    wait(dve, opj, b)
                    wait(dve, xob, b)
                    v.tensor_tensor(xs(b), ps_m[1][:, :].rearrange("p (t d) -> p t d", t=NT), xs(b),
                                    ALU.add).then_inc(xat.sem, 1)

                def batch(b, u, first, later):
                    for n in range(N_UNITS):
                        if not first:
                            if n in (7, 8):
                                normalise(b - 1, n - 7)
                            if n in (10, 11):
                                normalise(b - 1, n - 8)
                            if n == 15:
                                add_out(b - 1)
                        if later == 2:
                            if n == 9:
                                attention_stats(b + 2)
                            if n == 13:
                                attention_norm(b + 2)
                            if n == 18:
                                x_low(b + 2)
                            if n == 24:
                                q_k_low(b + 2)
                        if later >= 1:
                            for a in beside(n):
                                reduce_(b + 1, a)
                    if later >= 1:
                        maxima(b + 1)

                attention_stats(1)
                attention_norm(1)
                for n in range(N_UNITS):
                    if n == 22:
                        x_low(1)
                    if n == 30:
                        q_k_low(1)
                    reduce_(0, n)
                maxima(0)
                over_batches(dve, batch)
                for i in range(NT):
                    normalise(BATCH - 1, i)
                add_out(BATCH - 1)

            dve.wait_ge(ld_x, 16)
            ffn(0)
            wait(dve, fzb, CH - 1)
            attention()
            wait(dve, xat, BATCH - 1)
            ffn(1)

        @block.tensor
        def _(pe):
            mm = nc.tensor.matmul

            def split_product(outp, a_hi, a_lo, b_hi, b_lo):
                mm(outp, a_hi, b_hi, start=True, stop=False)
                mm(outp, a_hi, b_lo, start=False, stop=False)
                return mm(outp, a_lo, b_hi, start=False, stop=True)

            def each(bank_, lhsT, rhs):
                for r in range(NROT):
                    last = mm(banks[bank_][:, r * P:(r + 1) * P], lhsT[:, r, :], rhs[:, r, :], start=True, stop=True)
                last.then_inc(setup_pe, 1)

            def each_transposed(bank_, src):
                for r in range(NROT):
                    last = nc.tensor.transpose(banks[bank_][:, r * P:(r + 1) * P], src[:, r, :], ident[:, :])
                last.then_inc(setup_pe, 1)

            pe.wait_ge(scaled, 1)
            each_transposed(0, gen_sb)
            pe.wait_ge(genT_ok, 1)
            each(1, gen_T, gen_sb)
            pe.wait_ge(pow2_ok, 1)
            each(2, gen_T, pow2)
            each(3, pow2, gen_T)
            pe.wait_ge(pow3_ok, 1)
            for i in range(3):
                pe.wait_ge(horner, 1 + i)
                each(i % 2, pow3_T, exp_m)
            pe.wait_ge(horner, 4)
            each_transposed(2, exp_m)
            for i in range(SQUARINGS):
                pe.wait_ge(squared, 1 + i)
                each(2 * (i % 2), exp_T, exp_m)
                each(1 + 2 * (i % 2), exp_m, exp_T)
            pe.wait_ge(squared, 1 + SQUARINGS)
            mm(banks[4][:, 0:P], exp_T[:, 1, :], exp_m[:, 2, :], start=True, stop=True).then_inc(setup_pe, 1)
            pe.wait_ge(rot_ok, 1)
            mm(banks[5][:, 0:P], exp_T[:, 0, :], poly[:, 0, :], start=True, stop=True).then_inc(setup_pe, 1)
            for q in range(4):
                for i in range(4):
                    e, j = 2 * q + i // 2, i % 2
                    last = nc.tensor.transpose(banks[q][:, i * P:(i + 1) * P], w2_in[:, e, j, :], ident[:, :])
                last.then_inc(setup_pe, 1)
            nc.tensor.transpose(banks[6][:, 0:P], b2_in, ident[:, :]).then_inc(setup_pe, 1)
            pe.wait_ge(w2T_ok, 1)
            pe.wait_ge(rot_ok, 2)
            for q in range(4):
                for i in range(4):
                    e, j = 2 * q + i // 2, i % 2
                    last = mm(banks[q][:, i * P:(i + 1) * P], w2_T[:, e, j, :], poly[:, 1, :], start=True, stop=True)
                last.then_inc(setup_pe, 1)
            pe.wait_ge(b2T_ok, 1)
            mm(banks[7][:, 0:P], b2_T, poly[:, 1, :], start=True, stop=True).then_inc(setup_pe, 1)
            pe.wait_ge(w_ready, 1)

            def tile(ap, t):
                return ap[:, t * P:(t + 1) * P]

            def transpose_x(b):
                wait(pe, aln, b)
                if early(b, 0):
                    wait(pe, route, CH - 1)
                    wait(pe, abb, CH - 1)
                elif early(b, 1):
                    wait(pe, khi, b - 1)
                elif early(b, 2):
                    wait(pe, mev, b - 2)
                else:
                    wait(pe, yev, b - 3)
                for t in range(NT):
                    last = nc.tensor.transpose(tile(ps_m[0], t), xh[:, t, :], ident[:, :])
                last.then_inc(atr.sem, 1)

            def project_q_k(b):
                wait(pe, asp, b)
                if not early(b, 2):
                    wait(pe, xat, b - 3)
                elif not early(b, 0):
                    wait(pe, vnx, b - 1)
                split_product(ps_m[1][:, :], small_hi[:, W_Q:W_Q + D], small_lo[:, W_Q:W_Q + D],
                              x_hi, x_lo).then_inc(qpj.sem, 1)
                split_product(ps_m[0][:, :], small_hi[:, W_K:W_K + D], small_lo[:, W_K:W_K + D],
                              x_hi, x_lo).then_inc(kpj.sem, 1)

            def project_v(b):
                wait(pe, qev, b)
                for t in range(NT):
                    last = split_product(tile(ps_m[1], t), tile(x_hi, t), tile(x_lo, t),
                                         small_hi[:, W_V:W_V + D], small_lo[:, W_V:W_V + D])
                last.then_inc(vpj.sem, 1)

            def ffn(layer):
                def at_turn(g):
                    return isinstance(g, int) and g == CH

                def transpose_z(g):
                    wait(pe, ln, g)
                    if at_turn(g):
                        wait(pe, oev, BATCH - 1)
                    elif not early(g, 0):
                        wait(pe, xnf, g - 1)
                    for t in range(NT):
                        last = nc.tensor.transpose(tile(ps_T, t), z[:, t, :], ident[:, :])
                    last.then_inc(tr.sem, 1)

                def abel_logits(g, u):
                    wait(pe, split, g)
                    if at_turn(g):
                        wait(pe, yev, BATCH - 1)
                        wait(pe, xat, BATCH - 1)
                    elif not early(g, 0):
                        wait(pe, route, g - 1, 1)
                        wait(pe, abb, g - 1)
                    for t in range(NT):
                        last = split_product(ps_al[:, t // 2, t % 2, :], tile(xn_hi[u], t), tile(xn_lo[u], t),
                                             small_hi[:, W_AB:W_AB + DA], small_lo[:, W_AB:W_AB + DA])
                    last.then_inc(alg.sem, 1)

                def transpose_w(g):
                    wait(pe, route, g)
                    if at_turn(g):
                        wait(pe, oev, BATCH - 1)
                    elif not early(g, 0):
                        wait(pe, moe0, g - 1)
                    for t in range(NT):
                        last = nc.tensor.transpose(tile(ps_w, t), w_pad[:, t, :], ident[:, :])
                    last.then_inc(wtr.sem, 1)

                def weighted_bias(g):
                    wait(pe, wtc, g)
                    for t in range(NT):
                        last = mm(tile(ps_w, t), tile(wT, t), b2_rot[:, :], start=True, stop=True)
                    last.then_inc(bim.sem, 1)

                def up_(g, u, e):
                    for j in range(NJ):
                        n = NJ * e + j
                        if not (early(g, 0) and e == 0):
                            if at_turn(g) and e == 0:
                                wait(pe, red, BATCH - 1)
                            pe.wait_ge(gel.sem, gel.value(g, n - 1))
                        last = split_product(ps_up[j][:, :], w1_hi[:, e, j * P:(j + 1) * P],
                                             w1_lo[:, e, j * P:(j + 1) * P], xn_hi[u], xn_lo[u])
                        last.then_inc(up.sem, 1)

                def down(g, e):
                    wait(pe, gel, g, NJ * (e + 1))
                    if at_turn(g) and e < 2:
                        wait(pe, ex, BATCH - 1)
                    elif not (early(g, 0) and e < 2):
                        pe.wait_ge(acc.sem, acc.value(g, NT * (e - 1)))
                    for t in range(NT):
                        for j in range(NJ):
                            last = mm(tile(ps_dn[e % 2], t), hT[e % 2][:, j, t * P:(t + 1) * P],
                                      w2_rot[:, e, j, :], start=(j == 0), stop=(j == NJ - 1))
                    last.then_inc(dn.sem, 1)

                def chunk(c, u, first, last):
                    g = CH * layer + c
                    up_(g, u, 0)
                    transpose_w(g)
                    up_(g, u, 1)
                    weighted_bias(g)
                    down(g, 0)
                    up_(g, u, 2)
                    down(g, 1)
                    up_(g, u, 3)
                    down(g, 2)
                    if not last:
                        transpose_z(g + 1)
                    elif layer == 0:
                        transpose_x(0)
                    up_(g, u, 4)
                    down(g, 3)
                    up_(g, u, 5)
                    down(g, 4)
                    if not last:
                        abel_logits(g + 1, 1 - u)
                    elif layer == 0:
                        project_q_k(0)
                    up_(g, u, 6)
                    down(g, 5)
                    if last and layer == 0:
                        project_v(0)
                    up_(g, u, 7)
                    down(g, 6)
                    down(g, 7)

                g0 = CH * layer
                transpose_z(g0)
                abel_logits(g0, 0)
                over_chunks(pe, chunk)

            def attention():
                def masks(bank_, kind, mask, cols_):
                    if kind == "full":
                        return mm(bank_[:, cols_[0]:cols_[0] + P], ident_bf[:, :], mask[:, 0, :],
                                  start=False, stop=True)
                    if kind == "mixed":
                        return mm(bank_[:, cols_[1]:cols_[1] + 2 * P], ident_bf[:, :],
                                  mask[:, :, :].rearrange("p a n -> p (a n)"), start=False, stop=True,
                                  skip_group_check=True)
                    return mm(bank_[:, :].rearrange("p (a n) -> p a n", a=2)[:, :, cols_[2]:cols_[2] + P],
                              ident_bf[:, :], mask[:, :, :], start=False, stop=True, skip_group_check=True)

                def scores_for_max(b, u, n):
                    t, i = divmod(n, UNITS)
                    kind, q = list(units())[i]
                    bank_ = ps_a[n % 2]
                    if n % (N_UNITS // 2) == 0:
                        wait(pe, opd[n // (N_UNITS // 2)], b)
                    if early(b, 0) and n < 2:
                        wait(pe, gel, CH - 1)
                    else:
                        pe.wait_ge(red.sem, red.value(b, n - 1))
                    head = NG * q + t

                    def rows_keys(outp, query_tile, h, keys, start):
                        mm(outp, qT[u][:, t, query_tile * P:(query_tile + 1) * P], kZ[u][:, h, 0:keys],
                           start=start, stop=False, skip_group_check=(kind != "full"))

                    if kind == "full":
                        rows_keys(bank_[:, :], 3, head, 4 * P, True)
                    elif kind == "mixed":
                        rows_keys(bank_[:, 0:3 * P], 2, head, 3 * P, True)
                        rows_keys(bank_[:, 3 * P:4 * P], 0, head, P, False)
                    else:
                        rows_keys(bank_[:, 0:2 * P], 1, head, 2 * P, True)
                        rows_keys(bank_[:, 2 * P:4 * P], 1, head + NG, 2 * P, False)
                    masks(bank_, kind, mask_qk, (3 * P, 2 * P, P)).then_inc(sa.sem, 1)

                def transpose_max(b):
                    wait(pe, mxs, b)
                    if isinstance(b, int) and b == BATCH - 1:
                        wait(pe, yev, b - 2)
                    else:
                        wait(pe, kev, b + 1)
                    for i in range(NT):
                        last = nc.tensor.transpose(ps_m[0][0:32, i * P:(i + 1) * P],
                                                   mx2[:, i, :, :, :].rearrange("p g a t -> p (g a t)"), ident[:, :])
                    last.then_inc(mtr.sem, 1)

                def scores(b, u, n):
                    t, i = divmod(n, UNITS)
                    kind, q = list(units())[i]
                    bank_ = ps_b[n % 2]
                    if n == 0:
                        wait(pe, mdm, b)
                    if early(b, 0) and n < 2:
                        wait(pe, acc, CH - 1)
                    else:
                        pe.wait_ge(ex.sem, ex.value(b, n - 1))
                    head = NG * q + t

                    def keys_rows(outp, block_, h, start):
                        lo = block_ * P
                        mm(outp, kZ[u][:, h, lo:lo + P], qT[u][:, t, lo:SEQ], start=start, stop=False,
                           skip_group_check=(kind != "full"))

                    if kind == "full":
                        keys_rows(bank_[:, :], 0, head, True)
                    elif kind == "mixed":
                        keys_rows(bank_[:, 0:P], 3, head, True)
                        keys_rows(bank_[:, P:4 * P], 1, head, False)
                    else:
                        keys_rows(bank_[:, 0:2 * P], 2, head, True)
                        keys_rows(bank_[:, 2 * P:4 * P], 2, head + NG, False)
                    masks(bank_, kind, mask_kq, (0, 0, 0)).then_inc(sbq.sem, 1)

                def values(b, u, t, kb):
                    if kb == 0:
                        pe.wait_ge(ex.sem, ex.value(b, UNITS * (t + 1)))
                        wait(pe, vev, b)
                        if early(b, 0) and t < 2:
                            wait(pe, xnf, CH - 1)
                            wait(pe, moe0, CH - 1)
                        else:
                            pe.wait_ge(oev.sem, oev.value(b, t - 1))
                    for q in range(NQ):
                        n = SEQ - kb * P
                        last = mm(ps_o[t % 2][32 * q:32 * q + HD + 1, kb * P:SEQ],
                                  vA[u][:, kb, NG * q + t, :], pT[t % 2][:, q, PT_KB[kb]:PT_KB[kb] + n],
                                  start=(kb == 0), stop=(kb == NT - 1))
                    if kb == NT - 1:
                        last.then_inc(pv.sem, 1)

                def transpose_o(b, i):
                    if i == 0:
                        wait(pe, oev, b)
                        if isinstance(b, int) and b == BATCH - 1:
                            wait(pe, yev, b - 1)
                        else:
                            wait(pe, mev, b + 1)
                    elif i == 1:
                        if isinstance(b, int) and b >= BATCH - 2:
                            wait(pe, xat, b - 1)
                        else:
                            wait(pe, vnx, b + 2)
                    else:
                        wait(pe, yno, b, 2 * (i - 1))
                    for t in range(NG):
                        ins = nc.tensor.transpose(tile(ps_m[i % 2], t), oT[:, t, i * P:(i + 1) * P], ident[:, :])
                    ins.then_inc(otr.sem, 1)

                def transpose_y(b):
                    wait(pe, yno, b)
                    for t in range(NT):
                        ins = nc.tensor.transpose(tile(ps_m[0], t), yn[:, t, :], ident[:, :])
                    ins.then_inc(ytr.sem, 1)

                def project_o(b):
                    wait(pe, yev, b)
                    for t in range(NT):
                        ins = mm(tile(ps_m[1], t), yT[:, t, :], wo_sb[:, :], start=True, stop=True)
                    ins.then_inc(opj.sem, 1)

                def batch(b, u, first, later):
                    for n in range(N_UNITS):
                        t, i = divmod(n, UNITS)
                        scores(b, u, n)
                        if not first:
                            if n < NT:
                                values(b - 1, 1 - u, NG - 1, n)
                            if n in (6, 7):
                                transpose_o(b - 1, n - 6)
                            if n in (9, 10):
                                transpose_o(b - 1, n - 7)
                            if n == 12:
                                transpose_y(b - 1)
                            if n == 14:
                                project_o(b - 1)
                        if t and i % 3 == 0:
                            values(b, u, t - 1, i // 3)
                        if later == 2:
                            if n == 16:
                                transpose_x(b + 2)
                            if n == 20:
                                project_q_k(b + 2)
                            if n == 22:
                                project_v(b + 2)
                        if later >= 1:
                            for a in beside(n):
                                scores_for_max(b + 1, 1 - u, a)
                            if n == 36:
                                transpose_max(b + 1)

                for n in range(N_UNITS):
                    if n == 20:
                        transpose_x(1)
                    if n == 24:
                        project_q_k(1)
                    if n == 27:
                        project_v(1)
                    scores_for_max(0, 0, n)
                transpose_max(0)
                over_batches(pe, batch)
                for kb in range(NT):
                    values(BATCH - 1, 1, 3, kb)
                for i in range(NT):
                    transpose_o(BATCH - 1, i)
                transpose_y(BATCH - 1)
                project_o(BATCH - 1)

            ffn(0)
            attention()
            ffn(1)


_FFN = ["ln_gamma", "ln_beta", "abel_w", "abel_b", "moe_gate_w", "moe_gate_b", "ew1", "eb1", "ew2", "eb2",
        "gens", "gc_w", "gc_b"]


def by_group(a):
    parts = a.reshape(a.shape[:-1] + (NQ, NG // HALF, HALF, HD))
    order = tuple(range(a.ndim - 1)) + tuple(a.ndim - 1 + i for i in (1, 0, 3, 2))
    return parts.transpose(order).reshape(a.shape)


def arguments(inputs):
    att = {n[len("L0_attn_"):]: np.asarray(a) for n, a in inputs.items() if n.startswith("L0_attn_")}
    named = {"x": att["x"], "q_w": by_group(att["q_w"]), "q_b": by_group(att["q_b"]),
             "k_w": by_group(att["kv_w"][:, :D]), "k_b": by_group(att["kv_b"][:D]),
             "v_w": att["kv_w"][:, D:], "v_b": att["kv_b"][D:], "o_w": att["o_w"], "o_b": att["o_b"]}
    named.update({n: np.asarray(inputs["L0_ffn_" + n]) for n in _FFN})
    named["eb1"] = named["eb1"].reshape(E, NJ, P).transpose(2, 0, 1)
    named.update(constants())
    return named


def constants():
    f = np.float32
    i = np.arange(SEQ)
    bias_q = np.zeros((P, NG, SEQ), f)
    bias_k = np.zeros((P, NQ, SEQ), f)
    for q in range(NQ):
        row = ROW_BIAS + 3 * q
        for t in range(NG):
            slope = (NG * q + t + 1) / NH
            bias_q[row, t] = slope
            bias_q[row + 1, t] = -slope * (i - i % 32)
            bias_q[row + 2, t] = -slope * (i % 32)
        bias_k[row, q] = i
        bias_k[row + 1:row + 3, q] = 1.0
        bias_k[ROW_MAX + 2 * q:ROW_MAX + 2 * (q + 1), q] = 1.0
    powers = np.zeros((P, 2 * SQUARINGS + 1), f)
    powers[:, :SQUARINGS] = 2.0 ** np.arange(SQUARINGS)
    powers[:, SQUARINGS:2 * SQUARINGS] = 2.0 ** -(np.arange(SQUARINGS) + 1.0) - 1.0
    powers[2 * E:, 2 * SQUARINGS] = -1.0
    return {"ident": np.eye(P, dtype=f), "bias_q": bias_q, "bias_k": bias_k, "powers": powers}


def kernel(**inputs):
    import concourse.bacc as bacc
    from concourse.bass_utils import run_bass_kernel_spmd

    nc = bacc.Bacc("TRN2", target_bir_lowering=False, num_devices=1)
    arrays, args = {}, []
    for name, a in arguments(inputs).items():
        a = np.ascontiguousarray(a)
        arrays[f"in_{name}"] = a
        args.append(nc.dram_tensor(f"in_{name}", a.shape, mybir.dt.from_np(a.dtype), kind="ExternalInput").ap())
    out = nc.dram_tensor("out", (BATCH, SEQ, D), FP32, kind="ExternalOutput").ap()
    macaron_block(nc, *args, out)
    r = run_bass_kernel_spmd(nc, [arrays], core_ids=[0])
    return r.results[0]["out"]
```

```python
from contextlib import ExitStack

import numpy as np

import concourse.bass as bass
from concourse import mybir

FP32 = mybir.dt.float32
FP32R = mybir.dt.float32r
BF16 = mybir.dt.bfloat16
U32 = mybir.dt.uint32
ALU = mybir.AluOpType
ACT = mybir.ActivationFunctionType
AX = mybir.AxisListType

P = 128
BATCH, SEQ, D = 8, 512, 128
NT = SEQ // P
CH = BATCH
NH = 16
HD = D // NH
NG = 4
NQ = NH // NG
E = 8
HID = 2 * D
NJ = HID // P
NROT = 3
EPS = 1e-5
SCALE = HD ** -0.5
MASKED = -1e30
SQUARINGS = 18
TAYLOR = 11

BLOCK = NQ * HD
ROW_MAX = 3 * BLOCK
ROW_BIAS = ROW_MAX + 2 * NQ
Q_PARTS = (0, 0, 1)
K_PARTS = (0, 1, 0)
HALF = NG // 2

AT_STATS = 3
AT_OUT, AT_NORMALISE = (5, 7, 9, 11), (6, 8, 10, 12)
AT_Y_T, AT_Y, AT_OUT_PROJECT, AT_NORM, AT_ADD = 13, 14, 15, 14, 17
AT_X_T, AT_X_HIGH, AT_X_LOW = 16, 17, 18
AT_QK_PROJECT, AT_QK, AT_V_PROJECT, AT_V, AT_LOW = 20, 21, 22, 23, 24
AT_VALUES = (2, 4, 5, 7)
AT_MAX_T, AT_MAX = 36, 37

UNITS = 10
N_UNITS = UNITS * NG
A_SLOTS, A_FIRST = 34, 3
PT_KB = (0, 640, 1024, 512)
PT_W = 1280


def units():
    for q in range(0, NQ, 2):
        yield "full", q
        yield "mixed", q
        yield "full", q + 1
        yield "mixed", q + 1
        yield "pair", q


def beside(slot):
    def until(n):
        return min(N_UNITS, A_FIRST + (N_UNITS - A_FIRST) * n // A_SLOTS)
    return range(until(slot) if slot else 0, until(slot + 1))


def early(item, last):
    return isinstance(item, int) and item <= last


class Steps:

    def __init__(self, sem, per):
        self.sem, self.per = sem, per

    def value(self, item, step=None):
        return item * self.per + (self.per if step is None else step)


class Run:

    def __init__(self, engine, steps, item):
        self.engine, self.steps, self.item, self.done = engine, steps, item, 0

    def step(self, instruction):
        instruction.then_inc(self.steps.sem, 1)
        self.done += 1

    def join(self):
        self.engine.wait_ge(self.steps.sem, self.steps.value(self.item, self.done))

    def join_alone(self, passed):
        self.join()
        self.engine.sem_inc(passed, 1)

    def end(self):
        assert self.done == self.steps.per, (self.done, self.steps.per)


def macaron_block(nc, x, q_w, q_b, k_w, k_b, v_w, v_b, o_w, o_b, ln_gamma, ln_beta, abel_w, abel_b,
                  moe_gate_w, moe_gate_b, ew1, eb1, ew2, eb2, gens, gc_w, gc_b,
                  ident_c, bias_q_c, bias_k_c, consts_c, out):
    ctx = ExitStack()
    with ctx:
        def sb(name, shape, dt=FP32):
            return ctx.enter_context(nc.sbuf_tensor(name, shape, dt))

        def bank(name, shape=(P, 512), dt=FP32):
            return ctx.enter_context(nc.psum_tensor(name, list(shape), dt))

        def sem(name):
            return ctx.enter_context(nc.semaphore(name))

        x_all = sb("x_all", [P, CH * NT, D])
        ident = sb("ident", [P, P])
        ident_bf = sb("ident_bf", [P, P], BF16)
        mask_qk = sb("mask_qk", [P, 2, P], BF16)
        mask_kq = sb("mask_kq", [P, 2, P], BF16)
        expert_no = sb("expert_no", [P, NT, E])
        expert_no_i = sb("expert_no_i", [P, NT, E], mybir.dt.int32)
        consts = sb("consts", [P, 2 * SQUARINGS + 1])
        w1_hi = sb("w1_hi", [P, E, HID], FP32R)
        w1_lo = sb("w1_lo", [P, E, HID], FP32R)
        w2_rot = sb("w2_rot", [P, E, NJ, D])
        b1_sb = sb("b1_sb", [P, E, NJ])
        b2_hi = sb("b2_hi", [P, D], FP32R)
        b2_rot = sb("b2_rot", [P, D], FP32R)
        W_Q, W_K, W_V, W_AB, W_G = (i * D for i in range(5))
        small_hi = sb("small_hi", [P, 4 * D + E], FP32R)
        small_lo = sb("small_lo", [P, 4 * D + E], FP32R)
        wo_sb = sb("wo_sb", [P, D])
        cols = sb("cols", [P, 8])
        C_GAMMA, C_BETA, C_QB, C_KB, C_GCB, C_QBS, C_GCBH, C_TMP = range(8)
        rows = sb("rows", [P, 5 * D + E])
        R_AB, R_VB, R_OB, R_G1, R_G2, R_GB = (i * D for i in range(6))
        stat = sb("stat", [P, NT, 6])
        mv = sb("mv", [P, NT, 2])
        var = sb("var", [P, 2, NT])
        rstd = sb("rstd", [P, 2, NT])
        minus_half = sb("minus_half", [P, 2, NT])
        logit = sb("logit", [P, NT, E])
        top = sb("top", [P, NT, 8])
        top_i = sb("top_i", [P, NT, 8], U32)
        top_f = sb("top_f", [P, NT, 2])
        gap, th = sb("gap", [P, NT]), sb("th", [P, NT])
        w12 = sb("w12", [P, NT, 2])
        pick = sb("pick", [P, 2, NT, E])
        w_exp = [sb(f"w_exp{i}", [P, NT, E]) for i in range(2)]
        w_hi = sb("w_hi", [P, NT, E], FP32R)
        z1, z2, thg, gate = (sb(n, [P, NT]) for n in ("z1", "z2", "thg", "gate"))
        wT = sb("wT", [P, SEQ], FP32R)
        work = sb("work", [P, 3 * SEQ])
        z = work[:, 0:SEQ].rearrange("p (t d) -> p t d", t=NT)
        xn = work[:, SEQ:2 * SEQ]
        ab_in = work[:, 2 * SEQ:3 * SEQ]
        parts = sb("parts", [P, 4, SEQ], FP32R)
        xn_hi, xn_lo = [parts[:, 0, :], parts[:, 2, :]], [parts[:, 1, :], parts[:, 3, :]]
        arena = sb("arena", [P, 2 * NQ * PT_W])
        taken = [0]

        def piece(*shape):
            n = int(np.prod(shape))
            ap = arena[:, taken[0]:taken[0] + n]
            taken[0] += n
            assert taken[0] <= 2 * NQ * PT_W
            if len(shape) == 2:
                return ap.rearrange("p (a b) -> p a b", a=shape[0])
            if len(shape) == 3:
                return ap.rearrange("p (a b c) -> p a b c", a=shape[0], b=shape[1])
            return ap

        w1_in = piece(E, HID)
        w2_in = piece(E, NJ, D)
        bias_k = piece(NQ, SEQ)
        bias_q = piece(NG, SEQ)
        small_w = piece(4 * D + E)
        b2_in = piece(D)
        b2_T = piece(P)
        b2_f = piece(D)
        mats = piece(NROT, 2, P)
        exp_m, exp_T = mats[:, :, 0, :], mats[:, :, 1, :]
        w2_T = bias_k.rearrange("p q (a d) -> p (q a) d", d=D).rearrange("p (e j) d -> p e j d", j=NJ)
        taken[0] = 0
        hT = [piece(NJ, SEQ) for _ in range(2)]
        y = [piece(NT, D) for _ in range(2)]
        ab = [piece(NT, D) for _ in range(2)]
        moe = [piece(NT, D) for _ in range(2)]
        skip, diff = piece(NT, D), piece(NT, D)
        w_pad = piece(NT, P)
        dot = piece(NT, D)
        taken[0] = 0
        pT = [piece(NQ, PT_W) for _ in range(2)]
        xh, qf, kf, yn = z, xn, work[:, 2 * SEQ:3 * SEQ], z
        yT = xn.rearrange("p (t d) -> p t d", t=NT)
        x_hi, x_lo, qs, ks = parts[:, 0, :], parts[:, 1, :], parts[:, 2:4, :], parts[:, 0:2, :]
        qT = [sb(f"qT{i}", [P, NG, SEQ], FP32R) for i in range(2)]
        kZ = [sb(f"kZ{i}", [P, NH, SEQ], FP32R) for i in range(2)]
        vA = [sb(f"vA{i}", [P, NT, NH, HD + 1]) for i in range(2)]
        mx = sb("mx", [P, NT, NQ, NG])
        mx_h = sb("mx_h", [P, NT, NQ, NG], FP32R)
        mx2 = sb("mx2", [P, NT, NQ, 2, NG])
        mT_zero = sb("mT_zero", [32 + 2 * NQ, SEQ], FP32R)
        mT, zeros_max = mT_zero[0:32, :], mT_zero[32:32 + 2 * NQ, :]
        v_next = sb("v_next", [P, SEQ])
        oT = sb("oT", [P, NG, SEQ])
        qs_first, ks_first = oT[:, 0:2, :].bitcast(FP32R), oT[:, 2:4, :].bitcast(FP32R)
        rden = [sb(f"rden{i}", [P, NG, NQ]) for i in range(2)]
        o_flat = oT[:, :, :].rearrange("p a b -> p (a b)")
        gen_sb, gen_T, pow2, rot, pow3_T = (
            o_flat[:, i * NROT * P:(i + 1) * NROT * P].rearrange("p (r n) -> p r n", r=NROT) for i in range(5))
        poly, poly2 = (
            work[:, i * NROT * P:(i + 1) * NROT * P].rearrange("p (r n) -> p r n", r=NROT) for i in range(2))
        norm, norm_all, shrink_m = (sb(n, [P, NROT]) for n in ("norm", "norm_all", "shrink_m"))
        over = sb("over", [P, NROT, SQUARINGS])
        shrink = sb("shrink", [P, NROT, SQUARINGS])

        pair = bank("pair", (P, 2, 512))
        banks = [bank(f"bank{i}") for i in range(6)] + [pair[:, 0, :], pair[:, 1, :]]
        ps_up, ps_dn = banks[0:2], banks[2:4]
        ps_T, ps_w = banks[4], banks[5]
        DA = D + E
        ps_al = pair[:, :, 0:2 * DA].rearrange("p b (t n) -> p b t n", t=2)
        ps_a, ps_b, ps_o, ps_m = [banks[0], banks[1], banks[4]], banks[2:4], banks[5], banks[6:8]
        NA = len(ps_a)
        ps_b_last = ps_b + ps_a[:2]

        def score_bank(b, n):
            ring = ps_b_last if isinstance(b, int) and b == BATCH - 1 else ps_b
            return ring[n % len(ring)], len(ring)


        ld_x, ld_w, ld_gen, ld_bias = sem("ld_x"), sem("ld_w"), sem("ld_gen"), sem("ld_bias")
        LOADS_W = 19
        ld_pool = sem("ld_pool")
        cst = sem("cst")
        w_pad_zero = sem("w_pad_zero")
        v_ones = sem("v_ones")
        norm_ok, norm_max = sem("norm_ok"), sem("norm_max")
        bias_in = sem("bias_in")
        set_dve = Steps(sem("set_dve"), 10**6)
        scaled, genT_ok, pow2_ok, pow3_ok = sem("scaled"), sem("genT_ok"), sem("pow2_ok"), sem("pow3_ok")
        horner, squared = sem("horner"), sem("squared")
        rot_ok, w2T_ok = sem("rot_ok"), sem("w2T_ok")
        hi_ok, lo_ok = sem("hi_ok"), sem("lo_ok")
        series_pe = sem("series_pe")
        w2T_pe = sem("w2T_pe")
        square_pe = sem("square_pe")
        rot_pe = sem("rot_pe")
        w_ready = sem("w_ready")
        gelu_table = sem("gelu_table")
        passed = sem("passed")
        stored = sem("stored")
        stats_and_z = Steps(sem("stats_and_z"), 14)
        roots_ok = Steps(sem("roots_ok"), 1)
        y_ok = Steps(sem("y_ok"), 2)
        z_transposed = Steps(sem("z_transposed"), 1)
        xn_ok = Steps(sem("xn_ok"), 1)
        xn_split = Steps(sem("xn_split"), 2)
        abel_logits_ok = Steps(sem("abel_logits_ok"), 1)
        routed = Steps(sem("routed"), 22)
        gap_tanh = Steps(sem("gap_tanh"), 1)
        abel_biased = Steps(sem("abel_biased"), 1)
        abel_out = Steps(sem("abel_out"), 1)
        w_transposed = Steps(sem("w_transposed"), 1)
        w_rows_ok = Steps(sem("w_rows_ok"), 1)
        bias_mixed = Steps(sem("bias_mixed"), 1)
        moe_started = Steps(sem("moe_started"), 1)
        up_ok = Steps(sem("up_ok"), E * NJ)
        hidden_ok = Steps(sem("hidden_ok"), E * NJ)
        down_ok = Steps(sem("down_ok"), E)
        expert_added = Steps(sem("expert_added"), E * NT)
        gate_dots_ok = Steps(sem("gate_dots_ok"), 2 * NT)
        gate_tanh_ok = Steps(sem("gate_tanh_ok"), 1)
        x_final = Steps(sem("x_final"), 2 + NT)
        skip_ok = Steps(sem("skip_ok"), 1)
        diff_ok = Steps(sem("diff_ok"), 1)
        xh_ok = Steps(sem("xh_ok"), 14)
        att_roots_ok = Steps(sem("att_roots_ok"), 1)
        x_transposed = Steps(sem("x_transposed"), 1)
        x_high_ok = Steps(sem("x_high_ok"), 1)
        x_low_ok = Steps(sem("x_low_ok"), 1)
        q_projected, k_projected, v_projected = Steps(sem("q_projected"), 1), Steps(sem("k_projected"), 1), Steps(sem("v_projected"), 1)
        q_out, k_out, q_high_ok, k_high_ok = (Steps(sem(n), 1) for n in ("q_out", "k_out", "q_high_ok", "k_high_ok"))
        v_next_ok = Steps(sem("v_next_ok"), 1)
        qk_split = Steps(sem("qk_split"), 2)
        v_placed = Steps(sem("v_placed"), 1)
        operands_in = [Steps(sem(f"operands_in{h}"), 16 * (3 + 3 * NQ + 1)) for h in range(2)]
        a_scores = Steps(sem("a_scores"), N_UNITS)
        reduced = Steps(sem("reduced"), N_UNITS)
        max_split = Steps(sem("max_split"), 3)
        max_transposed = Steps(sem("max_transposed"), 1)
        max_rows = Steps(sem("max_rows"), 1)
        max_in = Steps(sem("max_in"), 16)
        b_scores = Steps(sem("b_scores"), N_UNITS)
        exp_ok = Steps(sem("exp_ok"), N_UNITS)
        values_ok = Steps(sem("values_ok"), NG)
        o_out = Steps(sem("o_out"), NG)
        o_transposed = Steps(sem("o_transposed"), NT)
        y_normalised = Steps(sem("y_normalised"), 2 * NT)
        y_transposed = Steps(sem("y_transposed"), 1)
        y_out = Steps(sem("y_out"), 1)
        o_projected = Steps(sem("o_projected"), 1)
        o_bias_added = Steps(sem("o_bias_added"), 1)
        x_attended = Steps(sem("x_attended"), 1)

        block = ctx.enter_context(nc.Block())

        def wait(engine, steps, item, step=None):
            engine.wait_ge(steps.sem, steps.value(item, step))

        def over_chunks(engine, body):
            body(0, 0, True, False)
            with engine.Fori(0, (CH - 2) // 2) as i:
                body(2 * i + 1, 1, False, False)
                body(2 * i + 2, 0, False, False)
            body(CH - 1, 1, False, True)

        def over_batches(engine, body):
            body(0, 0, True, 2)
            with engine.Fori(0, (BATCH - 4) // 2) as i:
                body(2 * i + 1, 1, False, 2)
                body(2 * i + 2, 0, False, 2)
            for b in range(BATCH - 3, BATCH):
                body(b, b % 2, False, min(2, BATCH - 1 - b))

        def xs(b, t=None):
            if isinstance(b, int):
                return x_all[:, NT * b:NT * b + NT, :] if t is None else x_all[:, NT * b + t, :]
            if t is None:
                return x_all[:, bass.ds(NT * b, NT), :]
            return x_all[:, bass.ds(NT * b + t, 1), :].rearrange("p a d -> p (a d)")

        def over_tiles(row, width):
            return rows[:, row:row + width].unsqueeze(1).to_broadcast([P, NT, width])

        @block.sync
        def _(sp):
            sp.dma_start(gen_sb, gens.rearrange("r p n -> p r n")).then_inc(ld_gen, 16)
            sp.dma_start(consts[:, :], consts_c).then_inc(ld_gen, 16)
            sp.dma_start(ident[:, :], ident_c).then_inc(ld_gen, 16)
            for dst, src in ((small_w[:, W_AB:W_AB + D], abel_w), (small_w[:, W_Q:W_Q + D], q_w),
                             (small_w[:, W_K:W_K + D], k_w), (small_w[:, W_V:W_V + D], v_w), (small_w[:, W_G:W_G + E], moe_gate_w),
                             (wo_sb[:, :], o_w), (w1_in, ew1.rearrange("e p h -> p e h")),
                             (w2_in, ew2.rearrange("e (j p) d -> p e j d", p=P))):
                sp.dma_start(dst, src).then_inc(ld_w, 16)
            sp.dma_start(x_all[:, :, :], x.rearrange("b (t p) d -> p (b t) d", p=P)).then_inc(ld_x, 16)

            def operands(b, u, h):
                if early(b, 1):
                    sp.wait_ge(bias_in, 2 * (1 + NQ))
                    sp.wait_ge(cst, 7)
                else:
                    wait(sp, b_scores, b - 2, UNITS * HALF * (h + 1))
                wait(sp, qk_split, b)
                groups = slice(HALF * h, HALF * (h + 1))
                sp.dma_start(qT[u][ROW_MAX:ROW_MAX + 2 * NQ, groups, :].bitcast(FP32),
                             zeros_max.bitcast(FP32).unsqueeze(1)
                             .to_broadcast([2 * NQ, HALF, SEQ])).then_inc(operands_in[h].sem, 16)
                q_src, k_src = (qs_first, ks_first) if early(b, 0) else (qs, ks)
                rows_h = P // 2 * h
                for r in range(3):
                    sp.dma_start(qT[u][BLOCK * r:BLOCK * (r + 1), groups, :].bitcast(FP32),
                                 q_src[rows_h:rows_h + P // 2, Q_PARTS[r], :].bitcast(FP32)).then_inc(operands_in[h].sem, 16)
                    for q in range(NQ):
                        row, src = BLOCK * r + HD * q, rows_h + HD * HALF * q
                        sp.dma_start(kZ[u][row:row + HD, NG * q + HALF * h:NG * q + HALF * (h + 1), :].bitcast(FP32),
                                     k_src[src:src + HD * HALF, K_PARTS[r], :].bitcast(FP32)).then_inc(operands_in[h].sem, 16)

            def maxima(b, u):
                wait(sp, max_rows, b)
                sp.dma_start(qT[u][ROW_MAX:ROW_MAX + 2 * NQ, :, :].bitcast(FP32),
                             mT.bitcast(FP32)).then_inc(max_in.sem, 16)

            operands(0, 0, 0)
            operands(0, 0, 1)
            operands(1, 1, 0)
            maxima(0, 0)

            def batch(b, u, first, later):
                if later >= 1:
                    operands(b + 1, 1 - u, 1)
                if later == 2:
                    operands(b + 2, u, 0)
                if later >= 1:
                    maxima(b + 1, 1 - u)

            over_batches(sp, batch)

            ov = out.rearrange("b (t p) d -> p (b t) d", p=P)
            with sp.Fori(0, CH) as c:
                wait(sp, x_final, CH + c)
                sp.dma_start(ov[:, bass.ds(NT * c, NT), :], x_all[:, bass.ds(NT * c, NT), :]).then_inc(stored, 16)
            sp.wait_ge(stored, 16 * CH)

        @block.gpsimd
        def _(pool):
            nc.gpsimd.memset(b2_in, 0.0).then_inc(cst, 1)
            nc.gpsimd.memset(mask_qk[:, :, :], 0.0).then_inc(cst, 1)
            nc.gpsimd.memset(mask_kq[:, :, :], 0.0).then_inc(cst, 1)
            nc.gpsimd.iota(expert_no_i[:, :, :], pattern=[[0, NT], [1, E]], base=0,
                           channel_multiplier=0).then_inc(cst, 1)
            pool.wait_ge(cst, 4)
            nc.gpsimd.affine_select(out=mask_qk[:, :, :], in_=mask_qk[:, :, :], compare_op=ALU.is_ge,
                                    fill=MASKED, base=0, pattern=[[0, 2], [-1, P]],
                                    channel_multiplier=1).then_inc(cst, 1)
            nc.gpsimd.affine_select(out=mask_kq[:, :, :], in_=mask_kq[:, :, :], compare_op=ALU.is_ge,
                                    fill=MASKED, base=0, pattern=[[0, 2], [1, P]],
                                    channel_multiplier=-1).then_inc(cst, 1)
            for part in range(3):
                pool.dma_start(b2_in[E * part:E * (part + 1), :], eb2).then_inc(ld_pool, 16)
            pool.dma_start(b1_sb[:, :, :], eb1).then_inc(ld_pool, 16)
            pool.wait_ge(norm_ok, 1)
            nc.gpsimd.partition_all_reduce(norm_all[:, :], norm[:, :], P,
                                           bass.bass_isa.ReduceOp.max).then_inc(norm_max, 1)
            pool.wait_ge(norm_max, 1)
            nc.gpsimd.memset(zeros_max.bitcast(FP32), 0.0).then_inc(cst, 1)
            pool.wait_ge(cst, 7)
            nc.gpsimd.memset(minus_half[:, :, :], -0.5).then_inc(cst, 1)
            for u in range(2):
                nc.gpsimd.memset(vA[u][:, :, :, HD:HD + 1], 1.0).then_inc(v_ones, 1)
            for i, (lo, whole, hi) in enumerate(((small_lo[:, :], small_w, small_hi[:, :]),
                                                 (w1_lo[:, :, :], w1_in, w1_hi[:, :, :]))):
                pool.wait_ge(hi_ok, i + 1)
                nc.gpsimd.tensor_tensor(lo, whole, hi.bitcast(FP32), ALU.subtract).then_inc(lo_ok, 1)
            pool.wait_ge(bias_in, 2 * (1 + NQ))
            nc.gpsimd.memset(w_pad, 0.0).then_inc(w_pad_zero, 1)
            pool.wait_ge(cst, 8)

            def inverse_roots(steps):
                nc.gpsimd.tensor_tensor(rstd[:, :, :], var[:, :, :], minus_half[:, :, :],
                                        ALU.pow).then_inc(steps.sem, 1)

            def attention_roots(b):
                wait(pool, xh_ok, b, 10)
                inverse_roots(att_roots_ok)

            def roots(g):
                wait(pool, stats_and_z, g, 10)
                inverse_roots(roots_ok)

            def ffn(layer):
                def first_norm(g, c, u):
                    wait(pool, roots_ok, g)
                    if not early(g, 1):
                        wait(pool, skip_ok, g - 2)
                    nc.gpsimd.tensor_tensor(y[u], xs(c), mv[:, :, 0:1].to_broadcast([P, NT, D]),
                                            ALU.subtract).then_inc(y_ok.sem, 1)
                    wait(pool, y_ok, g, 1)
                    nc.gpsimd.tensor_tensor(y[u], y[u], rstd[:, 0, :].unsqueeze(2).to_broadcast([P, NT, D]),
                                            ALU.mult).then_inc(y_ok.sem, 1)

                def difference(g, u):
                    wait(pool, expert_added, g)
                    if not early(g, 0):
                        wait(pool, x_final, g - 1)
                    nc.gpsimd.tensor_tensor(diff, moe[u], ab[u], ALU.subtract).then_inc(diff_ok.sem, 1)

                def chunk(c, u, first, last):
                    g = CH * layer + c
                    if not first:
                        difference(g - 1, 1 - u)
                    if not last:
                        roots(g + 1)
                        first_norm(g + 1, c + 1, 1 - u)
                    if last and layer == 0:
                        attention_roots(0)
                    wait(pool, abel_out, g)
                    wait(pool, y_ok, g)
                    if not early(g, 0):
                        wait(pool, x_final, g - 1, 1)
                    nc.gpsimd.tensor_tensor(skip, y[u], ab[u], ALU.add).then_inc(skip_ok.sem, 1)

                if layer == 0:
                    roots(0)
                    pool.wait_ge(w2T_pe, 5)
                first_norm(CH * layer, 0, 0)
                if layer == 0:
                    pool.wait_ge(w_ready, 1)
                over_chunks(pool, chunk)
                difference(CH * layer + CH - 1, 1)

            ffn(0)

            def obias(b):
                wait(pool, xh_ok, b)
                nc.gpsimd.tensor_tensor(xs(b), xs(b), over_tiles(R_OB, D),
                                        ALU.add).then_inc(o_bias_added.sem, 1)

            def v_place(b, u):
                wait(pool, v_next_ok, b)
                if early(b, 0):
                    pool.wait_ge(v_ones, 2)
                if not early(b, 1):
                    wait(pool, values_ok, b - 2)
                nc.gpsimd.tensor_tensor(vA[u][:, :, :, 0:HD],
                                        v_next[:, :].rearrange("p (t h d) -> p t h d", t=NT, h=NH),
                                        rows[:, R_VB:R_VB + D].rearrange("p (h d) -> p h d", h=NH).unsqueeze(1)
                                        .to_broadcast([P, NT, NH, HD]), ALU.add).then_inc(v_placed.sem, 1)

            def batch(b, u, first, later):
                if later >= 1:
                    v_place(b + 1, 1 - u)
                if later == 2:
                    attention_roots(b + 2)
                    obias(b + 2)

            obias(0)
            v_place(0, 0)
            attention_roots(1)
            obias(1)
            over_batches(pool, batch)
            roots(CH)
            wait(pool, values_ok, BATCH - 1)
            nc.gpsimd.memset(w_pad, 0.0).then_inc(w_pad_zero, 1)
            ffn(1)

        @block.scalar
        def _(act):
            def x_high(b):
                wait(act, x_transposed, b)
                if early(b, 0):
                    wait(act, up_ok, CH - 2)
                elif early(b, 1):
                    wait(act, v_projected, b - 1)
                else:
                    for half in operands_in:
                        wait(act, half, b - 1)
                nc.scalar.activation(x_hi, ps_m[0][:, :], ACT.Copy).then_inc(x_high_ok.sem, 1)

            def q_k(b):
                wait(act, q_projected, b)
                if early(b, 0):
                    wait(act, xn_split, CH - 1)
                elif early(b, 2):
                    wait(act, qk_split, b - 1)
                else:
                    wait(act, o_projected, b - 3)
                nc.scalar.activation(qf, ps_m[1][:, :], ACT.Identity, bias=cols[:, C_QBS:C_QBS + 1],
                                     scale=SCALE).then_inc(q_out.sem, 1)
                wait(act, k_projected, b)
                if early(b, 0):
                    wait(act, abel_out, CH - 1)
                nc.scalar.activation(kf, ps_m[0][:, :], ACT.Identity,
                                     bias=cols[:, C_KB:C_KB + 1]).then_inc(k_out.sem, 1)

            def v_k_high(b):
                wait(act, v_projected, b)
                if not early(b, 0):
                    wait(act, v_placed, b - 1)
                nc.scalar.activation(v_next[:, :], ps_m[1][:, :], ACT.Copy).then_inc(v_next_ok.sem, 1)
                wait(act, x_low_ok, b)
                wait(act, k_out, b)
                dst = ks_first if early(b, 0) else ks
                nc.scalar.activation(dst[:, 0, :], kf, ACT.Copy).then_inc(k_high_ok.sem, 1)

            def q_high(b):
                if early(b, 1) and not early(b, 0):
                    wait(act, up_ok, CH - 1)
                wait(act, q_out, b)
                dst = qs_first if early(b, 0) else qs
                nc.scalar.activation(dst[:, 0, :], qf, ACT.Copy).then_inc(q_high_ok.sem, 1)

            act.dma_start(bias_k, bias_k_c).then_inc(ld_bias, 16)
            act.dma_start(bias_q, bias_q_c).then_inc(ld_bias, 16)
            for dst, vec in ((C_GAMMA, ln_gamma), (C_BETA, ln_beta), (C_QB, q_b), (C_KB, k_b)):
                act.dma_start(cols[:, dst:dst + 1], vec.rearrange("(p a) -> p a", a=1)).then_inc(ld_w, 16)
            act.dma_start(cols[:, C_GCB:C_GCB + 1], gc_b.partition_broadcast(P)).then_inc(ld_w, 16)
            for dst, vec in ((R_AB, abel_b), (R_VB, v_b), (R_OB, o_b),
                             (R_G1, gc_w[0:D, 0]), (R_G2, gc_w[D:2 * D, 0]), (R_GB, moe_gate_b)):
                n = vec.shape[0]
                act.dma_start(rows[:, dst:dst + n], vec.partition_broadcast(P)).then_inc(ld_w, 16)
            act.wait_ge(ld_bias, 32)
            for u in range(2):
                nc.scalar.activation(qT[u][:, :, :], bias_q, ACT.Copy).then_inc(bias_in, 1)
                for g in range(NQ):
                    nc.scalar.activation(kZ[u][:, NG * g:NG * g + NG, :], bias_k[:, g:g + 1, :].to_broadcast([P, NG, SEQ]),
                                         ACT.Copy).then_inc(bias_in, 1)
            act.wait_ge(ld_w, LOADS_W * 16)
            nc.scalar.activation(small_hi[:, :], small_w, ACT.Copy).then_inc(hi_ok, 1)
            nc.scalar.activation(w1_hi[:, :, :], w1_in, ACT.Copy).then_inc(hi_ok, 1)
            act.wait_ge(bias_in, 2 * (1 + NQ))
            for q in range(4):
                act.wait_ge(w2T_pe, q + 1)
                nc.scalar.activation(w2_T[:, 2 * q:2 * q + 2, :, :],
                                     banks[4 + q][:, :].rearrange("p (e j d) -> p e j d", e=2, j=NJ),
                                     ACT.Copy).then_inc(w2T_ok, 1)
            act.wait_ge(w2T_pe, 5)
            nc.scalar.activation(b2_T, banks[3][:, 0:P], ACT.Copy).then_inc(w2T_ok, 1)
            nc.scalar.activation(cols[:, C_TMP:C_TMP + 1], cols[:, C_BETA:C_BETA + 1],
                                 ACT.Gelu).then_inc(gelu_table, 1)

            def xn_(g):
                wait(act, z_transposed, g)
                if early(g, 0):
                    act.wait_ge(horner, 4)
                if isinstance(g, int) and g == CH:
                    wait(act, o_projected, BATCH - 2)
                if not early(g, 0):
                    wait(act, xn_split, g - 1)
                nc.scalar.activation(xn, ps_T[:, :], ACT.Identity, bias=cols[:, C_BETA:C_BETA + 1],
                                     scale=cols[:, C_GAMMA:C_GAMMA + 1]).then_inc(xn_ok.sem, 1)

            def ffn(layer):
                def tanh_gap(g):
                    wait(act, routed, g, 10)
                    nc.scalar.activation(th[:, :], gap[:, :], ACT.Tanh, scale=0.5).then_inc(gap_tanh.sem, 1)

                def abel(g, u):
                    wait(act, abel_biased, g)
                    if not early(g, 1):
                        wait(act, x_final, g - 2)
                    nc.scalar.activation(ab[u], ab_in.rearrange("p (t d) -> p t d", t=NT),
                                         ACT.Gelu).then_inc(abel_out.sem, 1)

                def w_rows(g):
                    wait(act, w_transposed, g)
                    if not early(g, 0):
                        wait(act, bias_mixed, g - 1)
                    nc.scalar.activation(wT[:, :], ps_w[:, :], ACT.Copy).then_inc(w_rows_ok.sem, 1)

                def moe_start(g, u):
                    wait(act, bias_mixed, g)
                    if not early(g, 1):
                        wait(act, x_final, g - 2)
                    nc.scalar.activation(moe[u], ps_w[:, :].rearrange("p (t d) -> p t d", t=NT),
                                         ACT.Copy).then_inc(moe_started.sem, 1)

                def hidden(g, e):
                    for j in range(NJ):
                        n = 2 * e + j
                        wait(act, up_ok, g, n + 1)
                        if not (early(g, 0) and e < 2):
                            act.wait_ge(down_ok.sem, down_ok.value(g, e - 1))
                        nc.scalar.activation(hT[e % 2][:, j, :], ps_up[j][:, :], ACT.Gelu,
                                             bias=b1_sb[:, e, j:j + 1]).then_inc(hidden_ok.sem, 1)

                def gate_tanh(g):
                    wait(act, gate_dots_ok, g)
                    nc.scalar.activation(thg[:, :], z2[:, :], ACT.Tanh, bias=cols[:, C_GCBH:C_GCBH + 1],
                                         scale=0.5).then_inc(gate_tanh_ok.sem, 1)

                def chunk(c, u, first, last):
                    g = CH * layer + c
                    hidden(g, 0)
                    w_rows(g)
                    hidden(g, 1)
                    moe_start(g, u)
                    hidden(g, 2)
                    if last and layer == 0:
                        x_high(0)
                    if not first:
                        gate_tanh(g - 1)
                    hidden(g, 3)
                    if not last:
                        xn_(g + 1)
                    elif layer == 0:
                        q_k(0)
                        q_high(0)
                    hidden(g, 4)
                    if last and layer == 0:
                        v_k_high(0)
                    for e in range(5, E):
                        hidden(g, e)
                    if not last:
                        abel(g + 1, 1 - u)
                        tanh_gap(g + 1)

                g0 = CH * layer
                if layer == 0:
                    xn_(0)
                abel(g0, 0)
                tanh_gap(g0)
                over_chunks(act, chunk)
                gate_tanh(g0 + CH - 1)

            def attention():
                def exp_(b, n):
                    t, i = divmod(n, UNITS)
                    kind, q = list(units())[i]
                    wait(act, b_scores, b, n + 1)
                    if i == 0 and not (early(b, 0) and t < 2):
                        act.wait_ge(values_ok.sem, values_ok.value(b, t - 1))
                    if kind == "full":
                        dst, src = pT[t % 2][:, q, 0:512], score_bank(b, n)[0][:, :]
                    elif kind == "mixed":
                        dst, src = pT[t % 2][:, q, 512:1024], score_bank(b, n)[0][:, :]
                    else:
                        dst = pT[t % 2][:, q:q + 2, 1024:PT_W]
                        src = score_bank(b, n)[0][:, :].rearrange("p (h n) -> p h n", h=2)
                    nc.scalar.activation(dst, src, ACT.Exp).then_inc(exp_ok.sem, 1)

                def maxima(b):
                    wait(act, max_transposed, b)
                    if not early(b, 0):
                        wait(act, max_in, b - 1)
                    nc.scalar.activation(mT, ps_m[0][0:32, :], ACT.Copy).then_inc(max_rows.sem, 1)

                def o_evac(b, t):
                    act.wait_ge(values_ok.sem, values_ok.value(b, t + 1))
                    if not early(b, 0):
                        wait(act, o_transposed, b - 1)
                    else:
                        for half in operands_in:
                            wait(act, half, 0)
                    nc.scalar.activation(oT[:, t, :], ps_o[:, :], ACT.Copy).then_inc(o_out.sem, 1)

                def y_evac(b):
                    wait(act, y_transposed, b)
                    if isinstance(b, int) and b == BATCH - 1:
                        wait(act, xn_split, CH)
                    elif isinstance(b, int) and b == BATCH - 2:
                        wait(act, qk_split, BATCH - 1)
                    else:
                        wait(act, qk_split, b + 2)
                    nc.scalar.activation(yT, ps_m[0][:, :].rearrange("p (t d) -> p t d", t=NT),
                                         ACT.Copy).then_inc(y_out.sem, 1)

                def batch(b, u, first, later):
                    for n in range(N_UNITS):
                        exp_(b, n)
                        if n == 2 and not first:
                            o_evac(b - 1, 3)
                        if n == AT_Y and not first:
                            y_evac(b - 1)
                        if later == 2:
                            if n == AT_X_HIGH:
                                x_high(b + 2)
                            if n == AT_QK:
                                q_k(b + 2)
                                q_high(b + 2)
                            if n == AT_V:
                                v_k_high(b + 2)
                        if n % UNITS == AT_VALUES[-1] + 1 and n > UNITS:
                            o_evac(b, n // UNITS - 1)
                        if n == AT_MAX and later >= 1:
                            maxima(b + 1)
                        if n == AT_X_HIGH and later == 0:
                            xn_(CH)

                x_high(1)
                q_k(1)
                q_high(1)
                v_k_high(1)
                maxima(0)
                over_batches(act, batch)
                o_evac(BATCH - 1, 3)
                y_evac(BATCH - 1)

            ffn(0)
            attention()
            nc.scalar.activation(cols[:, C_TMP:C_TMP + 1], cols[:, C_BETA:C_BETA + 1],
                                 ACT.Gelu).then_inc(gelu_table, 1)
            ffn(1)

        @block.vector
        def _(dve):
            v = nc.vector
            s = Run(dve, set_dve, 0)

            def hand(semaphore):
                s.join()
                dve.sem_inc(semaphore, 1)

            dve.wait_ge(ld_gen, 48)
            v.tensor_reduce(norm[:, :], gen_sb, AX.X, ALU.add,
                            apply_absolute_value=True).then_inc(norm_ok, 1)
            s.step(v.tensor_copy(ident_bf[:, :], ident[:, :]))
            dve.wait_ge(cst, 6)
            s.step(v.tensor_copy(expert_no[:, :, :], expert_no_i[:, :, :]))
            dve.wait_ge(norm_max, 1)
            for r in range(NROT):
                s.step(v.tensor_scalar(over[:, r, :], consts[:, 0:SQUARINGS], norm_all[:, r:r + 1], None,
                                       ALU.is_lt))
            s.join()
            s.step(v.tensor_tensor(shrink[:, :, :], over[:, :, :],
                                   consts[:, SQUARINGS:2 * SQUARINGS].unsqueeze(1)
                                   .to_broadcast([P, NROT, SQUARINGS]), ALU.mult))
            s.join()
            s.step(v.tensor_scalar(shrink[:, :, :], shrink[:, :, :], 1.0, None, ALU.add))
            s.join()
            s.step(v.tensor_reduce(shrink_m[:, :], shrink[:, :, :], AX.X, ALU.min))
            s.join()
            for r in range(NROT):
                s.step(v.tensor_scalar(gen_sb[:, r, :], gen_sb[:, r, :], shrink_m[:, r:r + 1], None, ALU.mult))
            hand(scaled)

            fact = [1.0]
            for k in range(1, TAYLOR + 1):
                fact.append(fact[-1] / k)
            identity = ident[:, :].unsqueeze(1).to_broadcast([P, NROT, P])

            def product(i):
                return banks[i][:, 0:NROT * P].rearrange("p (r n) -> p r n", r=NROT)

            dve.wait_ge(series_pe, 1)
            s.step(v.tensor_copy(gen_T, product(0)))
            hand(genT_ok)
            dve.wait_ge(series_pe, 2)
            s.step(v.tensor_copy(pow2, product(1)))
            hand(pow2_ok)
            dve.wait_ge(series_pe, 4)
            s.step(v.tensor_copy(pow3_T, product(3)))
            hand(pow3_ok)

            def series(dst, k):
                s.step(v.tensor_scalar(poly, gen_sb, fact[k + 1], None, ALU.mult))
                s.join()
                s.step(v.scalar_tensor_tensor(poly, pow2, fact[k + 2], poly, ALU.mult, ALU.add))
                s.join()
                s.step(v.scalar_tensor_tensor(dst, identity, fact[k], poly, ALU.mult, ALU.add))
                s.join()

            series(exp_m, 9)
            hand(horner)
            for i, k in enumerate((6, 3, 0)):
                series(poly2, k)
                dve.wait_ge(series_pe, 5 + i)
                s.step(v.tensor_tensor(exp_m, product(i % 2), poly2, ALU.add))
                hand(horner)
            dve.wait_ge(series_pe, 8)
            s.step(v.tensor_copy(exp_T, product(2)))
            hand(squared)
            dve.wait_ge(ld_w, LOADS_W * 16)
            s.step(v.tensor_scalar(cols[:, C_QBS:C_QBS + 1], cols[:, C_QB:C_QB + 1], SCALE, None, ALU.mult))
            s.step(v.tensor_scalar(cols[:, C_GCBH:C_GCBH + 1], cols[:, C_GCB:C_GCB + 1], 0.5, None, ALU.mult))

            def keep_squares(rounds):
                for i in rounds:
                    for r in range(NROT):
                        dve.wait_ge(square_pe, NROT * i + r + 1)
                        v.copy_predicated(mats[:, r, :, :], over[:, r, i:i + 1].bitcast(U32).unsqueeze(2)
                                          .to_broadcast([P, 2, P]),
                                          banks[r][:, 0:2 * P].rearrange("p (a n) -> p a n", a=2)).then_inc(squared, 1)

            def fold_rotation():
                dve.wait_ge(rot_pe, 1)
                v.tensor_copy(rot[:, 0, :], banks[3][:, 0:P]).then_inc(rot_ok, 1)
                dve.wait_ge(rot_pe, 2)
                v.tensor_copy(rot[:, 1, :], banks[5][:, 0:P]).then_inc(rot_ok, 1)
                dve.wait_ge(rot_pe, 3)
                s.step(v.tensor_copy(b2_f, banks[5][:, 0:D]))
                s.join()
                s.step(v.tensor_copy(b2_hi[:, :], b2_f))
                for q in range(4):
                    dve.wait_ge(rot_pe, 4 + q)
                    s.step(v.tensor_copy(w2_rot[:, 2 * q:2 * q + 2, :, :],
                                         banks[q][:, :].rearrange("p (e j d) -> p e j d", e=2, j=NJ)))
                s.join()
                s.step(v.scalar_tensor_tensor(b2_rot[:, :], b2_hi[:, :].bitcast(FP32),
                                              consts[:, 2 * SQUARINGS:2 * SQUARINGS + 1], b2_f, ALU.mult, ALU.add))
                dve.wait_ge(lo_ok, 2)
                s.join()
                dve.sem_inc(w_ready, 1)

            def statistics(run, src):
                for t in range(NT):
                    run.step(v.bn_stats(stat[:, t, :], src(t)))
                run.join_alone(passed)
                for t in range(NT):
                    run.step(v.bn_aggr(mv[:, t, :], stat[:, t, :]))
                run.join()
                run.step(v.tensor_scalar(var[:, 0, :], mv[:, :, 1], EPS, None, ALU.add))
                run.step(v.tensor_scalar(var[:, 1, :], mv[:, :, 1], 1.0 + EPS, EPS * EPS, ALU.mult, ALU.add))

            def normalise_tiles(run, src, rs, dst):
                for t in range(NT):
                    run.step(v.tensor_scalar(dst(t), src(t), mv[:, t, 0:1], rs[:, t:t + 1],
                                             ALU.subtract, ALU.mult))

            def attention_stats(b):
                if early(b, 0):
                    wait(dve, y_ok, CH - 1)
                statistics(Run(dve, xh_ok, b), lambda t: xs(b, t))

            def attention_norm(b):
                run = Run(dve, xh_ok, b)
                run.done = 10
                if early(b, 0):
                    wait(dve, z_transposed, CH - 1)
                elif early(b, 2):
                    wait(dve, x_transposed, b - 1)
                else:
                    wait(dve, y_transposed, b - 3)
                wait(dve, att_roots_ok, b)
                normalise_tiles(run, lambda t: xs(b, t), rstd[:, 0, :], lambda t: xh[:, t, :])
                run.end()

            def x_low(b):
                wait(dve, x_high_ok, b)
                v.tensor_tensor(x_lo, ps_m[0][:, :], x_hi.bitcast(FP32), ALU.subtract).then_inc(x_low_ok.sem, 1)

            def q_k_low(b):
                q_, k_ = (qs_first, ks_first) if early(b, 0) else (qs, ks)
                wait(dve, q_high_ok, b)
                v.tensor_tensor(q_[:, 1, :], qf, q_[:, 0, :].bitcast(FP32), ALU.subtract).then_inc(qk_split.sem, 1)
                wait(dve, k_high_ok, b)
                v.tensor_tensor(k_[:, 1, :], kf, k_[:, 0, :].bitcast(FP32), ALU.subtract).then_inc(qk_split.sem, 1)

            def stats_(g, c):
                if not early(g, 0):
                    wait(dve, y_ok, g - 1)
                run = Run(dve, stats_and_z, g)
                statistics(run, lambda t: xs(c, t))

            def norms(g, c):
                run = Run(dve, stats_and_z, g)
                run.done = 10
                wait(dve, roots_ok, g)
                if isinstance(g, int) and g == CH:
                    wait(dve, y_transposed, BATCH - 2)
                elif not early(g, 0):
                    wait(dve, z_transposed, g - 1)
                normalise_tiles(run, lambda t: xs(c, t), rstd[:, 1, :], lambda t: z[:, t, :])
                run.end()

            def split_(g, u):
                run = Run(dve, xn_split, g)
                wait(dve, xn_ok, g)
                if isinstance(g, int) and g == CH:
                    for half in operands_in:
                        wait(dve, half, BATCH - 1)
                elif not early(g, 1):
                    wait(dve, up_ok, g - 2)
                run.step(v.tensor_copy(xn_hi[u], xn))
                run.join()
                run.step(v.tensor_tensor(xn_lo[u], xn, xn_hi[u].bitcast(FP32), ALU.subtract))
                run.end()

            def top_two(g):
                run = Run(dve, routed, g)
                wait(dve, abel_logits_ok, g)
                run.step(v.tensor_tensor(logit[:, :, :].rearrange("p (b t) e -> p b t e", b=2),
                                         ps_al[:, :, :, D:DA],
                                         rows[:, R_GB:R_GB + E].unsqueeze(1).unsqueeze(1)
                                         .to_broadcast([P, 2, 2, E]), ALU.add))
                run.join_alone(passed)
                for t in range(NT):
                    run.step(v.max(top[:, t, :], logit[:, t, :]))
                run.join_alone(passed)
                for t in range(NT):
                    run.step(v.max_index(top_i[:, t, :], top[:, t, :], logit[:, t, :]))
                run.step(v.tensor_tensor(gap[:, :], top[:, :, 0], top[:, :, 1], ALU.subtract))

            def abel_bias(g):
                wait(dve, abel_logits_ok, g)
                if not early(g, 0):
                    wait(dve, abel_out, g - 1)
                v.tensor_tensor(ab_in.rearrange("p (b t d) -> p b t d", b=2, t=2), ps_al[:, :, :, 0:D],
                                rows[:, R_AB:R_AB + D].unsqueeze(1).unsqueeze(1)
                                .to_broadcast([P, 2, 2, D]), ALU.add).then_inc(abel_biased.sem, 1)

            def ffn(layer):
                def expert_weights(g, u):
                    run = Run(dve, routed, g)
                    run.done = 10
                    run.join()
                    run.step(v.tensor_copy(top_f[:, :, :], top_i[:, :, 0:2]))
                    run.join()
                    for k in range(2):
                        run.step(v.tensor_tensor(pick[:, k, :, :], expert_no[:, :, :],
                                                 top_f[:, :, k:k + 1].to_broadcast([P, NT, E]), ALU.is_equal))
                    wait(dve, gap_tanh, g)
                    run.step(v.tensor_scalar(w12[:, :, 0], th[:, :], 0.5, 0.5, ALU.mult, ALU.add))
                    run.step(v.tensor_scalar(w12[:, :, 1], th[:, :], -0.5, 0.5, ALU.mult, ALU.add))
                    run.join()
                    for k in range(2):
                        run.step(v.tensor_tensor(pick[:, k, :, :], pick[:, k, :, :],
                                                 w12[:, :, k:k + 1].to_broadcast([P, NT, E]), ALU.mult))
                    run.join()
                    run.step(v.tensor_tensor(w_exp[u][:, :, :], pick[:, 0, :, :], pick[:, 1, :, :], ALU.add))
                    run.join()
                    run.step(v.tensor_copy(w_hi[:, :, :], w_exp[u][:, :, :]))
                    run.join()
                    if early(g, 0) or (isinstance(g, int) and g == CH):
                        dve.wait_ge(w_pad_zero, 1 + layer)
                    else:
                        wait(dve, w_transposed, g - 1)
                    run.step(v.tensor_copy(w_pad[:, :, 0:E], w_hi[:, :, :].bitcast(FP32)))
                    run.step(v.tensor_tensor(w_pad[:, :, E:2 * E], w_exp[u][:, :, :],
                                             w_hi[:, :, :].bitcast(FP32), ALU.subtract))
                    run.step(v.tensor_copy(w_pad[:, :, 2 * E:3 * E], w_hi[:, :, :].bitcast(FP32)))
                    run.end()

                def accumulate(g, u, e):
                    wait(dve, down_ok, g, e + 1)
                    if e == 0:
                        wait(dve, moe_started, g)
                    else:
                        wait(dve, expert_added, g, NT * e)
                    for t in range(NT):
                        v.scalar_tensor_tensor(moe[u][:, t, :], ps_dn[e % 2][:, t * D:(t + 1) * D],
                                               w_exp[u][:, t, e:e + 1], moe[u][:, t, :],
                                               ALU.mult, ALU.add).then_inc(expert_added.sem, 1)

                def gate_dots(g, src, row, ins, outs, step):
                    run = Run(dve, gate_dots_ok, g)
                    run.done = step
                    if step:
                        wait(dve, expert_added, g)
                        run.join()
                    else:
                        wait(dve, abel_out, g)
                        if not early(g, 0):
                            wait(dve, gate_dots_ok, g - 1)
                    for t in range(NT):
                        run.step(v.tensor_tensor_reduce(out=dot[:, t, :], in0=src[:, t, :], in1=rows[:, row:row + D],
                                                        scale=1.0, scalar=ins(t), op0=ALU.mult, op1=ALU.add,
                                                        accum_out=outs[:, t:t + 1]))

                def abel_dots(g, u):
                    gate_dots(g, ab[u], R_G1, lambda t: 0.0, z1, 0)

                def moe_dots(g, u):
                    gate_dots(g, moe[u], R_G2, lambda t: z1[:, t:t + 1], z2, NT)

                def finish_skip(g, c):
                    run = Run(dve, x_final, g)
                    wait(dve, skip_ok, g)
                    run.step(v.scalar_tensor_tensor(xs(c), skip, 0.5, xs(c), ALU.mult, ALU.add))

                def finish_gate(g, c):
                    run = Run(dve, x_final, g)
                    run.done = 1
                    wait(dve, gate_tanh_ok, g)
                    run.step(v.tensor_scalar(gate[:, :], thg[:, :], 0.25, 0.25, ALU.mult, ALU.add))
                    wait(dve, diff_ok, g)
                    run.join()
                    for t in range(NT):
                        run.step(v.scalar_tensor_tensor(xs(c, t), diff[:, t, :], gate[:, t:t + 1], xs(c, t),
                                                        ALU.mult, ALU.add))
                    run.end()

                def chunk(c, u, first, last):
                    g = CH * layer + c
                    if not last:
                        stats_(g + 1, c + 1)
                    elif layer == 0:
                        attention_stats(0)
                    accumulate(g, u, 0)
                    if not last:
                        norms(g + 1, c + 1)
                    elif layer == 0:
                        attention_norm(0)
                    accumulate(g, u, 1)
                    if last and layer == 0:
                        x_low(0)
                    if not first:
                        finish_skip(g - 1, c - 1)
                    accumulate(g, u, 2)
                    if not first:
                        finish_gate(g - 1, c - 1)
                    accumulate(g, u, 3)
                    if not last:
                        split_(g + 1, 1 - u)
                    accumulate(g, u, 4)
                    if last and layer == 0:
                        q_k_low(0)
                    abel_dots(g, u)
                    accumulate(g, u, 5)
                    if not last:
                        abel_bias(g + 1)
                        top_two(g + 1)
                    accumulate(g, u, 6)
                    if not last:
                        expert_weights(g + 1, 1 - u)
                    accumulate(g, u, 7)
                    moe_dots(g, u)

                if layer == 0:
                    keep_squares(range(0, 3))
                    dve.wait_ge(ld_x, 16)
                    stats_(0, 0)
                    keep_squares(range(3, 5))
                    norms(0, 0)
                    keep_squares(range(5, 8))
                    split_(0, 0)
                    keep_squares(range(8, 12))
                    abel_bias(0)
                    top_two(0)
                    keep_squares(range(12, 15))
                g0 = CH * layer
                expert_weights(g0, 0)
                if layer == 0:
                    keep_squares(range(15, SQUARINGS))
                    fold_rotation()
                over_chunks(dve, chunk)
                finish_skip(g0 + CH - 1, CH - 1)
                finish_gate(g0 + CH - 1, CH - 1)

            def attention():
                def reduce_(b, n):
                    t, i = divmod(n, UNITS)
                    kind, q = list(units())[i]
                    wait(dve, a_scores, b, n + 1)
                    if n == 0 and not early(b, 0):
                        wait(dve, max_split, b - 1)
                    src = ps_a[n % NA]
                    if kind == "full":
                        v.tensor_reduce(mx[:, 3, q, t:t + 1], src[:, :], AX.X, ALU.max).then_inc(reduced.sem, 1)
                    elif kind == "mixed":
                        v.tensor_reduce(mx[:, 2, q, t:t + 1], src[:, 0:384], AX.X, ALU.max)
                        v.tensor_reduce(mx[:, 0, q, t:t + 1], src[:, 384:512], AX.X, ALU.max).then_inc(reduced.sem, 1)
                    else:
                        v.tensor_reduce(mx[:, 1, q:q + 2, t], src[:, :].rearrange("p (h n) -> p h n", h=2),
                                        AX.X, ALU.max).then_inc(reduced.sem, 1)

                def maxima(b):
                    run = Run(dve, max_split, b)
                    wait(dve, reduced, b)
                    run.step(v.tensor_scalar(mx_h[:, :, :, :], mx[:, :, :, :], -1.0, None, ALU.mult))
                    run.join()
                    if not early(b, 0):
                        wait(dve, max_transposed, b - 1)
                    mh = mx_h[:, :, :, :].bitcast(FP32)
                    run.step(v.tensor_copy(mx2[:, :, :, 0, :], mh))
                    run.step(v.scalar_tensor_tensor(mx2[:, :, :, 1, :], mx[:, :, :, :], -1.0, mh,
                                                    ALU.mult, ALU.subtract))
                    run.end()

                def normalise(b, i):
                    run = Run(dve, y_normalised, b)
                    run.done = 2 * i
                    wait(dve, o_transposed, b, i + 1)
                    src = ps_m[i % 2][:, :].rearrange("p (t q c) -> p t q c", t=NG, q=NQ)
                    if i == 0 and isinstance(b, int) and b == BATCH - 1:
                        wait(dve, z_transposed, CH)
                    elif i == 0 and not early(b, 0):
                        wait(dve, y_transposed, b - 1)
                    run.step(v.reciprocal(rden[i % 2][:, :, :], src[:, :, :, HD]))
                    run.join()
                    run.step(v.tensor_tensor(yn[:, i, :].rearrange("p (q t c) -> p t q c", t=NG, q=NQ),
                                             src[:, :, :, 0:HD],
                                             rden[i % 2][:, :, :].unsqueeze(3).to_broadcast([P, NG, NQ, HD]), ALU.mult))

                def add_out(b):
                    wait(dve, o_projected, b)
                    wait(dve, o_bias_added, b)
                    v.tensor_tensor(xs(b), ps_m[1][:, :].rearrange("p (t d) -> p t d", t=NT), xs(b),
                                    ALU.add).then_inc(x_attended.sem, 1)

                def batch(b, u, first, later):
                    for n in range(N_UNITS):
                        if not first:
                            if n in AT_NORMALISE:
                                normalise(b - 1, AT_NORMALISE.index(n))
                            if n == AT_ADD:
                                add_out(b - 1)
                        if later == 2:
                            if n == AT_STATS:
                                attention_stats(b + 2)
                            if n == AT_NORM:
                                attention_norm(b + 2)
                            if n == AT_X_LOW:
                                x_low(b + 2)
                            if n == AT_LOW:
                                q_k_low(b + 2)
                        if later >= 1:
                            for a in beside(n):
                                reduce_(b + 1, a)
                        if later == 0:
                            if n == AT_STATS:
                                stats_(CH, 0)
                            if n == AT_NORM:
                                norms(CH, 0)
                            if n == AT_X_LOW:
                                split_(CH, 0)
                            if n == AT_QK_PROJECT + 1:
                                abel_bias(CH)
                                top_two(CH)
                    if later >= 1:
                        maxima(b + 1)

                attention_stats(1)
                attention_norm(1)
                for n in range(N_UNITS):
                    if n == 5:
                        x_low(1)
                    if n == 12:
                        q_k_low(1)
                    reduce_(0, n)
                maxima(0)
                over_batches(dve, batch)
                for i in range(NT):
                    normalise(BATCH - 1, i)
                add_out(BATCH - 1)

            ffn(0)
            wait(dve, x_final, CH - 1)
            attention()
            wait(dve, x_attended, BATCH - 1)
            ffn(1)

        @block.tensor
        def _(pe):
            mm = nc.tensor.matmul

            def split_product(outp, a_hi, a_lo, b_hi, b_lo):
                mm(outp, a_hi, b_hi, start=True, stop=False)
                mm(outp, a_hi, b_lo, start=False, stop=False)
                return mm(outp, a_lo, b_hi, start=False, stop=True)

            def each(bank_, lhsT, rhs):
                for r in range(NROT):
                    last = mm(banks[bank_][:, r * P:(r + 1) * P], lhsT[:, r, :], rhs[:, r, :], start=True, stop=True)
                last.then_inc(series_pe, 1)

            def each_transposed(bank_, src):
                for r in range(NROT):
                    last = nc.tensor.transpose(banks[bank_][:, r * P:(r + 1) * P], src[:, r, :], ident[:, :])
                last.then_inc(series_pe, 1)

            pe.wait_ge(scaled, 1)
            each_transposed(0, gen_sb)
            pe.wait_ge(genT_ok, 1)
            each(1, gen_T, gen_sb)
            pe.wait_ge(pow2_ok, 1)
            each(2, gen_T, pow2)
            each(3, pow2, gen_T)
            pe.wait_ge(pow3_ok, 1)
            for i in range(3):
                pe.wait_ge(horner, 1 + i)
                each(i % 2, pow3_T, exp_m)
            pe.wait_ge(horner, 4)
            each_transposed(2, exp_m)
            def transpose_w2(q):
                for i in range(4):
                    e, j = 2 * q + i // 2, i % 2
                    last = nc.tensor.transpose(banks[4 + q][:, i * P:(i + 1) * P], w2_in[:, e, j, :], ident[:, :])
                last.then_inc(w2T_pe, 1)

            def transpose_b2():
                pe.wait_ge(ld_pool, 4 * 16)
                nc.tensor.transpose(banks[3][:, 0:P], b2_in, ident[:, :]).then_inc(w2T_pe, 1)

            def square(rounds):
                for i in rounds:
                    for r in range(NROT):
                        pe.wait_ge(squared, NROT * (i - 1) + r + 2 if i else 1)
                        mm(banks[r][:, 0:P], exp_T[:, r, :], exp_m[:, r, :], start=True, stop=True)
                        mm(banks[r][:, P:2 * P], exp_m[:, r, :], exp_T[:, r, :], start=True,
                           stop=True).then_inc(square_pe, 1)

            def fold_rotation():
                pe.wait_ge(squared, 1 + NROT * SQUARINGS)
                mm(banks[3][:, 0:P], exp_T[:, 1, :], exp_m[:, 2, :], start=True, stop=True).then_inc(rot_pe, 1)
                pe.wait_ge(rot_ok, 1)
                mm(banks[5][:, 0:P], exp_T[:, 0, :], rot[:, 0, :], start=True, stop=True).then_inc(rot_pe, 1)
                pe.wait_ge(rot_ok, 2)
                mm(banks[5][:, 0:P], b2_T, rot[:, 1, :], start=True, stop=True).then_inc(rot_pe, 1)
                for q in range(4):
                    for i in range(4):
                        e, j = 2 * q + i // 2, i % 2
                        last = mm(banks[q][:, i * P:(i + 1) * P], w2_T[:, e, j, :], rot[:, 1, :],
                                  start=True, stop=True)
                    last.then_inc(rot_pe, 1)
                pe.wait_ge(w_ready, 1)

            def tile(ap, t):
                return ap[:, t * P:(t + 1) * P]

            def transpose_x(b):
                wait(pe, xh_ok, b)
                if early(b, 0):
                    wait(pe, routed, CH - 1)
                    wait(pe, abel_biased, CH - 1)
                elif early(b, 1):
                    wait(pe, k_high_ok, b - 1)
                elif early(b, 2):
                    wait(pe, max_rows, b - 2)
                else:
                    wait(pe, y_out, b - 3)
                for t in range(NT):
                    last = nc.tensor.transpose(tile(ps_m[0], t), xh[:, t, :], ident[:, :])
                last.then_inc(x_transposed.sem, 1)

            def project_q_k(b):
                wait(pe, x_low_ok, b)
                if not early(b, 2):
                    wait(pe, x_attended, b - 3)
                elif not early(b, 0):
                    wait(pe, v_next_ok, b - 1)
                split_product(ps_m[1][:, :], small_hi[:, W_Q:W_Q + D], small_lo[:, W_Q:W_Q + D],
                              x_hi, x_lo).then_inc(q_projected.sem, 1)
                split_product(ps_m[0][:, :], small_hi[:, W_K:W_K + D], small_lo[:, W_K:W_K + D],
                              x_hi, x_lo).then_inc(k_projected.sem, 1)

            def project_v(b):
                wait(pe, q_out, b)
                for t in range(NT):
                    last = split_product(tile(ps_m[1], t), tile(x_hi, t), tile(x_lo, t),
                                         small_hi[:, W_V:W_V + D], small_lo[:, W_V:W_V + D])
                last.then_inc(v_projected.sem, 1)

            def at_turn(g):
                return isinstance(g, int) and g == CH

            def transpose_z(g):
                wait(pe, stats_and_z, g)
                if at_turn(g):
                    wait(pe, reduced, BATCH - 1)
                elif not early(g, 0):
                    wait(pe, xn_ok, g - 1)
                for t in range(NT):
                    last = nc.tensor.transpose(tile(ps_T, t), z[:, t, :], ident[:, :])
                last.then_inc(z_transposed.sem, 1)

            def abel_logits(g, u):
                wait(pe, xn_split, g)
                if at_turn(g):
                    wait(pe, y_out, BATCH - 2)
                    wait(pe, x_attended, BATCH - 2)
                elif not early(g, 0):
                    wait(pe, routed, g - 1, 1)
                    wait(pe, abel_biased, g - 1)
                for t in range(NT):
                    last = split_product(ps_al[:, t // 2, t % 2, :], tile(xn_hi[u], t), tile(xn_lo[u], t),
                                         small_hi[:, W_AB:W_AB + DA], small_lo[:, W_AB:W_AB + DA])
                last.then_inc(abel_logits_ok.sem, 1)

            def ffn(layer):
                def transpose_w(g):
                    wait(pe, routed, g)
                    if at_turn(g):
                        wait(pe, o_out, BATCH - 1)
                    elif not early(g, 0):
                        wait(pe, moe_started, g - 1)
                    for t in range(NT):
                        last = nc.tensor.transpose(tile(ps_w, t), w_pad[:, t, :], ident[:, :])
                    last.then_inc(w_transposed.sem, 1)

                def weighted_bias(g):
                    wait(pe, w_rows_ok, g)
                    for t in range(NT):
                        last = mm(tile(ps_w, t), tile(wT, t), b2_rot[:, :], start=True, stop=True)
                    last.then_inc(bias_mixed.sem, 1)

                def up_(g, u, e):
                    for j in range(NJ):
                        n = NJ * e + j
                        if not (early(g, 0) and e == 0):
                            if at_turn(g) and e == 0:
                                wait(pe, exp_ok, BATCH - 1)
                            pe.wait_ge(hidden_ok.sem, hidden_ok.value(g, n - 1))
                        last = split_product(ps_up[j][:, :], w1_hi[:, e, j * P:(j + 1) * P],
                                             w1_lo[:, e, j * P:(j + 1) * P], xn_hi[u], xn_lo[u])
                        last.then_inc(up_ok.sem, 1)

                def down(g, e):
                    wait(pe, hidden_ok, g, NJ * (e + 1))
                    if at_turn(g) and e < 2:
                        wait(pe, exp_ok, BATCH - 1)
                    elif not (early(g, 0) and e < 2):
                        pe.wait_ge(expert_added.sem, expert_added.value(g, NT * (e - 1)))
                    for t in range(NT):
                        for j in range(NJ):
                            last = mm(tile(ps_dn[e % 2], t), hT[e % 2][:, j, t * P:(t + 1) * P],
                                      w2_rot[:, e, j, :], start=(j == 0), stop=(j == NJ - 1))
                    last.then_inc(down_ok.sem, 1)

                def chunk(c, u, first, last):
                    g = CH * layer + c
                    up_(g, u, 0)
                    transpose_w(g)
                    up_(g, u, 1)
                    weighted_bias(g)
                    down(g, 0)
                    up_(g, u, 2)
                    down(g, 1)
                    if last and layer == 0:
                        transpose_x(0)
                    up_(g, u, 3)
                    down(g, 2)
                    if not last:
                        transpose_z(g + 1)
                    elif layer == 0:
                        project_q_k(0)
                    up_(g, u, 4)
                    down(g, 3)
                    if last and layer == 0:
                        project_v(0)
                    up_(g, u, 5)
                    down(g, 4)
                    if not last:
                        abel_logits(g + 1, 1 - u)
                    up_(g, u, 6)
                    down(g, 5)
                    up_(g, u, 7)
                    down(g, 6)
                    down(g, 7)

                if layer == 0:
                    pe.wait_ge(ld_w, LOADS_W * 16)
                    for q in range(4):
                        square(range(q, q + 1))
                        transpose_w2(q)
                    transpose_b2()
                    square(range(4, 6))
                    pe.wait_ge(w2T_ok, 5)
                    transpose_z(0)
                    square(range(6, 10))
                    pe.wait_ge(lo_ok, 1)
                    abel_logits(0, 0)
                    square(range(10, SQUARINGS))
                    fold_rotation()
                over_chunks(pe, chunk)

            def attention():
                def masks(bank_, kind, mask, cols_):
                    if kind == "full":
                        return mm(bank_[:, cols_[0]:cols_[0] + P], ident_bf[:, :], mask[:, 0, :],
                                  start=False, stop=True)
                    if kind == "mixed":
                        return mm(bank_[:, cols_[1]:cols_[1] + 2 * P], ident_bf[:, :],
                                  mask[:, :, :].rearrange("p a n -> p (a n)"), start=False, stop=True,
                                  skip_group_check=True)
                    return mm(bank_[:, :].rearrange("p (a n) -> p a n", a=2)[:, :, cols_[2]:cols_[2] + P],
                              ident_bf[:, :], mask[:, :, :], start=False, stop=True, skip_group_check=True)

                def scores_for_max(b, u, n):
                    t, i = divmod(n, UNITS)
                    kind, q = list(units())[i]
                    bank_ = ps_a[n % NA]
                    if n % (N_UNITS // 2) == 0:
                        wait(pe, operands_in[n // (N_UNITS // 2)], b)
                    if n >= NA:
                        wait(pe, reduced, b, n - NA + 1)
                    elif not early(b, 0):
                        wait(pe, reduced, b - 1)
                    else:
                        wait(pe, hidden_ok, CH - 1)
                        wait(pe, xn_ok, CH - 1)
                    head = NG * q + t

                    def rows_keys(outp, query_tile, h, keys, start):
                        mm(outp, qT[u][:, t, query_tile * P:(query_tile + 1) * P], kZ[u][:, h, 0:keys],
                           start=start, stop=False, skip_group_check=(kind != "full"))

                    if kind == "full":
                        rows_keys(bank_[:, :], 3, head, 4 * P, True)
                    elif kind == "mixed":
                        rows_keys(bank_[:, 0:3 * P], 2, head, 3 * P, True)
                        rows_keys(bank_[:, 3 * P:4 * P], 0, head, P, False)
                    else:
                        rows_keys(bank_[:, 0:2 * P], 1, head, 2 * P, True)
                        rows_keys(bank_[:, 2 * P:4 * P], 1, head + NG, 2 * P, False)
                    masks(bank_, kind, mask_qk, (3 * P, 2 * P, P)).then_inc(a_scores.sem, 1)

                def transpose_max(b):
                    wait(pe, max_split, b)
                    if isinstance(b, int) and b == BATCH - 1:
                        wait(pe, y_out, b - 2)
                    else:
                        wait(pe, k_out, b + 1)
                    for i in range(NT):
                        last = nc.tensor.transpose(ps_m[0][0:32, i * P:(i + 1) * P],
                                                   mx2[:, i, :, :, :].rearrange("p g a t -> p (g a t)"), ident[:, :])
                    last.then_inc(max_transposed.sem, 1)

                def scores(b, u, n):
                    t, i = divmod(n, UNITS)
                    kind, q = list(units())[i]
                    bank_, ring = score_bank(b, n)
                    if n == 0:
                        wait(pe, max_in, b)
                    if early(b, 0) and n < ring:
                        wait(pe, expert_added, CH - 1)
                    elif ring == 2:
                        pe.wait_ge(exp_ok.sem, exp_ok.value(b, n - 1))
                    elif n < 2:
                        wait(pe, exp_ok, b - 1)
                    elif n < ring:
                        wait(pe, reduced, b)
                    else:
                        wait(pe, exp_ok, b, n - ring + 1)
                    head = NG * q + t

                    def keys_rows(outp, block_, h, start):
                        lo = block_ * P
                        mm(outp, kZ[u][:, h, lo:lo + P], qT[u][:, t, lo:SEQ], start=start, stop=False,
                           skip_group_check=(kind != "full"))

                    if kind == "full":
                        keys_rows(bank_[:, :], 0, head, True)
                    elif kind == "mixed":
                        keys_rows(bank_[:, 0:P], 3, head, True)
                        keys_rows(bank_[:, P:4 * P], 1, head, False)
                    else:
                        keys_rows(bank_[:, 0:2 * P], 2, head, True)
                        keys_rows(bank_[:, 2 * P:4 * P], 2, head + NG, False)
                    masks(bank_, kind, mask_kq, (0, 0, 0)).then_inc(b_scores.sem, 1)

                def values(b, u, t, kb):
                    if kb == 0:
                        pe.wait_ge(exp_ok.sem, exp_ok.value(b, UNITS * (t + 1)))
                        wait(pe, v_placed, b)
                        if early(b, 0) and t < 1:
                            wait(pe, moe_started, CH - 1)
                        else:
                            wait(pe, o_out, b, t)
                    for q in range(NQ):
                        n = SEQ - kb * P
                        last = mm(ps_o[32 * q:32 * q + HD + 1, kb * P:SEQ],
                                  vA[u][:, kb, NG * q + t, :], pT[t % 2][:, q, PT_KB[kb]:PT_KB[kb] + n],
                                  start=(kb == 0), stop=(kb == NT - 1))
                    if kb == NT - 1:
                        last.then_inc(values_ok.sem, 1)

                def transpose_o(b, i):
                    if i == 0:
                        wait(pe, o_out, b)
                        if isinstance(b, int) and b == BATCH - 1:
                            wait(pe, abel_biased, CH)
                            wait(pe, routed, CH, 1)
                        else:
                            wait(pe, max_rows, b + 1)
                    elif i == 1:
                        if isinstance(b, int) and b == BATCH - 2:
                            wait(pe, x_attended, b - 1)
                        elif isinstance(b, int) and b == BATCH - 1:
                            wait(pe, abel_biased, CH)
                        else:
                            wait(pe, v_next_ok, b + 2)
                    else:
                        wait(pe, y_normalised, b, 2 * (i - 1))
                    for t in range(NG):
                        ins = nc.tensor.transpose(tile(ps_m[i % 2], t), oT[:, t, i * P:(i + 1) * P], ident[:, :])
                    ins.then_inc(o_transposed.sem, 1)

                def transpose_y(b):
                    wait(pe, y_normalised, b)
                    for t in range(NT):
                        ins = nc.tensor.transpose(tile(ps_m[0], t), yn[:, t, :], ident[:, :])
                    ins.then_inc(y_transposed.sem, 1)

                def project_o(b):
                    wait(pe, y_out, b)
                    for t in range(NT):
                        ins = mm(tile(ps_m[1], t), yT[:, t, :], wo_sb[:, :], start=True, stop=True)
                    ins.then_inc(o_projected.sem, 1)

                def batch(b, u, first, later):
                    if later >= 1:
                        for a in beside(0):
                            scores_for_max(b + 1, 1 - u, a)
                    if not first:
                        for kb in range(NT // 2):
                            values(b - 1, 1 - u, NG - 1, kb)
                    for n in range(N_UNITS):
                        t, i = divmod(n, UNITS)
                        if later >= 1 and n:
                            for a in beside(n):
                                scores_for_max(b + 1, 1 - u, a)
                        scores(b, u, n)
                        if not first:
                            if n < NT // 2:
                                values(b - 1, 1 - u, NG - 1, NT // 2 + n)
                            if n in AT_OUT:
                                transpose_o(b - 1, AT_OUT.index(n))
                            if n == AT_Y_T:
                                transpose_y(b - 1)
                            if n == AT_OUT_PROJECT:
                                project_o(b - 1)
                        if t and i in AT_VALUES:
                            values(b, u, t - 1, AT_VALUES.index(i))
                        if later == 2:
                            if n == AT_X_T:
                                transpose_x(b + 2)
                            if n == AT_QK_PROJECT:
                                project_q_k(b + 2)
                            if n == AT_V_PROJECT:
                                project_v(b + 2)
                        if later >= 1 and n == AT_MAX_T:
                            transpose_max(b + 1)
                        if later == 0:
                            if n == AT_X_T:
                                transpose_z(CH)
                            if n == AT_QK_PROJECT:
                                abel_logits(CH, 0)

                for n in range(N_UNITS):
                    if n == 3:
                        transpose_x(1)
                    if n == 8:
                        project_q_k(1)
                    if n == 10:
                        project_v(1)
                    scores_for_max(0, 0, n)
                transpose_max(0)
                over_batches(pe, batch)
                for kb in range(NT):
                    values(BATCH - 1, 1, 3, kb)
                for i in range(NT):
                    transpose_o(BATCH - 1, i)
                transpose_y(BATCH - 1)
                project_o(BATCH - 1)

            ffn(0)
            attention()
            ffn(1)


_FFN = ["ln_gamma", "ln_beta", "abel_w", "abel_b", "moe_gate_w", "moe_gate_b", "ew1", "eb1", "ew2", "eb2",
        "gens", "gc_w", "gc_b"]


def by_group(a):
    parts = a.reshape(a.shape[:-1] + (NQ, NG // HALF, HALF, HD))
    order = tuple(range(a.ndim - 1)) + tuple(a.ndim - 1 + i for i in (1, 0, 3, 2))
    return parts.transpose(order).reshape(a.shape)


def arguments(inputs):
    att = {n[len("L0_attn_"):]: np.asarray(a) for n, a in inputs.items() if n.startswith("L0_attn_")}
    named = {"x": att["x"], "q_w": by_group(att["q_w"]), "q_b": by_group(att["q_b"]),
             "k_w": by_group(att["kv_w"][:, :D]), "k_b": by_group(att["kv_b"][:D]),
             "v_w": att["kv_w"][:, D:], "v_b": att["kv_b"][D:], "o_w": att["o_w"], "o_b": att["o_b"]}
    named.update({n: np.asarray(inputs["L0_ffn_" + n]) for n in _FFN})
    named["eb1"] = named["eb1"].reshape(E, NJ, P).transpose(2, 0, 1)
    named.update(constants())
    return named


def constants():
    f = np.float32
    i = np.arange(SEQ)
    bias_q = np.zeros((P, NG, SEQ), f)
    bias_k = np.zeros((P, NQ, SEQ), f)
    for q in range(NQ):
        row = ROW_BIAS + 3 * q
        for t in range(NG):
            slope = (NG * q + t + 1) / NH
            bias_q[row, t] = slope
            bias_q[row + 1, t] = -slope * (i - i % 32)
            bias_q[row + 2, t] = -slope * (i % 32)
        bias_k[row, q] = i
        bias_k[row + 1:row + 3, q] = 1.0
        bias_k[ROW_MAX + 2 * q:ROW_MAX + 2 * (q + 1), q] = 1.0
    powers = np.zeros((P, 2 * SQUARINGS + 1), f)
    powers[:, :SQUARINGS] = 2.0 ** np.arange(SQUARINGS)
    powers[:, SQUARINGS:2 * SQUARINGS] = 2.0 ** -(np.arange(SQUARINGS) + 1.0) - 1.0
    powers[2 * E:, 2 * SQUARINGS] = -1.0
    return {"ident": np.eye(P, dtype=f), "bias_q": bias_q, "bias_k": bias_k, "powers": powers}


def kernel(**inputs):
    import concourse.bacc as bacc
    from concourse.bass_utils import run_bass_kernel_spmd

    nc = bacc.Bacc("TRN2", target_bir_lowering=False, num_devices=1)
    arrays, args = {}, []
    for name, a in arguments(inputs).items():
        a = np.ascontiguousarray(a)
        arrays[f"in_{name}"] = a
        args.append(nc.dram_tensor(f"in_{name}", a.shape, mybir.dt.from_np(a.dtype), kind="ExternalInput").ap())
    out = nc.dram_tensor("out", (BATCH, SEQ, D), FP32, kind="ExternalOutput").ap()
    macaron_block(nc, *args, out)
    r = run_bass_kernel_spmd(nc, [arrays], core_ids=[0])
    return r.results[0]["out"]
```
